# Optimizing a Trainium2 kernel written in Bass

```python
import numpy as np
import jax
import jax.numpy as jnp

def _softmax(x, axis=-1):
    return jax.nn.softmax(x, axis=axis)

def _gelu(x):
    return jax.nn.gelu(x, approximate=True)

def _silu(x):
    return jax.nn.silu(x)

def _sigmoid(x):
    return jax.nn.sigmoid(x)

def _layernorm(x, axis=-1, eps=1e-05):
    m = jnp.mean(x, axis=axis, keepdims=True)
    v = jnp.var(x, axis=axis, keepdims=True)
    return (x - m) / jnp.sqrt(v + eps)

def _scatter_add(tgt, idx, src, axis=0):
    return tgt.at[idx].add(src)

def _segment_sum(src, seg, n):
    return jax.ops.segment_sum(src, seg, n)
kernel_name = 'mk_gnn_preln_d2_gnn_r8_9c9a03'

def setup_inputs(seed: int=0):
    np.random.seed(seed)
    _w = jnp.asarray

    def _rec_inputs():
        import jax
        import jax.numpy as jnp
        _gk = jax.random.key(seed)
        x = -0.000202 + 1 * jax.random.normal(jax.random.fold_in(_gk, 1), (6250, 128), jnp.float32)
        _s = jax.random.randint(jax.random.fold_in(_gk, 2), (100000,), 0, 6250, jnp.int32)
        _d = jax.random.randint(jax.random.fold_in(_gk, 3), (100000,), 0, 6250, jnp.int32)
        _loop = jnp.arange(6250, dtype=jnp.int32)
        src = jnp.concatenate([_s, _d, _loop])
        dst = jnp.concatenate([_d, _s, _loop])
        _o = jnp.argsort(dst, stable=True)
        src = src[_o]
        dst = dst[_o]
        edge_attr_64 = 0.000167468 + 1.0002 * jax.random.normal(jax.random.fold_in(_gk, 11), (206250, 64), jnp.float32)
        return (x, src, dst, edge_attr_64)
    x, src, dst, edge_attr_64 = _rec_inputs()

    def _L0_gnn_setup():
        import jax, jax.numpy as jnp
        import numpy as np
        N = 6250
        E = 100000
        IN = 128
        OUT = 32
        H = 4
        NEG_SLOPE = 0.2
        key = jax.random.key(seed)
        k1, k2, k3, k4, k5 = jax.random.split(key, 5)
        x = jax.random.normal(k1, (N, IN), dtype=jnp.float32)
        edge_index = jax.random.randint(k2, (2, E), 0, N, dtype=jnp.int32)
        W = jax.random.normal(k3, (H * OUT, IN), dtype=jnp.float32) * (1.0 / np.sqrt(IN))
        att_src = jax.random.normal(k4, (1, H, OUT), dtype=jnp.float32) * (1.0 / np.sqrt(OUT))
        att_dst = jax.random.normal(k5, (1, H, OUT), dtype=jnp.float32) * (1.0 / np.sqrt(OUT))
        bias = jnp.zeros((H * OUT,), dtype=jnp.float32)
        return {'x': x, 'edge_index': edge_index, 'W': W, 'att_src': att_src, 'att_dst': att_dst, 'bias': bias}
    _L0_gnn_all = _L0_gnn_setup()
    _L0_gnn_in = {k: v for k, v in _L0_gnn_all.items() if k in ('W', 'att_src', 'att_dst', 'bias')}
    del _L0_gnn_all

    def _L1_gnn_setup():
        import jax, jax.numpy as jnp
        import numpy as np
        N_NODES = 12500
        NODE_DIM = 128
        EDGE_DIM = 64
        HIDDEN_DIM = 256
        N_EDGES = 80000
        key = jax.random.key(seed)
        k1, k2, k3, k4, k5, k6, k7 = jax.random.split(key, 7)
        x = jax.random.normal(k1, (N_NODES, NODE_DIM), dtype=jnp.float32)
        edge_index = jax.random.randint(k2, (2, N_EDGES), 0, N_NODES, dtype=jnp.int64)
        edge_attr = jax.random.normal(k3, (N_EDGES, EDGE_DIM), dtype=jnp.float32)
        in_dim = 2 * NODE_DIM + EDGE_DIM
        lim1 = 1.0 / np.sqrt(in_dim)
        lim2 = 1.0 / np.sqrt(HIDDEN_DIM)
        W1 = jax.random.uniform(k4, (in_dim, HIDDEN_DIM), minval=-lim1, maxval=lim1, dtype=jnp.float32)
        b1 = jax.random.uniform(k5, (HIDDEN_DIM,), minval=-lim1, maxval=lim1, dtype=jnp.float32)
        W2 = jax.random.uniform(k6, (HIDDEN_DIM, NODE_DIM), minval=-lim2, maxval=lim2, dtype=jnp.float32)
        b2 = jax.random.uniform(k7, (NODE_DIM,), minval=-lim2, maxval=lim2, dtype=jnp.float32)
        return {'x': x, 'edge_index': edge_index, 'edge_attr': edge_attr, 'W1': W1, 'b1': b1, 'W2': W2, 'b2': b2}
    _L1_gnn_all = _L1_gnn_setup()
    _L1_gnn_in = {k: v for k, v in _L1_gnn_all.items() if k in ('W1', 'b1', 'W2', 'b2')}
    del _L1_gnn_all
    return {'x': x, 'src': src, 'dst': dst, 'edge_attr_64': edge_attr_64, 'L0_gnn_W': _L0_gnn_in['W'], 'L0_gnn_att_src': _L0_gnn_in['att_src'], 'L0_gnn_att_dst': _L0_gnn_in['att_dst'], 'L0_gnn_bias': _L0_gnn_in['bias'], 'L1_gnn_W1': _L1_gnn_in['W1'], 'L1_gnn_b1': _L1_gnn_in['b1'], 'L1_gnn_W2': _L1_gnn_in['W2'], 'L1_gnn_b2': _L1_gnn_in['b2']}

def reference(x, src, dst, edge_attr_64, L0_gnn_W, L0_gnn_att_src, L0_gnn_att_dst, L0_gnn_bias, L1_gnn_W1, L1_gnn_b1, L1_gnn_W2, L1_gnn_b2):
    import jax
    import jax.numpy as jnp

    def _L0_gnn_ref(x, edge_index, W, att_src, att_dst, bias):
        import jax, jax.numpy as jnp
        import numpy as np
        N = 6250
        E = 100000
        IN = 128
        OUT = 32
        H = 4
        NEG_SLOPE = 0.2
        loop = jnp.arange(N, dtype=edge_index.dtype)
        src = jnp.concatenate([edge_index[0], loop])
        dst = jnp.concatenate([edge_index[1], loop])
        h = (x @ W.T).reshape(N, H, OUT)
        a_src = (h * att_src).sum(-1)
        a_dst = (h * att_dst).sum(-1)
        alpha = a_src[src] + a_dst[dst]
        alpha = jax.nn.leaky_relu(alpha, NEG_SLOPE)
        amax = jax.ops.segment_max(alpha, dst, num_segments=N)
        ex = jnp.exp(alpha - amax[dst])
        denom = jax.ops.segment_sum(ex, dst, num_segments=N)
        w = ex / denom[dst]
        msg = h[src] * w[:, :, None]
        out = jax.ops.segment_sum(msg, dst, num_segments=N)
        return out.reshape(N, H * OUT) + bias

    def _L1_gnn_ref(x, edge_index, edge_attr, W1, b1, W2, b2):
        import jax, jax.numpy as jnp
        import numpy as np
        N_NODES = 12500
        NODE_DIM = 128
        EDGE_DIM = 64
        HIDDEN_DIM = 256
        N_EDGES = 80000
        row = edge_index[0]
        col = edge_index[1]
        msg = jnp.concatenate([x[row], x[col], edge_attr], axis=-1)
        h = jax.nn.relu(msg @ W1 + b1)
        msg_out = h @ W2 + b2
        out = jax.ops.segment_sum(msg_out, row, num_segments=x.shape[0])
        return out
    edge_index = jnp.stack([src, dst])
    h = jnp.maximum(_layernorm(x, axis=-1), 0.0)
    x = x + _L0_gnn_ref(h, edge_index, L0_gnn_W, L0_gnn_att_src, L0_gnn_att_dst, L0_gnn_bias)
    h = jnp.maximum(_layernorm(x, axis=-1), 0.0)
    x = x + _L1_gnn_ref(h, edge_index, edge_attr_64, L1_gnn_W1, L1_gnn_b1, L1_gnn_W2, L1_gnn_b2)
    return x

_drawn_inputs = setup_inputs


def setup_inputs(seed=0):
    import zlib

    import numpy as np

    out = dict(_drawn_inputs(seed))
    spreads = {'L0_gnn_bias': (0.0, 0.1)}
    factors = {}
    for name, (base, spread) in spreads.items():
        noise = np.random.default_rng([zlib.crc32(name.encode()), seed]).standard_normal(out[name].shape)
        drawn = base * np.exp(spread * noise) if base else spread * noise
        out[name] = jnp.asarray(drawn.astype(out[name].dtype))
    for name, factor in factors.items():
        out[name] = (out[name] * factor).astype(out[name].dtype)
    return out
```

```python
import concourse.bass as bass
from concourse import mybir
from contextlib import ExitStack

F32 = mybir.dt.float32
BF16 = mybir.dt.bfloat16
I32 = mybir.dt.int32
ALU = mybir.AluOpType
ACT = mybir.ActivationFunctionType
AX = mybir.AxisListType
ENG = mybir.EngineType

P = 128
N = 6250
D = 128
E = 206250
DE = 64
HID = 256
H = 4
DH = D // H
NT = -(-N // P)
NLAST = N - (NT - 1) * P
NPAD = NT * P
T = -(-E // P)
ELAST = E - (T - 1) * P
BT = 26
NB = T // BT
TG = 124
NG = T // TG
TP = T + BT
RB = 28
GW = D + H
XC = D + 2 * H
MW = DH + 2
BIG = 1e30
EPS = 1e-5
SLOPE = 0.2
NC = 7
NCH = NT // NC
PR = 2
GR = PR * P
CP = 2
NS = 4
SB = CP * NS
NPAIR = -(-((E + NT * (GR - 1)) // GR) // SB) * SB
NTURN = NPAIR // SB
XROWS = NPAIR * GR
FILLR = 4 * P
NFILL = -(-(XROWS - E) // FILLR)
XW = HID + 1
PBJ = -(-NPAIR // P)
CK = 512
RK = CK // NT
assert NB * BT == T and NG * TG == T and NCH * NC == NT and NB % 2 == 0


def dims(n):
    return " ".join("abcd"[:n])


def gnn(nc, x, src, dst, ea, W, asrc, adst, bias, W1, b1, W2, b2, out):
    h_tab = nc.dram_tensor("h_tab", (NPAD, GW), F32).ap()
    x_tab = nc.dram_tensor("x_tab", (NPAD, D), F32).ap()
    x1_tab = nc.dram_tensor("x1_tab", (NPAD, D), F32).ap()
    p_tab = nc.dram_tensor("p_tab", (P, NT * 3 * HID), BF16).ap()
    xr = nc.dram_tensor("xr", (XROWS + GR, XW), F32).ap()
    pb_tab = nc.dram_tensor("pb_tab", (P * PBJ,), I32).ap()

    ctx = ExitStack()
    sems = {}
    with ctx:
        WORDS = 53120
        arena = ctx.enter_context(nc.sbuf_tensor("arena", [P, WORDS], F32))
        PSB = [ctx.enter_context(nc.psum_tensor(f"bank{i}", [P, CK], F32)) for i in range(8)]

        def sem(name):
            if name not in sems:
                sems[name] = ctx.enter_context(nc.semaphore(name))
            return sems[name]

        class Region:
            def __init__(self, start, end=WORDS):
                self.at, self.end = start, end

            def __call__(self, shape, dt=F32, parts=P):
                n = 1
                for s in shape:
                    n *= s
                words = -(-n // 2) if dt == BF16 else n
                words = -(-words // 8) * 8
                v = arena[0:parts, self.at:self.at + words]
                if dt != F32:
                    v = v.bitcast(dt)
                v = v[:, 0:n]
                if len(shape) > 1:
                    d = dims(len(shape))
                    v = v.rearrange(f"p ({d}) -> p {d}", **dict(zip(d.split(), shape)))
                self.at += words
                assert self.at <= self.end, (self.at, self.end)
                return v

        K = Region(0)
        ident, ones, iota = K([P]), K([P]), K([2 * P])
        identb, onesb, iota49 = K([P], BF16), K([P], BF16), K([NT], BF16)
        srcE, dBE = K([TP]), K([TP])
        hiE, lastE = K([TP], BF16), K([TP], BF16)
        bin_row = K([(NB + 1) * RB], I32, 1)
        run0, rend, eps = K([NT]), K([NT], I32, 1), K([1])
        mean, rstd = K([NT]), K([NT])
        w1n, w1e, w2_sb = K([2, HID]), K([HID]), K([2, D])
        biasB, b2B, b1r = K([D]), K([D]), K([HID], F32, 1)
        tri, band = K([P], BF16), K([2 * BT + 1], BF16)
        tri27, col27, row26 = K([BT], F32, BT + 1), K([BT + 1], F32, BT + 1), K([1], F32, BT + 1)
        dump = K([1])
        X0 = K.at
        X = Region(X0)
        G, OH = X([2, BT, GW]), X([2, BT, 2 * P])
        Y0 = X.at
        Y = Region(Y0)
        acc = Y([NT + 1, H * MW])
        Y1 = Y.at
        aT = Y([NT + 1, 2 * H])
        s1E, s2E = Y([TP], BF16), Y([TP], BF16)
        thruF, thruB, contN = Y([TP], BF16, 1), Y([TP], BF16, 1), Y([TP], F32, 1)
        zfill = Y([FILLR // P, XW])
        Z0 = Y.at

        S = Region(X0, Y0)
        rI, rF = S([3, NG * P], I32, TG), S([3, NG * P], F32, TG)
        sq = Region(X0, Y0)([NT, D])
        xs = S([NT, D])
        hc, hcT, hx = S([NC, D]), S([NC, P]), S([NC, XC])
        w_sb, wx, att, attb, hm = S([P]), S([XC]), S([2]), S([2 * H]), S([H])
        S = Region(X0 + 3 * NG * P * 2)
        oh49p = S([2, BT, NT], BF16)
        c3, cnt, cnti = S([3, NT]), S([8, NT]), S([2, NT], I32)
        k256, pbc, pbf, pbi = S([PBJ]), S([PBJ, NT]), S([PBJ]), S([PBJ], I32)
        S = Region(Z0)
        isrc, dE, nE = S([TP], I32), S([TP]), S([TP])
        lastr, lflag, tmpr = S([TP], F32, 1), S([TP], F32, 1), S([TP])
        irow = isrc

        S = Region(Z0)
        ohT, msg, idx = S([2, 2 * P]), S([BT, H, MW]), S([2, BT], I32)
        abS, vE, isl4 = S([BT, 2 * H]), S([H, BT]), S([H, BT])
        rb, FT, BK = S([P + 1], F32, H * BT), S([P], F32, H * BT), S([P], F32, H * BT)
        resF, resB = S([H, BT + 1], F32, 1), S([H, BT], F32, 1)
        rowF, rowB = S([H, BT + 1], F32, 1), S([H, BT], F32, 1)
        CF, CB, cin = S([H, BT + 1], F32, 1), S([H, BT], F32, 1), S([2, H, BT], F32, 1)
        y12, ym, R = S([2, H, BT]), S([H, BT]), S([H, BT])
        ZZ, LL, DF, WT = S([3, H, BT]), S([3, H, BT]), S([2, H, BT]), S([2, H, BT])
        ru, fac = S([5, H], F32, 1), S([H])

        Qt = Region(X0, Y0)([NT + 1, 3, HID], BF16)
        S = Region(Y1)
        hs, xi, t1, x1c, sqm, h2, h2T = (S([NC, D]) for _ in range(7))
        den, rec, m7, v7 = S([NC, H]), S([NC, H]), S([NC]), S([NC])
        Pst, res = S([NC, 3, HID], BF16), S([2, 2, HID])

        S = Region(Y0)
        Rb, EAb, EAT = S([2, BT, XW]), S([2, BT, DE]), S([2, P])
        OHb, ohTb, oh49 = S([4, 2 * P], BF16), S([2, 2 * P], BF16), S([2, BT, NT], BF16)
        cnt27, t49, posf, padf, pos = S([2, NT], F32, BT + 1), S([BT, NT]), S([BT]), S([BT]), S([2, BT], I32)

        Pt = Region(X0, Y0)([NT, 3, HID], BF16)
        S = Region(Y0)
        accB, XR, OHp = S([NT, XW]), S([NS, CP, PR * XW]), S([4, PR, P])
        ohTp, hp, hid = S([2, PR, P], BF16), S([2, PR, HID]), S([2, PR, XW])
        pbrow = S([NPAIR + 16], I32, 1)
        S = Region(X0, Y0)
        stg, sT, x1b, fo, fo2 = S([NC, HID]), S([NC, HID]), S([NC, D]), S([NC, D]), S([NC, D])

        ab_ps = PSB[2][:, 0:BT * 2 * H].rearrange("p (t c) -> p t c", c=2 * H)
        vT_ps = PSB[5][0:H * BT, 0:P]
        rT_ps = PSB[5][0:H * BT, P:2 * P]
        BE_ps = PSB[6][:, 0:H * BT].rearrange("p (h t) -> p h t", h=H)
        fac_ps = PSB[6][:, 128:128 + H]
        rows_ps = PSB[7][0:1, 0:2 * H * BT]
        bc_ps = PSB[7][:, 256:256 + 2 * H * BT].rearrange("p (c h t) -> p c h t", c=2, h=H)

        def flat(v):
            d = dims(len(v.shape) - 1)
            return v.rearrange(f"p {d} -> p ({d})") if len(v.shape) > 2 else v

        chunks = [(c, min(c + CK, TP)) for c in range(0, TP, CK)]
        e0 = (NG - 1) * TG * P
        NCONST = 14
        block = ctx.enter_context(nc.Block())

        def bins(engine, b, count):
            return nc.values_load_multi_w_load_instructions(
                bin_row[0:1, bass.ds(b * RB, count)], engines=[engine], min_val=0, max_val=NT - 1,
                skip_runtime_bounds_check_because="a node's tile, clamped at 0")[1]

        def pair_bins(engine, i):
            return nc.values_load_multi_w_load_instructions(
                pbrow[0:1, bass.ds(i * SB, SB + 2)], engines=[engine], min_val=0, max_val=NT - 1,
                skip_runtime_bounds_check_because="counted over the bins, held under their number")[1]

        @block.sync
        def _(sp):
            sp.dma_start(xs[:, 0:NT - 1, :], x[0:(NT - 1) * P, :].rearrange("(n p) f -> p n f", p=P)).then_inc(sem("x_in"), 16)
            sp.wait_ge(sem("xpad"), 1)
            sp.dma_start(xs[0:NLAST, NT - 1, :], x[(NT - 1) * P:N, :]).then_inc(sem("x_in"), 16)
            sp.wait_ge(sem("x_in"), 32)
            sp.dma_start(x_tab.rearrange("(n p) f -> p n f", p=P), xs).then_inc(sem("x_out"), 16)
            sp.wait_ge(sem("zf_ready"), 2)
            for f in range(NFILL):
                r0 = XROWS - (NFILL - f) * FILLR
                sp.dma_start(xr[r0:r0 + FILLR, :].rearrange("(p j) w -> p j w", p=P), zfill).then_inc(sem("filled"), 16)
            sp.wait_ge(sem("pbi_ready"), 1)
            sp.dma_start(pb_tab.rearrange("(p j) -> p j", p=P), pbi).then_inc(sem("pb_out"), 16)
            sp.wait_ge(sem("rend_ready"), 1)
            with sp.Fori(0, NT) as b:
                r = nc.values_load_multi_w_load_instructions(
                    rend[0:1, bass.ds(b, 1)], engines=[ENG.SP], min_val=0, max_val=XROWS,
                    skip_runtime_bounds_check_because="a sum of counts of edges, rounded up")[1][0]
                sp.wait_ge(sem("filled"), 16 * NFILL + 16 * b)
                sp.dma_start(xr[bass.ds(r, GR), :].rearrange("(p j) w -> p j w", p=P), zfill[:, 0:2, :]).then_inc(sem("filled"), 16)
            sp.wait_ge(sem("pb_out"), 16)
            sp.wait_ge(sem("x_out"), 16)
            sp.wait_ge(sem("filled"), 16 * (NFILL + NT))
            sp.wait_ge(sem("acc_done"), 1 + NB * (BT + 1))
            sp.wait_ge(sem("expanded"), (NB + 1) * BT)
            for c in range(NCH):
                rows = lambda v: v[c * NC * P:(c + 1) * NC * P, :].rearrange("(n p) f -> p n f", p=P)
                if c:
                    sp.wait_ge(sem("x1_ready"), c)
                sp.dma_start(hs, rows(h_tab)[:, :, 0:D]).then_inc(sem("hs_in"), 16)
                sp.dma_start(xi, rows(x_tab)).then_inc(sem("hs_in"), 16)
                sp.wait_ge(sem("x1_ready"), c + 1)
                sp.dma_start(rows(x1_tab), x1c).then_inc(sem("x1_out"), 16)
                sp.wait_ge(sem("split_done"), c + 1)
                sp.dma_start(p_tab[:, c * NC * 3 * HID:(c + 1) * NC * 3 * HID], flat(Pst)).then_inc(sem("p_out"), 16)

            def load_ea(b, q, first=False):
                if not first:
                    sp.wait_ge(sem("eaT_ps"), (b - 1) * (BT // 2))
                sp.dma_start(EAb[:, q, :, :], ea[bass.ds(b * (BT * P), BT * P), :].rearrange("(t e) f -> e t f", e=P)).then_inc(sem(f"ea_in{q}"), 16)
            load_ea(0, 0, True)
            load_ea(1, 1, True)
            with sp.Fori(1, NB // 2 - 1) as i:
                for q in range(2):
                    load_ea(2 * i + q, q)
            load_ea(NB - 2, 0)
            sp.wait_ge(sem("eaT_ps"), (NB - 2) * (BT // 2))
            r0 = (NB - 1) * BT * P
            sp.dma_start(EAb[:, 1, 0:BT - 1, :], ea[r0:r0 + (BT - 1) * P, :].rearrange("(t e) f -> e t f", e=P)).then_inc(sem("ea_last"), 16)
            sp.dma_start(EAb[0:ELAST, 1, BT - 1, :], ea[r0 + (BT - 1) * P:E, :]).then_inc(sem("ea_last"), 16)

            sp.wait_ge(sem("main_done"), T)
            sp.dma_start(Pt.rearrange("p a b c -> p (a b c)"), p_tab, max_dma_last_dim=32768).then_inc(sem("pt_in"), 16)
            for q in range(2):
                sp.wait_ge(sem(f"scat{q}"), 16 * BT * (NB // 2))
            sp.wait_ge(sem("pbz"), 1)
            sp.dma_start(pbrow[:, 2:2 + NPAIR], pb_tab[0:NPAIR].rearrange("(a n) -> a n", a=1)).then_inc(sem("pb_in"), 16)

            def load_xr(c, s, first=False):
                if not first:
                    sp.wait_ge(sem("hp_ready"), c * CP - (NS - 1) * CP)
                sp.dma_start(XR[:, s, :, :], xr[bass.ds(c * (CP * GR), CP * GR), :].rearrange("(k p j) w -> p k (j w)", p=P, j=PR)).then_inc(sem(f"xr_in{s}"), 16)
            for s in range(NS):
                load_xr(s, s, True)
            with sp.Fori(1, NTURN) as i:
                for s in range(NS):
                    load_xr(NS * i + s, s)
            sp.wait_ge(sem("accB_done"), NPAIR + 1)
            for c in range(NCH):
                if c:
                    sp.wait_ge(sem("fo_ready"), c)
                sp.dma_start(x1b, x1_tab[c * NC * P:(c + 1) * NC * P, :].rearrange("(n p) f -> p n f", p=P)).then_inc(sem("x1_in"), 16)
                sp.wait_ge(sem("fo_ready"), c + 1)
                full = NC if c < NCH - 1 else NC - 1
                o0 = c * NC * P
                sp.dma_start(out[o0:o0 + full * P, :].rearrange("(n p) f -> p n f", p=P), fo2[:, 0:full, :]).then_inc(sem("stored"), 16)
                if full < NC:
                    sp.dma_start(out[o0 + full * P:N, :], fo2[0:NLAST, full, :]).then_inc(sem("stored"), 16)
            sp.wait_ge(sem("stored"), 16 * (NCH + 1))

        @block.gpsimd
        def _(pool):
            M = nc.gpsimd
            M.memset(rI[:, :, (NG - 1) * P:], -1).then_inc(sem("ipad"), 1)
            M.memset(xs[:, NT - 1, :], 0.0).then_inc(sem("xpad"), 1)
            M.memset(ident, 0.0).then_inc(sem("c0"), 1)
            pool.wait_ge(sem("c0"), 1)
            M.affine_select(out=ident, in_=ident, compare_op=ALU.not_equal, fill=1.0, base=0,
                            pattern=[[-1, P]], channel_multiplier=1).then_inc(sem("c0"), 1)
            M.iota(iota, pattern=[[1, 2 * P]], base=0, channel_multiplier=0,
                   allow_small_or_imprecise_dtypes=True).then_inc(sem("c0"), 1)
            M.iota(iota49, pattern=[[1, NT]], base=0, channel_multiplier=0,
                   allow_small_or_imprecise_dtypes=True).then_inc(sem("c0"), 1)
            M.memset(ones, 1.0).then_inc(sem("c0"), 1)
            M.memset(onesb, 1.0).then_inc(sem("c0"), 1)
            M.memset(eps, EPS).then_inc(sem("c0"), 1)
            pool.wait_ge(sem("c0"), 7)
            M.tensor_copy(identb, ident).then_inc(sem("c0"), 1)
            M.memset(zfill, 0.0).then_inc(sem("zf_ready"), 1)
            pool.wait_ge(sem("zf_ready"), 1)
            M.memset(zfill[:, :, HID:XW], -1.0).then_inc(sem("zf_ready"), 1)
            M.memset(aT[:, NT, :], 0.0).then_inc(sem("aT0"), 1)
            M.memset(acc, 0.0).then_inc(sem("acc_done"), 1)
            for m in (tri, tri27):
                M.memset(m, 1.0).then_inc(sem("c1"), 1)
            for m in (band, col27, row26):
                M.memset(m, 0.0).then_inc(sem("c1"), 1)
            pool.wait_ge(sem("c1"), 5)
            M.affine_select(out=tri, in_=tri, compare_op=ALU.is_gt, fill=0.0, base=0, pattern=[[1, P]], channel_multiplier=-1).then_inc(sem("c1"), 1)
            M.affine_select(out=tri27, in_=tri27, compare_op=ALU.is_gt, fill=0.0, base=0, pattern=[[1, BT]], channel_multiplier=-1).then_inc(sem("c1"), 1)
            M.affine_select(out=row26, in_=row26, compare_op=ALU.not_equal, fill=1.0, base=-BT, pattern=[[0, 1]], channel_multiplier=1).then_inc(sem("c1"), 1)
            M.memset(band[:, BT:BT + 1], 1.0).then_inc(sem("c1"), 1)
            M.memset(col27[:, BT:BT + 1], 1.0).then_inc(sem("c1"), 1)
            M.iota(dump, pattern=[[0, 1]], base=XROWS, channel_multiplier=1, allow_small_or_imprecise_dtypes=True).then_inc(sem("c1"), 1)
            pool.wait_ge(sem("c1"), 11)
            M.affine_select(out=tri27, in_=tri27, compare_op=ALU.not_equal, fill=1.0, base=-BT, pattern=[[0, BT]], channel_multiplier=1).then_inc(sem("c1"), 1)
            pool.wait_ge(sem("hx_used"), NCH)
            M.iota(k256, pattern=[[GR, PBJ]], base=0, channel_multiplier=GR * PBJ,
                   allow_small_or_imprecise_dtypes=True).then_inc(sem("k256_ready"), 1)
            pool.wait_ge(sem("h_out"), 16 * NCH)

            def gather(i, q, first=False):
                pool.wait_ge(sem("idx_ready"), 2 * i + q + 1)
                if not first:
                    pool.wait_ge(sem("msg_ready"), 2 * (2 * i + q - 1))
                pool.nop(nofuse=True)
                for t in range(BT):
                    pool.indirect_dma_start(G[:, q, t, :], None, h_tab,
                                            bass.IndirectOffsetOnAxis(ap=idx[:, q, t:t + 1], axis=0)
                                            ).then_inc(sem(f"gath{q}"), 16)
            gather(0, 0, True)
            gather(0, 1, True)
            with pool.Fori(1, NB // 2) as i:
                for q in range(2):
                    gather(i, q)

            pool.wait_ge(sem("filled"), 16 * (NFILL + NT))
            with pool.Fori(0, NB // 2) as i:
                for q in range(2):
                    n = 2 * i + q + 1
                    pool.wait_ge(sem("pos_ready"), n)
                    pool.wait_ge(sem("r_out"), n * BT)
                    pool.nop(nofuse=True)
                    for t in range(BT):
                        pool.indirect_dma_start(xr, bass.IndirectOffsetOnAxis(ap=pos[:, q, t:t + 1], axis=0),
                                                Rb[:, q, t, :], None).then_inc(sem(f"scat{q}"), 16)

        @block.scalar
        def _(act):
            A = nc.scalar
            act.wait_ge(sem("ipad"), 1)
            for a, (v, off) in enumerate(((src, 0), (dst, 0), (dst, 1))):
                act.dma_start(rI[:, a, 0:(NG - 1) * P].rearrange("p (g e) -> p g e", e=P),
                              v[off:off + e0].rearrange("(g p e) -> p g e", p=TG, e=P)).then_inc(sem("e_in"), 16)
                act.dma_start(rI[0:TG - 1, a, (NG - 1) * P:],
                              v[off + e0:off + e0 + (TG - 1) * P].rearrange("(p e) -> p e", e=P)).then_inc(sem("e_in"), 16)
                act.dma_start(rI[TG - 1:TG, a, (NG - 1) * P:(NG - 1) * P + ELAST - off],
                              v[off + e0 + (TG - 1) * P:E].rearrange("(p e) -> p e", p=1)).then_inc(sem("e_in"), 16)
            act.dma_start(w_sb, W).then_inc(sem("w_in"), 16)
            act.dma_start(att[:, 0:1], asrc.rearrange("a h o -> (h o) a")).then_inc(sem("w_in"), 16)
            act.dma_start(att[:, 1:2], adst.rearrange("a h o -> (h o) a")).then_inc(sem("w_in"), 16)
            act.dma_start(w1n[:, 0, :], W1[0:D, :]).then_inc(sem("w1_in"), 16)
            act.dma_start(w1n[:, 1, :], W1[D:2 * D, :]).then_inc(sem("w1_in"), 16)
            act.dma_start(w1e[0:DE, :], W1[2 * D:, :]).then_inc(sem("w1_in"), 16)
            act.dma_start(w1e[DE:P, :], W1[2 * D:, :]).then_inc(sem("w1_in"), 16)
            act.dma_start(w2_sb, W2.rearrange("(k p) f -> p k f", p=P)).then_inc(sem("w1_in"), 16)
            act.dma_start(biasB, bias.partition_broadcast(P)).then_inc(sem("w1_in"), 16)
            act.dma_start(b2B, b2.partition_broadcast(P)).then_inc(sem("w1_in"), 16)
            act.dma_start(b1r, b1.rearrange("(a n) -> a n", a=1)).then_inc(sem("w1_in"), 16)
            act.wait_ge(sem("xc_ready"), 1)
            act.wait_ge(sem("eT_used"), NG)
            A.activation(sq, xs, ACT.Square).then_inc(sem("sq_ready"), 1)
            act.wait_ge(sem("var_ready"), 1)
            act.wait_ge(sem("c0"), 8)
            A.activation(rstd, mean, ACT.Sqrt, bias=eps, scale=1.0 / D).then_inc(sem("std_ready"), 1)

            def chunk(c, first=False):
                act.wait_ge(sem("hT_ps"), c + 1)
                A.activation(flat(hcT[:, 0:4, :]), PSB[0][:], ACT.Copy)
                A.activation(flat(hcT[:, 4:NC, :]), PSB[1][:, 0:(NC - 4) * P], ACT.Copy).then_inc(sem("hcT_ready"), 1)
                act.wait_ge(sem("hx_ready"), c + 1)
                A.activation(aT[:, bass.ds(c * NC, NC), :], hx[:, :, D:], ACT.Copy).then_inc(sem("hx_used"), 1)
                act.dma_start(h_tab[bass.ds(c * (NC * P), NC * P), :].rearrange("(n p) f -> p n f", p=P),
                              hx[:, :, 0:GW]).then_inc(sem("h_out"), 16)
            with act.Fori(0, NCH) as c:
                chunk(c)

            def turn_out(b, t):
                act.wait_ge(sem("ohT_ps"), b * BT + t + 1)
                if t >= 2:
                    act.wait_ge(sem("expanded"), b * BT + t - 1)
                A.activation(ohT[:, t % 2, :], PSB[t % 2][:, 0:2 * P], ACT.Copy).then_inc(sem("ohT_ready"), 1)

            for t in range(BT):
                turn_out(0, t)
            with act.Fori(0, NB // 2) as i:
                for q in range(2):
                    b = 2 * i + q
                    A.activation(isl4, lastE[:, bass.ds(b * BT, BT)].unsqueeze(1).to_broadcast([P, H, BT]),
                                 ACT.Copy, scale=-BIG).then_inc(sem("isl_ready"), 1)
                    act.wait_ge(sem("expanded"), b * BT + BT)
                    A.activation(abS, ab_ps, ACT.Copy).then_inc(sem("ab_ready"), 1)
                    act.wait_ge(sem("rT_ready"), b + 1)
                    A.activation(rb[:, 1:P + 1], rT_ps, ACT.Copy).then_inc(sem("rb_ready"), 1)
                    act.wait_ge(sem("df_ready"), b + 1)
                    A.activation(WT, DF, ACT.Exp).then_inc(sem("wt_ready"), 1)
                    act.wait_ge(sem("ru_ready"), b + 1)
                    A.activation(ru[:, 4, :], ru[:, 3, :], ACT.Exp).then_inc(sem("f_ready"), 1)
                    for t in range(BT):
                        turn_out(b + 1, t)

            for c in range(NCH):
                act.wait_ge(sem("t_cent"), c + 1)
                A.activation(sqm, t1, ACT.Square).then_inc(sem("sqm_ready"), 1)
                act.wait_ge(sem("v_sum"), c + 1)
                A.activation(m7, v7, ACT.Sqrt, bias=eps, scale=1.0 / D).then_inc(sem("s_ready"), 1)
                act.wait_ge(sem("h2T_ps"), c + 1)
                A.activation(flat(h2T[:, 0:4, :]), PSB[0][:], ACT.Copy)
                A.activation(flat(h2T[:, 4:NC, :]), PSB[1][:, 0:(NC - 4) * P], ACT.Copy).then_inc(sem("h2T_ready"), 1)
                if c:
                    act.wait_ge(sem("p_out"), 16 * c)
                for j in range(NC):
                    n, pq = c * NC + j, PSB[2 + (c * NC + j) % 6]
                    act.wait_ge(sem("pq_ps"), n + 1)
                    A.activation(Pst[:, j, 0, :], pq[:, 0:HID], ACT.Copy)
                    A.activation(Qt[:, n, 0, :], pq[:, HID:], ACT.Copy).then_inc(sem("hi_ready"), 1)
                    act.wait_ge(sem("res_ready"), n + 1)
                    A.activation(Pst[:, j, 1, :], res[:, n % 2, 0, :], ACT.Copy)
                    A.activation(Qt[:, n, 1, :], res[:, n % 2, 1, :], ACT.Copy).then_inc(sem("mid_ready"), 1)

            def turn_outb(b, t, first):
                g = b * BT + t
                act.wait_ge(sem("bT_ps"), g + 1)
                if not (first and t < 2):
                    act.wait_ge(sem("main_done"), g - 1)
                A.activation(ohTb[:, t % 2, :], PSB[t % 2][:].bitcast(BF16)[:, 0:2 * P], ACT.Copy).then_inc(sem("bT_ready"), 1)

            def rows_out(b, q, t):
                act.wait_ge(sem("main_done"), b * BT + t + 1)
                A.activation(Rb[:, q, t, 0:HID], PSB[2 + t % 2][:, 0:HID], ACT.Copy).then_inc(sem("r_out"), 1)

            def targets(i, q, first=False):
                b = 2 * i + q
                turn_outb(b, 0, first and q == 0)
                if not first:
                    act.wait_ge(sem(f"scat{q}"), 16 * BT * i)
                act.wait_ge(sem("c27_ps"), b + 1)
                A.activation(cnt27[:, 1 - q, :], PSB[7][0:BT + 1, 0:NT], ACT.Copy).then_inc(sem("c27_ready"), 1)
                for t in range(BT):
                    if t < BT - 1:
                        turn_outb(b, t + 1, first and q == 0)
                    rows_out(b, q, t)
            targets(0, 0, True)
            targets(0, 1, True)
            with act.Fori(1, NB // 2) as i:
                for q in range(2):
                    targets(i, q)

            def turn_outp(g, m, first):
                act.wait_ge(sem("pT_ps"), g + 1)
                if not (first and m < 2):
                    act.wait_ge(sem("pp_ps"), g - 1)
                A.activation(flat(ohTp[:, m % 2, :, :]), PSB[m % 2][:, 0:PR * P], ACT.Copy).then_inc(sem("pT_ready"), 1)

            def relu(g, m, first):
                act.wait_ge(sem("hp_ready"), g + 1)
                if not (first and m < 2):
                    act.wait_ge(sem("seg_ps"), g - 1)
                A.activation(hid[:, m % 2, :, 0:HID], hp[:, m % 2, :, :], ACT.Relu).then_inc(sem("hid_ready"), 1)

            def sources(i, first=False):
                for m in range(SB):
                    turn_outp(SB * i + m, m, first)
                    if not (first and m < 1):
                        relu(SB * i + m - 1, (m - 1) % SB, first and m > 0)
            sources(0, True)
            with act.Fori(1, NTURN) as i:
                sources(i)
            relu(NPAIR - 1, SB - 1, False)
            for c in range(NCH):
                if c:
                    act.wait_ge(sem("sT_ps"), c)
                else:
                    act.wait_ge(sem("accB_done"), NPAIR + 1)
                A.activation(stg, accB[:, c * NC:(c + 1) * NC, 0:HID], ACT.Copy).then_inc(sem("stg_ready"), 1)
                act.wait_ge(sem("sT_ps"), c + 1)
                if c:
                    act.wait_ge(sem("fo_ps"), c)
                for m in range(4):
                    n = min(2, NC - 2 * m)
                    last = A.activation(flat(sT[:, 2 * m:2 * m + n, :]), PSB[m][:, 0:n * HID], ACT.Copy)
                last.then_inc(sem("sT_ready"), 1)

        @block.vector
        def _(dve):
            V = nc.vector
            k = [0]

            def link(ins):
                k[0] += 1
                ins.then_inc(sem("dve_prep"), 1)
                dve.wait_ge(sem("dve_prep"), k[0])

            link(V.memset(hm, 0.0))
            for h in range(H):
                V.memset(hm[h * DH:(h + 1) * DH, h:h + 1], 1.0)
            V.memset(srcE[:, T:], -1.0)
            V.memset(dE[:, T:], -1.0)
            V.memset(nE[:, T:], -1.0)
            dve.wait_ge(sem("e_in"), 16 * 9)
            V.tensor_copy(rF, rI).then_inc(sem("rF_ready"), 1)
            dve.wait_ge(sem("x_in"), 32)
            link(V.tensor_reduce(mean, xs, AX.X, ALU.add))
            link(V.tensor_scalar(rstd, mean, 1.0 / D, None, ALU.mult))
            dve.wait_ge(sem("x_out"), 16)
            V.tensor_tensor(xs, xs, rstd.unsqueeze(2).to_broadcast([P, NT, D]), ALU.subtract).then_inc(sem("xc_ready"), 1)
            for g in range(NG):
                dve.wait_ge(sem("eT_ps"), g + 1)
                v = PSB[2 + g % 2][:, 0:3 * TG].rearrange("p (a t) -> p a t", a=3)
                V.tensor_copy(srcE[:, g * TG:(g + 1) * TG], v[:, 0, :])
                V.tensor_copy(dE[:, g * TG:(g + 1) * TG], v[:, 1, :])
                V.tensor_copy(nE[:, g * TG:(g + 1) * TG], v[:, 2, :]).then_inc(sem("eT_used"), 1)
            dve.wait_ge(sem("sq_ready"), 1)
            V.tensor_reduce(mean, sq, AX.X, ALU.add).then_inc(sem("var_ready"), 1)
            dve.wait_ge(sem("w_in"), 48)
            dve.wait_ge(sem("c0"), 8)
            V.tensor_scalar(attb[:, 0:H], hm, att[:, 0:1], None, ALU.mult)
            V.tensor_scalar(attb[:, H:], hm, att[:, 1:2], None, ALU.mult).then_inc(sem("attb_ready"), 1)
            dve.wait_ge(sem("wx_ps"), 1)
            V.tensor_copy(wx, PSB[4][:, 0:XC]).then_inc(sem("wx_ready"), 1)
            dve.wait_ge(sem("std_ready"), 1)
            link(V.reciprocal(mean, rstd))

            def chunk(c, first=False):
                if not first:
                    dve.wait_ge(sem("hT_ps"), c)
                V.scalar_tensor_tensor(hc, xs[:, bass.ds(c * NC, NC), :], 0.0,
                                       mean[:, bass.ds(c * NC, NC)].unsqueeze(2).to_broadcast([P, NC, D]),
                                       ALU.max, ALU.mult).then_inc(sem("hc_ready"), 1)
                dve.wait_ge(sem("hx_ps"), c + 1)
                if not first:
                    dve.wait_ge(sem("hx_used"), c)
                    dve.wait_ge(sem("h_out"), 16 * c)
                V.tensor_copy(hx[:, 0:3, :], PSB[5][:, 0:3 * XC].rearrange("p (j f) -> p j f", j=3))
                V.tensor_copy(hx[:, 3:6, :], PSB[6][:, 0:3 * XC].rearrange("p (j f) -> p j f", j=3))
                V.tensor_copy(hx[:, 6, :], PSB[7][:, 0:XC]).then_inc(sem("hx_ready"), 1)
            chunk(0, True)
            with dve.Fori(1, NCH) as c:
                chunk(c)

            link(V.tensor_tensor(tmpr, nE, dE, ALU.not_equal))
            V.tensor_copy(lastE, tmpr).then_inc(sem("last_ready"), 1)
            link(V.tensor_copy(isrc, srcE))
            link(V.tensor_scalar(isrc, isrc, 7, None, ALU.arith_shift_right))
            link(V.tensor_copy(hiE, isrc))
            for j, (lo, hi) in enumerate(chunks):
                dve.wait_ge(sem("rows_ps"), 2 * j + 2)
                V.tensor_copy(lastr[:, lo:hi], PSB[2][0:1, 0:hi - lo])
                V.tensor_copy(lflag[:, lo:hi], PSB[3][0:1, 0:hi - lo]).then_inc(sem("rows_used"), 1)
            dve.wait_ge(sem("rows_used"), len(chunks))
            V.memset(contN[:, 0:1], -BIG)
            V.tensor_scalar(contN[:, 1:], lflag[:, 0:TP - 1], -BIG, None, ALU.mult).then_inc(sem("cont_ready"), 1)
            dve.wait_ge(sem("cont_ready"), 1)
            link(V.tensor_tensor(lflag, dE[0:1, :], lastr, ALU.not_equal))
            link(V.tensor_scalar(lflag, lflag, -BIG, None, ALU.mult))
            V.tensor_tensor(thruF, contN, lflag, ALU.min)
            V.tensor_tensor(thruB[:, 0:TP - 1], contN[:, 1:], lflag[:, 0:TP - 1], ALU.min)
            ir = irow[0:1, :]
            link(V.tensor_copy(ir, dE[0:1, :]))
            link(V.tensor_scalar(ir, ir, 7, None, ALU.arith_shift_right))
            link(V.tensor_scalar(ir, ir, 0, None, ALU.max))
            V.tensor_copy(bin_row.rearrange("p (b t) -> p b t", t=RB)[:, :, 0:BT],
                          ir.rearrange("p (b t) -> p b t", t=BT)).then_inc(sem("bins_ready"), 1)
            V.tensor_scalar(tmpr[0:1, :], ir, float(P), None, ALU.mult).then_inc(sem("binf_ready"), 1)
            for j, (lo, hi) in enumerate(chunks):
                dve.wait_ge(sem("cols_ps"), j + 1)
                V.tensor_tensor(dBE[:, lo:hi], dE[:, lo:hi], PSB[4][:, 0:hi - lo], ALU.subtract)
                V.tensor_tensor(s1E[:, lo:hi], dE[:, lo:hi], PSB[5][:, 0:hi - lo], ALU.not_equal)
                V.tensor_tensor(s2E[:, lo:hi], dE[:, lo:hi], PSB[6][:, 0:hi - lo], ALU.not_equal).then_inc(sem("cols_used"), 1)
            dve.wait_ge(sem("cols_used"), len(chunks))
            V.tensor_scalar(s1E, s1E, -BIG, None, ALU.mult)
            link(V.tensor_scalar(s2E, s2E, -BIG, None, ALU.mult))

            def hot49(b, s, first=False):
                if not first:
                    dve.wait_ge(sem("counted"), b - 1)
                V.tensor_tensor(oh49p[:, s, :, :], hiE[:, bass.ds(b * BT, BT)].unsqueeze(2).to_broadcast([P, BT, NT]),
                                iota49.unsqueeze(1).to_broadcast([P, BT, NT]), ALU.is_equal).then_inc(sem("oh49_ready"), 1)
            hot49(0, 0, True)
            hot49(1, 1, True)
            with dve.Fori(1, NB // 2) as i:
                for q in range(2):
                    hot49(2 * i + q, q)
            dve.wait_ge(sem("counted"), NB)
            for m, tiles in enumerate((RK, RK, BT - 2 * RK)):
                last = V.tensor_reduce(c3[:, m, :], PSB[5 + m][:, 0:tiles * NT].rearrange("p (t b) -> p b t", b=NT), AX.X, ALU.add)
            link(last)
            link(V.tensor_tensor(cnt[:, 0, :], c3[:, 0, :], c3[:, 1, :], ALU.add))
            link(V.tensor_tensor(cnt[:, 1, :], cnt[:, 0, :], c3[:, 2, :], ALU.add))
            link(V.tensor_scalar(cnt[:, 2, :], cnt[:, 1, :], float(GR - 1), None, ALU.add))
            link(V.tensor_copy(cnti[:, 0, :], cnt[:, 2, :]))
            link(V.tensor_scalar(cnti[:, 1, :], cnti[:, 0, :], 8, None, ALU.arith_shift_right))
            link(V.tensor_copy(cnt[:, 3, :], cnti[:, 1, :]))
            link(V.tensor_scalar(cnt[:, 4, :], cnt[:, 3, :], float(GR), None, ALU.mult))
            link(V.memset(cnt[:, 5, :], 1.0))
            link(V.tensor_tensor_scan(cnt[:, 6, :], cnt[:, 5, :], cnt[:, 4, :], 0.0, ALU.mult, ALU.add))
            link(V.tensor_tensor(run0, cnt[:, 6, :], cnt[:, 4, :], ALU.subtract))
            link(V.tensor_tensor(cnt[:, 7, :], run0, cnt[:, 1, :], ALU.add))
            V.tensor_copy(rend, cnt[0:1, 7, :]).then_inc(sem("rend_ready"), 1)
            dve.wait_ge(sem("k256_ready"), 1)
            link(V.tensor_tensor(pbc, cnt[:, 6, :].unsqueeze(1).to_broadcast([P, PBJ, NT]),
                                 k256.unsqueeze(2).to_broadcast([P, PBJ, NT]), ALU.is_le))
            link(V.tensor_reduce(pbf, pbc, AX.X, ALU.add))
            link(V.tensor_scalar(pbf, pbf, float(NT - 1), None, ALU.min))
            V.tensor_copy(pbi, pbf).then_inc(sem("pbi_ready"), 1)

            dve.wait_ge(sem("pb_out"), 16)
            V.memset(rb, -BIG)
            V.memset(resF, -BIG)
            V.memset(resB, -BIG)
            V.memset(CF, -BIG)
            link(V.memset(cin, -BIG))

            def indices(b, s):
                V.tensor_scalar(idx[:, s, :], srcE[:, bass.ds(b * BT, BT)], 0.0, None, ALU.max).then_inc(sem("idx_ready"), 1)

            def hot(b, s, t):
                V.tensor_scalar(OH[:, s, t, :], iota, dBE[:, bass.ds(b * BT + t, 1)], None, ALU.is_equal).then_inc(sem("oh_ready"), 1)
            indices(0, 0)
            for t in range(BT):
                hot(0, 0, t)

            def weights(i, q):
                b, n = 2 * i + q, 2 * i + q + 1
                B = b * BT
                row = lambda v: v[:, bass.ds(B, BT)].unsqueeze(1).to_broadcast([1, H, BT])
                V.tensor_copy(resF[:, :, 1:], row(thruF))
                V.tensor_copy(resB[:, :, 0:BT - 1], thruB[:, bass.ds(B, BT - 1)].unsqueeze(1).to_broadcast([1, H, BT - 1]))
                V.tensor_copy(rowF[:, :, 0:1], CF[:, :, BT:]).then_inc(sem("rres_ready"), 1)
                dve.wait_ge(sem(f"gath{q}"), 16 * BT * (i + 1))
                dve.wait_ge(sem("ab_ready"), n)
                g4 = G[:, q, :, D:GW].rearrange("p t h -> p h t")
                as4 = abS[:, :, 0:H].rearrange("p t h -> p h t")
                ad4 = abS[:, :, H:].rearrange("p t h -> p h t")
                V.tensor_tensor(vE, g4, as4, ALU.max).then_inc(sem("v_ready"), 1)
                indices(b + 1, 1 - q)
                V.tensor_tensor(ZZ[:, 0, :, :], g4, ad4, ALU.add)
                V.tensor_tensor(ZZ[:, 1, :, :], as4, ad4, ALU.add)
                dve.wait_ge(sem("vT_ready"), n)
                dve.wait_ge(sem("rb_ready"), n)
                V.tensor_tensor_scan(FT, rb[:, 0:P], vT_ps, -BIG, ALU.add, ALU.max).then_inc(sem("ft_ready"), 1)
                dve.wait_ge(sem("ft_ready"), n)
                V.tensor_tensor_scan(BK[:, ::-1], rb[:, 1:P + 1][:, ::-1], FT[:, ::-1], -BIG, ALU.add, ALU.max).then_inc(sem("bk_ready"), 1)
                dve.wait_ge(sem("rows_ready"), n)
                V.tensor_copy(rowF[:, :, 1:], rows_ps[:, 0:H * BT].rearrange("p (h t) -> p h t", h=H))
                V.tensor_copy(rowB, rows_ps[:, H * BT:].rearrange("p (h t) -> p h t", h=H)).then_inc(sem("row_ready"), 1)
                dve.wait_ge(sem("row_ready"), n)
                V.tensor_tensor_scan(flat(CF), flat(resF), flat(rowF), -BIG, ALU.add, ALU.max)
                V.tensor_tensor_scan(flat(CB)[:, ::-1], flat(resB)[:, ::-1], flat(rowB)[:, ::-1], -BIG, ALU.add, ALU.max).then_inc(sem("carry_ready"), 1)
                dve.wait_ge(sem("carry_ready"), n)
                V.tensor_tensor(cin[:, 0, :, :], CF[:, :, 0:BT], row(contN), ALU.add)
                V.tensor_tensor(cin[:, 1, :, 0:BT - 1], CB[:, :, 1:],
                                contN[:, bass.ds(B + 1, BT - 1)].unsqueeze(1).to_broadcast([1, H, BT - 1]), ALU.add).then_inc(sem("cin_ready"), 1)
                dve.wait_ge(sem("bc_ready"), n)
                col = lambda v: v[:, bass.ds(B, BT)].unsqueeze(1).to_broadcast([P, H, BT])
                V.tensor_tensor(y12[:, 0, :, :], bc_ps[:, 0, :, :], col(s1E), ALU.add)
                V.tensor_tensor(y12[:, 1, :, :], bc_ps[:, 1, :, :], col(s2E), ALU.add).then_inc(sem("y_ready"), 1)
                dve.wait_ge(sem("y_ready"), n)
                V.tensor_tensor(ym, y12[:, 0, :, :], y12[:, 1, :, :], ALU.max).then_inc(sem("ym_ready"), 1)
                dve.wait_ge(sem("ym_ready"), n)
                V.tensor_tensor(R, ym, BE_ps, ALU.max).then_inc(sem("R_ready"), 1)
                dve.wait_ge(sem("R_ready"), n)
                V.tensor_tensor(ZZ[:, 2, :, :], R, ad4, ALU.add).then_inc(sem("Z_ready"), 1)
                V.tensor_tensor(ru[:, 0, :], cin[:, 0, :, 0], abS[0:1, 0, H:], ALU.add).then_inc(sem("r_step"), 1)
                dve.wait_ge(sem("Z_ready"), n)
                V.scalar_tensor_tensor(flat(LL), flat(ZZ), SLOPE, flat(ZZ), ALU.mult, ALU.max).then_inc(sem("L_ready"), 1)
                dve.wait_ge(sem("L_ready"), n)
                V.tensor_tensor(DF, LL[:, 0:2, :, :], LL[:, 2, :, :].unsqueeze(1).to_broadcast([P, 2, H, BT]), ALU.subtract).then_inc(sem("df_ready"), 1)
                V.scalar_tensor_tensor(ru[:, 1, :], ru[:, 0, :], SLOPE, ru[:, 0, :], ALU.mult, ALU.max).then_inc(sem("r_step"), 1)
                dve.wait_ge(sem("r_step"), 4 * b + 2)
                V.tensor_tensor(ru[:, 2, :], ru[:, 1, :], LL[0:1, 2, :, 0], ALU.subtract).then_inc(sem("r_step"), 1)
                dve.wait_ge(sem("r_step"), 4 * b + 3)
                V.tensor_scalar(ru[:, 3, :], ru[:, 2, :], -1e4, None, ALU.max).then_inc(sem("ru_ready"), 1)
                dve.wait_ge(sem("wt_ready"), n)
                wt = WT.rearrange("p s h t -> p s t h")
                V.tensor_copy(msg[:, :, :, DH], wt[:, 0, :, :])
                V.tensor_tensor(msg[:, :, :, DH + 1], wt[:, 1, :, :],
                                lastE[:, bass.ds(B, BT)].unsqueeze(2).to_broadcast([P, BT, H]), ALU.mult)
                dve.wait_ge(sem("f_ready"), n)
                V.tensor_scalar(ru[:, 2, :], ru[:, 4, :], -1.0, None, ALU.add).then_inc(sem("g_ready"), 1)
                for lo, hi in ((0, BT // 2), (BT // 2, BT)):
                    last = V.tensor_tensor(msg[:, lo:hi, :, 0:DH], G[:, q, lo:hi, 0:D].rearrange("p t (h o) -> p t h o", h=H),
                                           wt[:, 0, lo:hi, :].unsqueeze(3).to_broadcast([P, hi - lo, H, DH]), ALU.mult)
                    last.then_inc(sem("msg_ready"), 1)
                regs = bins(ENG.DVE, b, BT)
                dve.wait_ge(sem("fac_ps"), n)
                V.tensor_scalar(fac, fac_ps, 1.0, None, ALU.add).then_inc(sem("r_step"), 1)
                dve.wait_ge(sem("r_step"), 4 * b + 4)
                a = acc[:, bass.ds(regs[0], 1), :].rearrange("p a (h m) -> p (a h) m", h=H)
                V.tensor_tensor(a, a, fac.unsqueeze(2).to_broadcast([P, H, MW]), ALU.mult).then_inc(sem("acc_done"), 1)
                return regs

            def add_up(b, t, regs):
                dve.wait_ge(sem("agg_ready"), b * BT + t + 1)
                dve.wait_ge(sem("acc_done"), b * (BT + 1) + 2 + t)
                a = flat(acc[:, bass.ds(regs[t], 2), :])
                V.tensor_tensor(a, a, PSB[3 + t % 2][:, 0:2 * H * MW], ALU.add).then_inc(sem("acc_done"), 1)

            dve.wait_ge(sem("acc_done"), 1)
            with dve.Fori(0, NB // 2) as i:
                for q in range(2):
                    b = 2 * i + q
                    regs = weights(i, q)
                    for t in range(BT):
                        hot(b + 1, 1 - q, t)
                        if t:
                            add_up(b, t - 1, regs)
                    add_up(b, BT - 1, regs)

            V.memset(Qt[:, NT, :, :], 0.0)
            dve.wait_ge(sem("w1_in"), 16 * 8)
            for c in range(NCH):
                a = acc[:, c * NC:(c + 1) * NC, :].rearrange("p n (h m) -> p n h m", h=H)
                hv = lambda v: v.rearrange("p n (h o) -> p n h o", h=H)
                wide = lambda v: v.unsqueeze(3).to_broadcast([P, NC, H, DH])
                link(V.tensor_tensor(den, a[:, :, :, DH], a[:, :, :, DH + 1], ALU.add))
                link(V.tensor_scalar(den, den, 1e-30, None, ALU.max))
                V.reciprocal(rec, den)
                dve.wait_ge(sem("hs_in"), 32 * (c + 1))
                link(V.tensor_tensor(hv(t1), hv(hs), wide(a[:, :, :, DH + 1]), ALU.mult))
                link(V.tensor_tensor(hv(t1), hv(t1), a[:, :, :, 0:DH], ALU.add))
                link(V.tensor_tensor(hv(t1), hv(t1), wide(rec), ALU.mult))
                link(V.tensor_tensor(t1, t1, biasB.unsqueeze(1).to_broadcast([P, NC, D]), ALU.add))
                if c:
                    dve.wait_ge(sem("x1_out"), 16 * c)
                V.tensor_tensor(x1c, t1, xi, ALU.add).then_inc(sem("x1_ready"), 1)
                dve.wait_ge(sem("x1_ready"), c + 1)
                link(V.tensor_reduce(v7, x1c, AX.X, ALU.add))
                link(V.tensor_scalar(v7, v7, 1.0 / D, None, ALU.mult))
                V.tensor_tensor(t1, x1c, v7.unsqueeze(2).to_broadcast([P, NC, D]), ALU.subtract).then_inc(sem("t_cent"), 1)
                dve.wait_ge(sem("sqm_ready"), c + 1)
                V.tensor_reduce(v7, sqm, AX.X, ALU.add).then_inc(sem("v_sum"), 1)
                dve.wait_ge(sem("s_ready"), c + 1)
                link(V.reciprocal(v7, m7))
                V.scalar_tensor_tensor(h2, t1, 0.0, v7.unsqueeze(2).to_broadcast([P, NC, D]), ALU.max, ALU.mult).then_inc(sem("h2_ready"), 1)
                for j in range(NC):
                    n, pq = c * NC + j, PSB[2 + (c * NC + j) % 6]
                    dve.wait_ge(sem("hi_ready"), n + 1)
                    V.tensor_tensor(res[:, n % 2, 0, :], pq[:, 0:HID], Pst[:, j, 0, :], ALU.subtract)
                    V.tensor_tensor(res[:, n % 2, 1, :], pq[:, HID:], Qt[:, n, 0, :], ALU.subtract).then_inc(sem("res_ready"), 1)
                    dve.wait_ge(sem("mid_ready"), n + 1)
                    V.tensor_tensor(Pst[:, j, 2, :], res[:, n % 2, 0, :], Pst[:, j, 1, :], ALU.subtract)
                    last = V.tensor_tensor(Qt[:, n, 2, :], res[:, n % 2, 1, :], Qt[:, n, 1, :], ALU.subtract)
                    if j < NC - 1:
                        last.then_inc(sem("lo_ready"), 1)
                last.then_inc(sem("split_done"), 1)

            V.tensor_scalar(cnt27[:, 0, :], run0[0:BT + 1, :], row26, None, ALU.mult).then_inc(sem("c27_init"), 1)

            def targets(i, q, first=False):
                b, n = 2 * i + q, 2 * i + q + 1
                B = b * BT
                hi = hiE[:, bass.ds(B, BT)]
                V.tensor_tensor(oh49[:, q, :, :], hi.unsqueeze(2).to_broadcast([P, BT, NT]),
                                iota49.unsqueeze(1).to_broadcast([P, BT, NT]), ALU.is_equal).then_inc(sem("b49_ready"), 1)
                if not (first and q == 0):
                    dve.wait_ge(sem("pos_ready"), b)
                V.tensor_scalar(padf, hi, 0.0, dump, ALU.is_lt, ALU.mult)
                if not first:
                    dve.wait_ge(sem(f"scat{q}"), 16 * BT * i)
                V.scalar_tensor_tensor(Rb[:, q, :, HID], hi, -float(P), srcE[:, bass.ds(B, BT)], ALU.mult, ALU.add)

                def hotb(t):
                    g = B + t
                    if not (first and q == 0 and t < 4):
                        dve.wait_ge(sem("bT_ps"), g - 3)
                    V.tensor_scalar(OHb[:, (t + 2 * q) % 4, :], iota, dBE[:, bass.ds(g, 1)], None, ALU.is_equal).then_inc(sem("ohb_ready"), 1)

                def ea_out(j):
                    Gp = b * (BT // 2) + j
                    dve.wait_ge(sem("eaT_ps"), Gp + 1)
                    if not (first and q == 0 and j < 2):
                        dve.wait_ge(sem("main_done"), 2 * Gp - 2)
                    V.tensor_copy(EAT[:, (j + q) % 2, :], PSB[4][:, 0:P]).then_inc(sem("ea_out"), 1)

                def rank(m):
                    lo, hi_ = m * RK, min((m + 1) * RK, BT)
                    dve.wait_ge(sem("rk_ps"), 3 * b + m + 1)
                    V.tensor_tensor(t49[:, lo:hi_, :], PSB[5 + m % 2][:, 0:(hi_ - lo) * NT].rearrange("p (t b) -> p t b", b=NT),
                                    oh49[:, q, lo:hi_, :], ALU.mult).then_inc(sem("rk_used"), 1)
                hotb(0)
                hotb(1)
                for t in range(BT):
                    if t % 2 == 0:
                        ea_out(t // 2)
                    if t < BT - 2:
                        hotb(t + 2)
                    if t in (4, 8, 18):
                        rank({4: 0, 8: 1, 18: 2}[t])
                    if t == 20:
                        dve.wait_ge(sem("rk_used"), 3 * n)
                        V.tensor_reduce(posf, t49, AX.X, ALU.add).then_inc(sem("posf_ready"), 1)
                    if t == 22:
                        dve.wait_ge(sem("posf_ready"), n)
                        V.tensor_tensor(pos[:, q, :], posf, padf, ALU.add).then_inc(sem("pos_ready"), 1)
            targets(0, 0, True)
            targets(0, 1, True)
            with dve.Fori(1, NB // 2) as i:
                for q in range(2):
                    targets(i, q)

            for q in range(2):
                dve.wait_ge(sem(f"scat{q}"), 16 * BT * (NB // 2))
            V.memset(pbrow, 0).then_inc(sem("pbz"), 1)
            V.memset(hid[:, :, :, HID:], 1.0)
            V.memset(accB, 0.0).then_inc(sem("accB_done"), 1)
            dve.wait_ge(sem("accB_done"), 1)
            dve.wait_ge(sem("pb_in"), 16)

            def hotp(i, m, first):
                s, k, g = m // CP, m % CP, SB * i + m
                if k == 0:
                    dve.wait_ge(sem(f"xr_in{s}"), 16 * (i + 1))
                if not (first and m < 4):
                    dve.wait_ge(sem("seg_ps"), g - 3)
                for j in range(PR):
                    c = j * XW + HID
                    last = V.tensor_scalar(OHp[:, m % 4, j, :], iota[:, 0:P], XR[:, s, k, c:c + 1], None, ALU.is_equal)
                last.then_inc(sem("ohp_ready"), 1)

            def add_r(g, m, first):
                s, k = m // CP, m % CP
                dve.wait_ge(sem("pp_ps"), g + 1)
                if not (first and m < 2):
                    dve.wait_ge(sem("hid_ready"), g - 1)
                V.tensor_tensor(hp[:, m % 2, :, :], PSB[2 + m % 2][:].rearrange("p (j h) -> p j h", j=PR),
                                XR[:, s, k, :].rearrange("p (j w) -> p j w", j=PR)[:, :, 0:HID], ALU.add).then_inc(sem("hp_ready"), 1)

            def add_up(g, m, reg):
                dve.wait_ge(sem("seg_ps"), g + 1)
                dve.wait_ge(sem("accB_done"), g + 1)
                a = flat(accB[:, bass.ds(reg, 1), :])
                V.tensor_tensor(a, a, PSB[4 + m % 2][:, 0:XW], ALU.add).then_inc(sem("accB_done"), 1)

            def sources(i, first=False):
                regs = pair_bins(ENG.DVE, i)
                for m in range(SB):
                    hotp(i, m, first)
                    if not (first and m < 1):
                        add_r(SB * i + m - 1, (m - 1) % SB, first)
                    if not (first and m < 2):
                        add_up(SB * i + m - 2, (m - 2) % SB, regs[m])
            sources(0, True)
            with dve.Fori(1, NTURN) as i:
                sources(i)
            regs = pair_bins(ENG.DVE, NTURN)
            add_r(NPAIR - 1, SB - 1, False)
            add_up(NPAIR - 2, SB - 2, regs[0])
            add_up(NPAIR - 1, SB - 1, regs[1])
            dve.wait_ge(sem("accB_done"), NPAIR + 1)
            for c in range(NCH):
                if c:
                    dve.wait_ge(sem("fo_ready"), c)
                link(V.tensor_tensor(fo, b2B.unsqueeze(1).to_broadcast([P, NC, D]),
                                     accB[:, c * NC:(c + 1) * NC, HID:].to_broadcast([P, NC, D]), ALU.mult))
                dve.wait_ge(sem("x1_in"), 16 * (c + 1))
                link(V.tensor_tensor(fo, fo, x1b, ALU.add))
                dve.wait_ge(sem("fo_ps"), c + 1)
                if c:
                    dve.wait_ge(sem("stored"), 16 * c)
                V.tensor_tensor(flat(fo2[:, 0:4, :]), flat(fo[:, 0:4, :]), PSB[4][:], ALU.add)
                V.tensor_tensor(flat(fo2[:, 4:NC, :]), flat(fo[:, 4:NC, :]), PSB[5][:, 0:(NC - 4) * D], ALU.add).then_inc(sem("fo_ready"), 1)

        @block.tensor
        def _(pe):
            pe.wait_ge(sem("c0"), 8)
            pe.wait_ge(sem("rF_ready"), 1)
            for g in range(NG):
                if g >= 2:
                    pe.wait_ge(sem("eT_used"), g - 1)
                for a in range(3):
                    last = pe.transpose(PSB[2 + g % 2][:, a * TG:(a + 1) * TG], rF[:, a, g * P:(g + 1) * P], ident[0:TG, 0:TG])
                last.then_inc(sem("eT_ps"), 1)
            pe.wait_ge(sem("w_in"), 48)
            pe.transpose(PSB[4][:, 0:D], w_sb, ident)
            pe.wait_ge(sem("attb_ready"), 1)
            pe.matmul(PSB[4][:, D:XC], w_sb, attb, start=True, stop=True).then_inc(sem("wx_ps"), 1)
            pe.wait_ge(sem("wx_ready"), 1)

            def chunk(c, first=False):
                pe.wait_ge(sem("hc_ready"), c + 1)
                for j in range(NC):
                    last = pe.transpose(PSB[j // 4][:, (j % 4) * P:(j % 4 + 1) * P], hc[:, j, :], ident)
                last.then_inc(sem("hT_ps"), 1)
                pe.wait_ge(sem("hcT_ready"), c + 1)
                if not first:
                    pe.wait_ge(sem("hx_ready"), c)
                for j in range(NC):
                    last = pe.matmul(PSB[5 + j // 3][:, (j % 3) * XC:(j % 3 + 1) * XC], hcT[:, j, :], wx, start=True, stop=True)
                last.then_inc(sem("hx_ps"), 1)
            chunk(0, True)
            with pe.Fori(1, NCH) as c:
                chunk(c)

            last127 = ident[:, P - 1:P]
            pe.wait_ge(sem("last_ready"), 1)
            for j, (lo, hi) in enumerate(chunks):
                if j:
                    pe.wait_ge(sem("rows_used"), j)
                pe.matmul(PSB[2][0:1, 0:hi - lo], last127, dE[:, lo:hi], start=True, stop=True).then_inc(sem("rows_ps"), 1)
                pe.matmul(PSB[3][0:1, 0:hi - lo], last127, tmpr[:, lo:hi], start=True, stop=True).then_inc(sem("rows_ps"), 1)
            pe.wait_ge(sem("binf_ready"), 1)
            for j, (lo, hi) in enumerate(chunks):
                if j:
                    pe.wait_ge(sem("cols_used"), j)
                pe.matmul(PSB[4][:, 0:hi - lo], ones[0:1, :], tmpr[0:1, lo:hi], start=True, stop=True)
                pe.matmul(PSB[5][:, 0:hi - lo], ones[0:1, :], dE[0:1, lo:hi], start=True, stop=True)
                pe.matmul(PSB[6][:, 0:hi - lo], ones[0:1, :], lastr[0:1, lo:hi], start=True, stop=True).then_inc(sem("cols_ps"), 1)
            pe.wait_ge(sem("cols_used"), len(chunks))

            def count(b, s, start=False, stop=False):
                pe.wait_ge(sem("oh49_ready"), b + 1)
                for m in range(3):
                    lo, hi = m * RK, min((m + 1) * RK, BT)
                    last = pe.matmul(PSB[5 + m][:, 0:(hi - lo) * NT], onesb, flat(oh49p[:, s, lo:hi, :]), start=start, stop=stop)
                last.then_inc(sem("counted"), 1)
            count(0, 0, start=True)
            count(1, 1)
            with pe.Fori(1, NB // 2 - 1) as i:
                for q in range(2):
                    count(2 * i + q, q)
            count(NB - 2, 0)
            count(NB - 1, 1, stop=True)

            def turn(b, s, t):
                pe.wait_ge(sem("oh_ready"), b * BT + t + 1)
                if t >= 2:
                    pe.wait_ge(sem("ohT_ready"), b * BT + t - 1)
                for k in range(2):
                    last = pe.transpose(PSB[t % 2][:, k * P:(k + 1) * P], OH[:, s, t, k * P:(k + 1) * P], ident)
                last.then_inc(sem("ohT_ps"), 1)

            def expand(b, t, regs):
                pe.wait_ge(sem("ohT_ready"), b * BT + t + 1)
                for k in range(2):
                    last = pe.matmul(ab_ps[:, t, :], ohT[:, t % 2, k * P:(k + 1) * P],
                                     flat(aT[:, bass.ds(regs[t] + k, 1), :]), start=(k == 0), stop=(k == 1))
                last.then_inc(sem("expanded"), 1)

            pe.wait_ge(sem("bins_ready"), 1)
            pe.wait_ge(sem("aT0"), 1)
            pe.wait_ge(sem("hx_used"), NCH)
            regs = bins(ENG.PE, 0, BT)
            for t in range(BT):
                turn(0, 0, t)
                expand(0, t, regs)
            with pe.Fori(0, NB // 2) as i:
                for q in range(2):
                    b, n = 2 * i + q, 2 * i + q + 1
                    pe.wait_ge(sem("isl_ready"), n)
                    pe.transpose(rT_ps, flat(isl4), ident).then_inc(sem("rT_ready"), 1)
                    pe.wait_ge(sem("rb_ready"), n)
                    pe.wait_ge(sem("v_ready"), n)
                    pe.transpose(vT_ps, flat(vE), ident).then_inc(sem("vT_ready"), 1)
                    HB = H * BT
                    pe.wait_ge(sem("bk_ready"), n)
                    pe.matmul(rows_ps[:, 0:HB], FT[:, P - 1:P], ident[0:HB, 0:HB], start=True, stop=True)
                    pe.matmul(rows_ps[:, HB:], BK[:, 0:1], ident[0:HB, 0:HB], start=True, stop=True).then_inc(sem("rows_ready"), 1)
                    pe.transpose(flat(BE_ps), BK, ident[0:HB, 0:HB])
                    pe.wait_ge(sem("cin_ready"), n)
                    pe.matmul(flat(bc_ps), ones[0:1, :], flat(cin), start=True, stop=True).then_inc(sem("bc_ready"), 1)
                    regs = bins(ENG.PE, b + 1, BT)
                    pe.wait_ge(sem("g_ready"), n)
                    pe.matmul(fac_ps, OH[0:1, q, 0, 0:P], ru[:, 2, :], start=True, stop=True).then_inc(sem("fac_ps"), 1)
                    for t in range(BT):
                        turn(b + 1, 1 - q, t)
                        pe.wait_ge(sem("msg_ready"), 2 * b + (1 if t < BT // 2 else 2))
                        if t >= 2:
                            pe.wait_ge(sem("acc_done"), b * (BT + 1) + t + 1)
                        for k in range(2):
                            last = pe.matmul(PSB[3 + t % 2][:, k * H * MW:(k + 1) * H * MW], OH[:, q, t, k * P:(k + 1) * P],
                                             flat(msg[:, t, :, :]), start=True, stop=True)
                        last.then_inc(sem("agg_ready"), 1)
                        expand(b + 1, t, regs)

            for c in range(NCH):
                pe.wait_ge(sem("h2_ready"), c + 1)
                for j in range(NC):
                    last = pe.transpose(PSB[j // 4][:, (j % 4) * P:(j % 4 + 1) * P], h2[:, j, :], ident)
                last.then_inc(sem("h2T_ps"), 1)
                pe.wait_ge(sem("h2T_ready"), c + 1)
                for j in range(NC):
                    n = c * NC + j
                    if n >= 6:
                        pe.wait_ge(sem("res_ready"), n - 5)
                    pe.matmul(PSB[2 + n % 6][:], h2T[:, j, :], flat(w1n), start=True, stop=False)
                    pe.matmul(PSB[2 + n % 6][:, 0:HID], ones[0:1, :], b1r, start=False, stop=True).then_inc(sem("pq_ps"), 1)

            def targets(i, q, first=False, final=False):
                b, n = 2 * i + q, 2 * i + q + 1
                B = b * BT
                regs = bins(ENG.PE, b, BT)

                def turn(t):
                    pe.wait_ge(sem("ohb_ready"), B + t + 1)
                    for k in range(2):
                        last = pe.transpose(PSB[t % 2][:].bitcast(BF16)[:, k * P:(k + 1) * P],
                                            OHb[:, (t + 2 * q) % 4, k * P:(k + 1) * P], identb)
                    last.then_inc(sem("bT_ps"), 1)

                def turn_ea(j):
                    if not (first and q == 0 and j == 0):
                        pe.wait_ge(sem("ea_out"), b * (BT // 2) + j)
                    pe.transpose(PSB[4][:, 0:P], flat(EAb[:, q, 2 * j:2 * j + 2, :]), ident).then_inc(sem("eaT_ps"), 1)

                def main(t):
                    g = B + t
                    pe.wait_ge(sem("bT_ready"), g + 1)
                    if not (first and q == 0 and t < 2):
                        pe.wait_ge(sem("r_out"), g - 1)
                    o = PSB[2 + t % 2][:, 0:HID]
                    for k in range(2):
                        for part in range(3):
                            pe.matmul(o, ohTb[:, t % 2, k * P:(k + 1) * P],
                                      flat(Qt[:, bass.ds(regs[t] + k, 1), part, :]), start=(k == 0 and part == 0), stop=False)
                    pe.wait_ge(sem("ea_out"), b * (BT // 2) + t // 2 + 1)
                    h = (t % 2) * DE
                    pe.matmul(o, EAT[h:h + DE, (t // 2 + q) % 2, :], w1e[h:h + DE, :], start=False, stop=True).then_inc(sem("main_done"), 1)

                def rank(m):
                    lo, hi = m * RK, min((m + 1) * RK, BT)
                    if m == 2:
                        pe.wait_ge(sem("rk_used"), 3 * b + 1)
                    elif m == 0 and not (first and q == 0):
                        pe.wait_ge(sem("rk_used"), 3 * b)
                    o = PSB[5 + m % 2]
                    pe.matmul(o[:, 0:(hi - lo) * NT], tri, flat(oh49[:, q, lo:hi, :]), start=True, stop=False)
                    for t in range(lo, hi):
                        last = pe.matmul(o[:, (t - lo) * NT:(t - lo + 1) * NT], tri27[:, t:t + 1].to_broadcast([BT + 1, P]),
                                         cnt27[:, 1 - q, :], start=False, stop=(t == hi - 1))
                    last.then_inc(sem("rk_ps"), 1)

                pe.wait_ge(sem("b49_ready"), n)
                c27 = PSB[7][0:BT + 1, 0:NT]
                for t in range(BT):
                    pe.matmul(c27, band[:, BT - t:2 * BT + 1 - t], oh49[:, q, t, :], start=(t == 0), stop=False)
                pe.matmul(c27, col27, cnt27[:, q, :], start=False, stop=True).then_inc(sem("c27_ps"), 1)
                if q == 0:
                    pe.wait_ge(sem("ea_in0"), 16 * (i + 1))
                elif final:
                    pe.wait_ge(sem("ea_last"), 32)
                else:
                    pe.wait_ge(sem("ea_in1"), 16 * (i + 1))
                turn(0)
                turn_ea(0)
                for t in range(BT):
                    if t < BT - 1:
                        turn(t + 1)
                    if t % 2 == 1 and t < BT - 1:
                        turn_ea((t + 1) // 2)
                    main(t)
                    if t == 1:
                        pe.wait_ge(sem("c27_ready"), n)
                    if t in (1, 4, 14):
                        rank({1: 0, 4: 1, 14: 2}[t])
            pe.wait_ge(sem("split_done"), NCH)
            pe.wait_ge(sem("c27_init"), 1)
            targets(0, 0, True)
            targets(0, 1, True)
            with pe.Fori(1, NB // 2 - 1) as i:
                for q in range(2):
                    targets(i, q)
            for q in range(2):
                targets(NB // 2 - 1, q, final=True)

            def turnp(g, m):
                pe.wait_ge(sem("ohp_ready"), g + 1)
                for j in range(PR):
                    last = pe.transpose(PSB[m % 2][:, j * P:(j + 1) * P], OHp[:, m % 4, j, :], ident)
                last.then_inc(sem("pT_ps"), 1)

            def source_rows(g, m, reg, first):
                pe.wait_ge(sem("pT_ready"), g + 1)
                if not (first and m < 2):
                    pe.wait_ge(sem("hp_ready"), g - 1)
                for j in range(PR):
                    for part in range(3):
                        last = pe.matmul(PSB[2 + m % 2][:, j * HID:(j + 1) * HID], ohTp[:, m % 2, j, :],
                                         flat(Pt[:, bass.ds(reg, 1), part, :]), start=(part == 0), stop=(part == 2))
                last.then_inc(sem("pp_ps"), 1)

            def segment(g, m, first):
                pe.wait_ge(sem("hid_ready"), g + 1)
                if not (first and m < 2):
                    pe.wait_ge(sem("accB_done"), g)
                for j in range(PR):
                    last = pe.matmul(PSB[4 + m % 2][:, 0:XW], OHp[:, m % 4, j, :], hid[:, m % 2, j, :], start=(j == 0), stop=(j == PR - 1))
                last.then_inc(sem("seg_ps"), 1)

            def sources(i, first=False):
                regs = pair_bins(ENG.PE, i)
                for m in range(SB):
                    turnp(SB * i + m, m)
                    if not (first and m < 1):
                        source_rows(SB * i + m - 1, (m - 1) % SB, regs[m + 1], first)
                    if not (first and m < 2):
                        segment(SB * i + m - 2, (m - 2) % SB, first)
            pe.wait_ge(sem("pt_in"), 16)
            pe.wait_ge(sem("pb_in"), 16)
            sources(0, True)
            with pe.Fori(1, NTURN) as i:
                sources(i)
            regs = pair_bins(ENG.PE, NTURN)
            source_rows(NPAIR - 1, SB - 1, regs[1], False)
            segment(NPAIR - 2, SB - 2, False)
            segment(NPAIR - 1, SB - 1, False)
            for c in range(NCH):
                pe.wait_ge(sem("stg_ready"), c + 1)
                if c:
                    pe.wait_ge(sem("sT_ready"), c)
                for j in range(NC):
                    for k in range(2):
                        last = pe.transpose(PSB[j // 2][:, (j % 2) * HID + k * P:(j % 2) * HID + (k + 1) * P], stg[:, j, k * P:(k + 1) * P], ident)
                last.then_inc(sem("sT_ps"), 1)
                pe.wait_ge(sem("sT_ready"), c + 1)
                if c:
                    pe.wait_ge(sem("fo_ready"), c)
                for j in range(NC):
                    for k in range(2):
                        last = pe.matmul(PSB[4 + j // 4][:, (j % 4) * D:(j % 4 + 1) * D], sT[:, j, k * P:(k + 1) * P], w2_sb[:, k, :],
                                         start=(k == 0), stop=(k == 1))
                last.then_inc(sem("fo_ps"), 1)


_INS = ['x', 'src', 'dst', 'edge_attr_64', 'L0_gnn_W', 'L0_gnn_att_src', 'L0_gnn_att_dst', 'L0_gnn_bias',
        'L1_gnn_W1', 'L1_gnn_b1', 'L1_gnn_W2', 'L1_gnn_b2']


def kernel(**inputs):
    import numpy as _np
    import concourse.bacc as _bacc
    from concourse.bass_utils import run_bass_kernel_spmd as _run

    nc = _bacc.Bacc("TRN2", target_bir_lowering=False, num_devices=1)
    arrays, args = {}, []
    for name in _INS:
        a = _np.ascontiguousarray(inputs[name])
        arrays[f"in_{name}"] = a
        args.append(nc.dram_tensor(f"in_{name}", a.shape, mybir.dt.from_np(a.dtype), kind="ExternalInput").ap())
    args.append(nc.dram_tensor("out_0", (N, D), F32, kind="ExternalOutput").ap())
    gnn(nc, *args)
    r = _run(nc, [arrays], core_ids=[0])
    return r.results[0]["out_0"]
```

```python
import concourse.bass as bass
from concourse import mybir
from contextlib import ExitStack

F32 = mybir.dt.float32
BF16 = mybir.dt.bfloat16
I32 = mybir.dt.int32
ALU = mybir.AluOpType
ACT = mybir.ActivationFunctionType
AX = mybir.AxisListType
ENG = mybir.EngineType

P = 128
N = 6250
D = 128
E = 206250
DE = 64
HID = 256
H = 4
DH = D // H
NT = -(-N // P)
NLAST = N - (NT - 1) * P
NPAD = NT * P
T = -(-E // P)
ELAST = E - (T - 1) * P
BT = 26
NB = T // BT
TG = 124
NG = T // TG
TP = T + BT
RB = 28
GW = D + H
XC = D + 2 * H
MW = DH + 2
BIG = 1e30
EPS = 1e-5
SLOPE = 0.2
NC = 7
NCH = NT // NC
PR = 2
GR = PR * P
CP = 2
NS = 4
SB = CP * NS
NPAIR = -(-((E + NT * (GR - 1)) // GR) // SB) * SB
NTURN = NPAIR // SB
XROWS = NPAIR * GR
FILLR = 4 * P
NFILL = -(-(XROWS - E) // FILLR)
XW = HID + 1
PBJ = -(-NPAIR // P)
CK = 512
RK = CK // NT
assert NB * BT == T and NG * TG == T and NCH * NC == NT and NB % 2 == 0


def dims(n):
    return " ".join("abcd"[:n])


def gnn(nc, x, src, dst, ea, W, asrc, adst, bias, W1, b1, W2, b2, out):
    h_tab = nc.dram_tensor("h_tab", (NPAD, GW), F32).ap()
    x_tab = nc.dram_tensor("x_tab", (NPAD, D), F32).ap()
    x1_tab = nc.dram_tensor("x1_tab", (NPAD, D), F32).ap()
    p_tab = nc.dram_tensor("p_tab", (P, NT * 3 * HID), BF16).ap()
    xr = nc.dram_tensor("xr", (XROWS + GR, XW), F32).ap()
    pb_tab = nc.dram_tensor("pb_tab", (P * PBJ,), I32).ap()

    ctx = ExitStack()
    sems = {}
    with ctx:
        WORDS = 53120
        arena = ctx.enter_context(nc.sbuf_tensor("arena", [P, WORDS], F32))
        PSB = [ctx.enter_context(nc.psum_tensor(f"bank{i}", [P, CK], F32)) for i in range(8)]

        def sem(name):
            if name not in sems:
                sems[name] = ctx.enter_context(nc.semaphore(name))
            return sems[name]

        class Region:
            def __init__(self, start, end=WORDS):
                self.at, self.end = start, end

            def __call__(self, shape, dt=F32, parts=P):
                n = 1
                for s in shape:
                    n *= s
                words = -(-n // 2) if dt == BF16 else n
                words = -(-words // 8) * 8
                v = arena[0:parts, self.at:self.at + words]
                if dt != F32:
                    v = v.bitcast(dt)
                v = v[:, 0:n]
                if len(shape) > 1:
                    d = dims(len(shape))
                    v = v.rearrange(f"p ({d}) -> p {d}", **dict(zip(d.split(), shape)))
                self.at += words
                assert self.at <= self.end, (self.at, self.end)
                return v

        K = Region(0)
        ident, ones, iota = K([P]), K([P]), K([2 * P])
        identb, onesb, iota49, iotab = K([P], BF16), K([P], BF16), K([NT], BF16), K([2 * P], BF16)
        srcE, dBE = K([TP]), K([TP])
        hiE, lastE = K([TP], BF16), K([TP], BF16)
        bin_row = K([(NB + 1) * RB], I32, 1)
        run0, rend, eps = K([NT]), K([NT], I32, 1), K([1])
        mean, rstd = K([NT]), K([NT])
        w1n, w1e, w2_sb = K([2, HID]), K([HID]), K([2, D])
        biasB, b2B, b1r = K([D]), K([D]), K([HID], F32, 1)
        tri, band = K([P], BF16), K([2 * BT + 1], BF16)
        tri27, col27, row26 = K([BT], F32, BT + 1), K([BT + 1], F32, BT + 1), K([1], F32, BT + 1)
        dump = K([1])
        X0 = K.at
        X = Region(X0)
        G, OHb = X([2, BT, GW]), X([2, BT, 2 * P], BF16)
        X([6500])
        Y0 = X.at
        Y = Region(Y0)
        acc = Y([NT + 1, H * MW])
        Y1 = Y.at
        aT, aT3 = Y([NT + 1, 2 * H]), Y([NT + 1, 3, 2 * H], BF16)
        s1E, s2E = Y([TP], BF16), Y([TP], BF16)
        thruF, thruB, contN = Y([TP], BF16, 1), Y([TP], BF16, 1), Y([TP], F32, 1)
        zfill = Y([FILLR // P, XW])
        Z0 = Y.at

        S = Region(X0, Y0)
        rI, rF = S([3, NG * P], I32, TG), S([3, NG * P], F32, TG)
        sq = Region(X0, Y0)([NT, D])
        xs = S([NT, D])
        hc, hcT, hx = S([NC, D]), S([NC, P]), S([NC, XC])
        w_sb, wx, att, attb, hm = S([P]), S([XC]), S([2]), S([2 * H]), S([H])
        S = Region(X0 + 3 * NG * P * 2)
        oh49p = S([2, BT, NT], BF16)
        c3, cnt, cnti = S([3, NT]), S([8, NT]), S([2, NT], I32)
        k256, pbc, pbf, pbi = S([PBJ]), S([PBJ, NT]), S([PBJ]), S([PBJ], I32)
        S = Region(Z0)
        isrc, dE, nE = S([TP], I32), S([TP]), S([TP])
        lastr, lflag, tmpr = S([TP], F32, 1), S([TP], F32, 1), S([TP])
        irow = isrc

        S = Region(Z0)
        aRes, ohT, OH, msg, idx = S([NT + 1, 2 * H]), S([2, 2 * P], BF16), S([4, 2 * P]), S([BT, H, MW]), S([2, BT], I32)
        abS, vE, isl4 = S([2, BT, 2 * H]), S([H, BT]), S([H, BT])
        rb, FT, BK = S([P + 1], F32, H * BT), S([P], F32, H * BT), S([P], F32, H * BT)
        resF, resB = S([H, BT + 1], F32, 1), S([H, BT], F32, 1)
        rowF, rowB = S([H, BT + 1], F32, 1), S([H, BT], F32, 1)
        CF, CB, cin = S([H, BT + 1], F32, 1), S([H, BT], F32, 1), S([2, H, BT], F32, 1)
        y12, ym, R = S([2, H, BT]), S([H, BT]), S([H, BT])
        ZZ, LL, DF, WT = S([3, H, BT]), S([3, H, BT]), S([2, H, BT]), S([2, H, BT])
        ru, fac = S([5, H], F32, 1), S([H])

        Qt = Region(X0, Y0)([NT + 1, 3, HID], BF16)
        S = Region(Y1)
        hs, xi, t1, x1c, sqm, h2, h2T = (S([NC, D]) for _ in range(7))
        den, rec, m7, v7 = S([NC, H]), S([NC, H]), S([NC]), S([NC])
        Pst, res = S([NC, 3, HID], BF16), S([2, 2, HID])

        S = Region(Y0)
        Rb, EAb, EAT = S([2, BT, XW]), S([2, BT, DE]), S([2, P])
        OHr, ohTb, oh49 = S([4, 2 * P], BF16), S([2, 2 * P], BF16), S([2, BT, NT], BF16)
        cnt27, t49, posf, padf, pos = S([2, NT], F32, BT + 1), S([BT, NT]), S([BT]), S([BT]), S([2, BT], I32)

        Pt = Region(X0, Y0)([NT, 3, HID], BF16)
        S = Region(Y0)
        accB, XR, OHp = S([NT, XW]), S([NS, CP, PR * XW]), S([SB, PR, P])
        ohTp, hp, hid = S([2, PR, P], BF16), S([2, PR, HID]), S([2, PR, XW])
        pbrow = S([NPAIR + 16], I32, 1)
        S = Region(X0, Y0)
        stg, sT, x1b, fo, fo2 = S([NC, HID]), S([NC, HID]), S([NC, D]), S([NC, D]), S([NC, D])

        ab_ps = [PSB[j][:, 0:BT // 2 * 3 * 2 * H].rearrange("p (t s c) -> p t s c", s=3, c=2 * H) for j in (2, 7)]
        vT_ps = PSB[5][0:H * BT, 0:P]
        rT_ps = PSB[5][0:H * BT, P:2 * P]
        BE_ps = PSB[6][:, 0:H * BT].rearrange("p (h t) -> p h t", h=H)
        fac_ps = PSB[6][:, 128:128 + H]
        rows_ps = PSB[5][0:1, 256:256 + 2 * H * BT]
        bc_ps = PSB[6][:, 256:256 + 2 * H * BT].rearrange("p (c h t) -> p c h t", c=2, h=H)

        def flat(v):
            d = dims(len(v.shape) - 1)
            return v.rearrange(f"p {d} -> p ({d})") if len(v.shape) > 2 else v

        chunks = [(c, min(c + CK, TP)) for c in range(0, TP, CK)]
        e0 = (NG - 1) * TG * P
        block = ctx.enter_context(nc.Block())

        def bins(engine, b, count):
            return nc.values_load_multi_w_load_instructions(
                bin_row[0:1, bass.ds(b * RB, count)], engines=[engine], min_val=0, max_val=NT - 1,
                skip_runtime_bounds_check_because="a node's tile, clamped at 0")[1]

        def pair_bins(engine, i):
            return nc.values_load_multi_w_load_instructions(
                pbrow[0:1, bass.ds(i * SB, SB + 4)], engines=[engine], min_val=0, max_val=NT - 1,
                skip_runtime_bounds_check_because="counted over the bins, held under their number")[1]

        @block.sync
        def _(sp):
            sp.dma_start(xs[:, 0:NT - 1, :], x[0:(NT - 1) * P, :].rearrange("(n p) f -> p n f", p=P)).then_inc(sem("x_in"), 16)
            sp.wait_ge(sem("xpad"), 1)
            sp.dma_start(xs[0:NLAST, NT - 1, :], x[(NT - 1) * P:N, :]).then_inc(sem("x_in"), 16)
            sp.wait_ge(sem("x_in"), 32)
            sp.dma_start(x_tab.rearrange("(n p) f -> p n f", p=P), xs).then_inc(sem("x_out"), 16)
            sp.wait_ge(sem("zf_ready"), 2)
            for f in range(NFILL):
                r0 = XROWS - (NFILL - f) * FILLR
                sp.dma_start(xr[r0:r0 + FILLR, :].rearrange("(p j) w -> p j w", p=P), zfill).then_inc(sem("filled"), 16)
            sp.wait_ge(sem("pbi_ready"), 1)
            sp.dma_start(pb_tab.rearrange("(p j) -> p j", p=P), pbi).then_inc(sem("pb_out"), 16)
            sp.wait_ge(sem("rend_ready"), 1)
            with sp.Fori(0, NT) as b:
                r = nc.values_load_multi_w_load_instructions(
                    rend[0:1, bass.ds(b, 1)], engines=[ENG.SP], min_val=0, max_val=XROWS,
                    skip_runtime_bounds_check_because="a sum of counts of edges, rounded up")[1][0]
                sp.wait_ge(sem("filled"), 16 * NFILL + 16 * b)
                sp.dma_start(xr[bass.ds(r, GR), :].rearrange("(p j) w -> p j w", p=P), zfill[:, 0:2, :]).then_inc(sem("filled"), 16)
            sp.wait_ge(sem("pb_out"), 16)
            sp.wait_ge(sem("x_out"), 16)
            sp.wait_ge(sem("filled"), 16 * (NFILL + NT))
            sp.wait_ge(sem("acc_done"), 1 + NB * (BT + 1))
            sp.wait_ge(sem("expanded"), NB * BT)
            for c in range(NCH):
                rows = lambda v: v[c * NC * P:(c + 1) * NC * P, :].rearrange("(n p) f -> p n f", p=P)
                if c:
                    sp.wait_ge(sem("x1_ready"), c)
                sp.dma_start(hs, rows(h_tab)[:, :, 0:D]).then_inc(sem("hs_in"), 16)
                sp.dma_start(xi, rows(x_tab)).then_inc(sem("hs_in"), 16)
                sp.wait_ge(sem("x1_ready"), c + 1)
                sp.dma_start(rows(x1_tab), x1c).then_inc(sem("x1_out"), 16)
                sp.wait_ge(sem("split_done"), c + 1)
                sp.dma_start(p_tab[:, c * NC * 3 * HID:(c + 1) * NC * 3 * HID], flat(Pst)).then_inc(sem("p_out"), 16)

            def load_ea(b, q, first=False):
                if not first:
                    sp.wait_ge(sem("eaT_ps"), (b - 1) * (BT // 2))
                sp.dma_start(EAb[:, q, :, :], ea[bass.ds(b * (BT * P), BT * P), :].rearrange("(t e) f -> e t f", e=P)).then_inc(sem(f"ea_in{q}"), 16)
            load_ea(0, 0, True)
            load_ea(1, 1, True)
            with sp.Fori(1, NB // 2 - 1) as i:
                for q in range(2):
                    load_ea(2 * i + q, q)
            load_ea(NB - 2, 0)
            sp.wait_ge(sem("eaT_ps"), (NB - 2) * (BT // 2))
            r0 = (NB - 1) * BT * P
            sp.dma_start(EAb[:, 1, 0:BT - 1, :], ea[r0:r0 + (BT - 1) * P, :].rearrange("(t e) f -> e t f", e=P)).then_inc(sem("ea_last"), 16)
            sp.dma_start(EAb[0:ELAST, 1, BT - 1, :], ea[r0 + (BT - 1) * P:E, :]).then_inc(sem("ea_last"), 16)

            sp.wait_ge(sem("main_done"), T)
            sp.dma_start(Pt.rearrange("p a b c -> p (a b c)"), p_tab, max_dma_last_dim=32768).then_inc(sem("pt_in"), 16)
            for q in range(2):
                sp.wait_ge(sem(f"scat{q}"), 16 * BT * (NB // 2))
            sp.wait_ge(sem("pbz"), 1)
            sp.dma_start(pbrow[:, 4:4 + NPAIR], pb_tab[0:NPAIR].rearrange("(a n) -> a n", a=1)).then_inc(sem("pb_in"), 16)

            def load_xr(c, s, first=False):
                if not first:
                    sp.wait_ge(sem("hp_ready"), c * CP - (NS - 1) * CP)
                sp.dma_start(XR[:, s, :, :], xr[bass.ds(c * (CP * GR), CP * GR), :].rearrange("(k p j) w -> p k (j w)", p=P, j=PR)).then_inc(sem(f"xr_in{s}"), 16)
            for s in range(NS):
                load_xr(s, s, True)
            with sp.Fori(1, NTURN) as i:
                for s in range(NS):
                    load_xr(NS * i + s, s)
            sp.wait_ge(sem("accB_done"), NPAIR + 1)
            for c in range(NCH):
                if c:
                    sp.wait_ge(sem("fo_ready"), c)
                sp.dma_start(x1b, x1_tab[c * NC * P:(c + 1) * NC * P, :].rearrange("(n p) f -> p n f", p=P)).then_inc(sem("x1_in"), 16)
                sp.wait_ge(sem("fo_ready"), c + 1)
                full = NC if c < NCH - 1 else NC - 1
                o0 = c * NC * P
                sp.dma_start(out[o0:o0 + full * P, :].rearrange("(n p) f -> p n f", p=P), fo2[:, 0:full, :]).then_inc(sem("stored"), 16)
                if full < NC:
                    sp.dma_start(out[o0 + full * P:N, :], fo2[0:NLAST, full, :]).then_inc(sem("stored"), 16)
            sp.wait_ge(sem("stored"), 16 * (NCH + 1))

        @block.gpsimd
        def _(pool):
            M = nc.gpsimd
            M.memset(rI[:, :, (NG - 1) * P:], -1).then_inc(sem("ipad"), 1)
            M.memset(xs[:, NT - 1, :], 0.0).then_inc(sem("xpad"), 1)
            M.memset(ident, 0.0).then_inc(sem("c0"), 1)
            pool.wait_ge(sem("c0"), 1)
            M.affine_select(out=ident, in_=ident, compare_op=ALU.not_equal, fill=1.0, base=0,
                            pattern=[[-1, P]], channel_multiplier=1).then_inc(sem("c0"), 1)
            M.iota(iota, pattern=[[1, 2 * P]], base=0, channel_multiplier=0,
                   allow_small_or_imprecise_dtypes=True).then_inc(sem("c0"), 1)
            M.iota(iotab, pattern=[[1, 2 * P]], base=0, channel_multiplier=0,
                   allow_small_or_imprecise_dtypes=True).then_inc(sem("c0"), 1)
            M.iota(iota49, pattern=[[1, NT]], base=0, channel_multiplier=0,
                   allow_small_or_imprecise_dtypes=True).then_inc(sem("c0"), 1)
            M.memset(ones, 1.0).then_inc(sem("c0"), 1)
            M.memset(onesb, 1.0).then_inc(sem("c0"), 1)
            M.memset(eps, EPS).then_inc(sem("c0"), 1)
            pool.wait_ge(sem("c0"), 8)
            M.tensor_copy(identb, ident).then_inc(sem("c0"), 1)
            M.memset(zfill, 0.0).then_inc(sem("zf_ready"), 1)
            pool.wait_ge(sem("zf_ready"), 1)
            M.memset(zfill[:, :, HID:XW], -1.0).then_inc(sem("zf_ready"), 1)
            M.memset(aT[:, NT, :], 0.0).then_inc(sem("aT0"), 1)
            M.memset(acc, 0.0).then_inc(sem("acc_done"), 1)
            for m in (tri, tri27):
                M.memset(m, 1.0).then_inc(sem("c1"), 1)
            for m in (band, col27, row26):
                M.memset(m, 0.0).then_inc(sem("c1"), 1)
            pool.wait_ge(sem("c1"), 5)
            M.affine_select(out=tri, in_=tri, compare_op=ALU.is_gt, fill=0.0, base=0, pattern=[[1, P]], channel_multiplier=-1).then_inc(sem("c1"), 1)
            M.affine_select(out=tri27, in_=tri27, compare_op=ALU.is_gt, fill=0.0, base=0, pattern=[[1, BT]], channel_multiplier=-1).then_inc(sem("c1"), 1)
            M.affine_select(out=row26, in_=row26, compare_op=ALU.not_equal, fill=1.0, base=-BT, pattern=[[0, 1]], channel_multiplier=1).then_inc(sem("c1"), 1)
            M.memset(band[:, BT:BT + 1], 1.0).then_inc(sem("c1"), 1)
            M.memset(col27[:, BT:BT + 1], 1.0).then_inc(sem("c1"), 1)
            M.iota(dump, pattern=[[0, 1]], base=XROWS, channel_multiplier=1, allow_small_or_imprecise_dtypes=True).then_inc(sem("c1"), 1)
            pool.wait_ge(sem("c1"), 11)
            M.affine_select(out=tri27, in_=tri27, compare_op=ALU.not_equal, fill=1.0, base=-BT, pattern=[[0, BT]], channel_multiplier=1).then_inc(sem("c1"), 1)
            pool.wait_ge(sem("hx_used"), NCH)
            M.iota(k256, pattern=[[GR, PBJ]], base=0, channel_multiplier=GR * PBJ,
                   allow_small_or_imprecise_dtypes=True).then_inc(sem("k256_ready"), 1)
            pool.wait_ge(sem("h_out"), 16 * NCH)

            def gather(i, q, first=False):
                pool.wait_ge(sem("idx_ready"), 2 * i + q + 1)
                for h in range(2):
                    if not first:
                        pool.wait_ge(sem("msg_ready"), 2 * (2 * i + q - 2) + h + 1)
                    pool.nop(nofuse=True)
                    for t in range(h * (BT // 2), (h + 1) * (BT // 2)):
                        pool.indirect_dma_start(G[:, q, t, :], None, h_tab,
                                                bass.IndirectOffsetOnAxis(ap=idx[:, q, t:t + 1], axis=0)
                                                ).then_inc(sem(f"gath{q}"), 16)
            gather(0, 0, True)
            gather(0, 1, True)
            with pool.Fori(1, NB // 2) as i:
                for q in range(2):
                    gather(i, q)

            pool.wait_ge(sem("filled"), 16 * (NFILL + NT))
            with pool.Fori(0, NB // 2) as i:
                for q in range(2):
                    n = 2 * i + q + 1
                    pool.wait_ge(sem("pos_ready"), n)
                    pool.wait_ge(sem("r_out"), n * BT)
                    pool.nop(nofuse=True)
                    for t in range(BT):
                        pool.indirect_dma_start(xr, bass.IndirectOffsetOnAxis(ap=pos[:, q, t:t + 1], axis=0),
                                                Rb[:, q, t, :], None).then_inc(sem(f"scat{q}"), 16)

        @block.scalar
        def _(act):
            A = nc.scalar
            act.wait_ge(sem("ipad"), 1)
            for a, (v, off) in enumerate(((src, 0), (dst, 0), (dst, 1))):
                act.dma_start(rI[:, a, 0:(NG - 1) * P].rearrange("p (g e) -> p g e", e=P),
                              v[off:off + e0].rearrange("(g p e) -> p g e", p=TG, e=P)).then_inc(sem("e_in"), 16)
                act.dma_start(rI[0:TG - 1, a, (NG - 1) * P:],
                              v[off + e0:off + e0 + (TG - 1) * P].rearrange("(p e) -> p e", e=P)).then_inc(sem("e_in"), 16)
                act.dma_start(rI[TG - 1:TG, a, (NG - 1) * P:(NG - 1) * P + ELAST - off],
                              v[off + e0 + (TG - 1) * P:E].rearrange("(p e) -> p e", p=1)).then_inc(sem("e_in"), 16)
            act.dma_start(w_sb, W).then_inc(sem("w_in"), 16)
            act.dma_start(att[:, 0:1], asrc.rearrange("a h o -> (h o) a")).then_inc(sem("w_in"), 16)
            act.dma_start(att[:, 1:2], adst.rearrange("a h o -> (h o) a")).then_inc(sem("w_in"), 16)
            act.dma_start(w1n[:, 0, :], W1[0:D, :]).then_inc(sem("w1_in"), 16)
            act.dma_start(w1n[:, 1, :], W1[D:2 * D, :]).then_inc(sem("w1_in"), 16)
            act.dma_start(w1e[0:DE, :], W1[2 * D:, :]).then_inc(sem("w1_in"), 16)
            act.dma_start(w1e[DE:P, :], W1[2 * D:, :]).then_inc(sem("w1_in"), 16)
            act.dma_start(w2_sb, W2.rearrange("(k p) f -> p k f", p=P)).then_inc(sem("w1_in"), 16)
            act.dma_start(biasB, bias.partition_broadcast(P)).then_inc(sem("w1_in"), 16)
            act.dma_start(b2B, b2.partition_broadcast(P)).then_inc(sem("w1_in"), 16)
            act.dma_start(b1r, b1.rearrange("(a n) -> a n", a=1)).then_inc(sem("w1_in"), 16)
            act.wait_ge(sem("xc_ready"), 1)
            act.wait_ge(sem("eT_used"), NG)
            A.activation(sq, xs, ACT.Square).then_inc(sem("sq_ready"), 1)
            act.wait_ge(sem("var_ready"), 1)
            act.wait_ge(sem("c0"), 9)
            A.activation(rstd, mean, ACT.Sqrt, bias=eps, scale=1.0 / D).then_inc(sem("std_ready"), 1)

            def chunk(c, first=False):
                act.wait_ge(sem("hT_ps"), c + 1)
                A.activation(flat(hcT[:, 0:4, :]), PSB[0][:], ACT.Copy)
                A.activation(flat(hcT[:, 4:NC, :]), PSB[1][:, 0:(NC - 4) * P], ACT.Copy).then_inc(sem("hcT_ready"), 1)
                act.wait_ge(sem("hx_ready"), c + 1)
                A.activation(aT[:, bass.ds(c * NC, NC), :], hx[:, :, D:], ACT.Copy).then_inc(sem("hx_used"), 1)
                act.dma_start(h_tab[bass.ds(c * (NC * P), NC * P), :].rearrange("(n p) f -> p n f", p=P),
                              hx[:, :, 0:GW]).then_inc(sem("h_out"), 16)
            with act.Fori(0, NCH) as c:
                chunk(c)

            def turn_out(b, t, first=False):
                act.wait_ge(sem("ohT_ps"), b * BT + t + 1)
                if not (first and t < 2):
                    act.wait_ge(sem("expanded"), b * BT + t - 1)
                A.activation(ohT[:, t % 2, :], PSB[t % 2][:].bitcast(BF16)[:, 0:2 * P], ACT.Copy).then_inc(sem("ohT_ready"), 1)

            def widen(b, q, t, first=False):
                if not (first and t < 4):
                    act.wait_ge(sem("agg_ready"), b * BT + t - 3)
                act.wait_ge(sem("oh_ready"), b * BT + t + 1)
                A.activation(OH[:, (t + 2 * q) % 4, :], OHb[:, q, t, :], ACT.Copy).then_inc(sem("wide_ready"), 1)

            def chain_isl(b):
                A.activation(isl4, lastE[:, bass.ds(b * BT, BT)].unsqueeze(1).to_broadcast([P, H, BT]),
                             ACT.Copy, scale=-BIG).then_inc(sem("isl_ready"), 1)

            def chain_rb(b):
                act.wait_ge(sem("rT_ready"), b + 1)
                A.activation(rb[:, 1:P + 1], rT_ps, ACT.Copy).then_inc(sem("rb_ready"), 1)

            def chain_exp(b, first=False):
                act.wait_ge(sem("df_ready"), b + 1)
                if not first:
                    act.wait_ge(sem("msg_ready"), 2 * b)
                A.activation(WT, DF, ACT.Exp).then_inc(sem("wt_ready"), 1)
                act.wait_ge(sem("ru_ready"), b + 1)
                A.activation(ru[:, 4, :], ru[:, 3, :], ACT.Exp).then_inc(sem("f_ready"), 1)

            act.wait_ge(sem("rb_init"), 1)
            for t in range(BT):
                turn_out(0, t, True)
            chain_isl(0)
            chain_rb(0)
            for t in range(BT):
                turn_out(1, t)
            chain_exp(0, True)

            def batch(b, q, ahead2=True, ahead1=True, first=False):
                widen(b, q, 0, first)
                for t in range(BT):
                    if t < BT - 1:
                        widen(b, q, t + 1, first)
                    if ahead2:
                        turn_out(b + 2, t)
                    if ahead1 and t == 1:
                        act.wait_ge(sem("vT_ready"), b + 1)
                        chain_isl(b + 1)
                    if ahead1 and t == 3:
                        chain_rb(b + 1)
                    if ahead1 and t == 22:
                        chain_exp(b + 1)
            batch(0, 0, first=True)
            batch(1, 1)
            with act.Fori(1, NB // 2 - 1) as i:
                for q in range(2):
                    batch(2 * i + q, q)
            batch(NB - 2, 0, ahead2=False)
            batch(NB - 1, 1, ahead2=False, ahead1=False)

            for c in range(NCH):
                act.wait_ge(sem("t_cent"), c + 1)
                A.activation(sqm, t1, ACT.Square).then_inc(sem("sqm_ready"), 1)
                act.wait_ge(sem("v_sum"), c + 1)
                A.activation(m7, v7, ACT.Sqrt, bias=eps, scale=1.0 / D).then_inc(sem("s_ready"), 1)
                act.wait_ge(sem("h2T_ps"), c + 1)
                A.activation(flat(h2T[:, 0:4, :]), PSB[0][:], ACT.Copy)
                A.activation(flat(h2T[:, 4:NC, :]), PSB[1][:, 0:(NC - 4) * P], ACT.Copy).then_inc(sem("h2T_ready"), 1)
                if c:
                    act.wait_ge(sem("p_out"), 16 * c)
                for j in range(NC):
                    n, pq = c * NC + j, PSB[2 + (c * NC + j) % 6]
                    act.wait_ge(sem("pq_ps"), n + 1)
                    A.activation(Pst[:, j, 0, :], pq[:, 0:HID], ACT.Copy)
                    A.activation(Qt[:, n, 0, :], pq[:, HID:], ACT.Copy).then_inc(sem("hi_ready"), 1)
                    act.wait_ge(sem("res_ready"), n + 1)
                    A.activation(Pst[:, j, 1, :], res[:, n % 2, 0, :], ACT.Copy)
                    A.activation(Qt[:, n, 1, :], res[:, n % 2, 1, :], ACT.Copy).then_inc(sem("mid_ready"), 1)

            def turn_outb(b, t, first):
                g = b * BT + t
                act.wait_ge(sem("bT_ps"), g + 1)
                if not (first and t < 2):
                    act.wait_ge(sem("main_done"), g - 1)
                A.activation(ohTb[:, t % 2, :], PSB[t % 2][:].bitcast(BF16)[:, 0:2 * P], ACT.Copy).then_inc(sem("bT_ready"), 1)

            def rows_out(b, q, t):
                act.wait_ge(sem("main_done"), b * BT + t + 1)
                A.activation(Rb[:, q, t, 0:HID], PSB[2 + t % 2][:, 0:HID], ACT.Copy).then_inc(sem("r_out"), 1)

            def targets(i, q, first=False):
                b = 2 * i + q
                turn_outb(b, 0, first and q == 0)
                if not first:
                    act.wait_ge(sem(f"scat{q}"), 16 * BT * i)
                act.wait_ge(sem("c27_ps"), b + 1)
                A.activation(cnt27[:, 1 - q, :], PSB[7][0:BT + 1, 0:NT], ACT.Copy).then_inc(sem("c27_ready"), 1)
                for t in range(BT):
                    if t < BT - 1:
                        turn_outb(b, t + 1, first and q == 0)
                    rows_out(b, q, t)
            targets(0, 0, True)
            targets(0, 1, True)
            with act.Fori(1, NB // 2) as i:
                for q in range(2):
                    targets(i, q)

            def turn_outp(g, m, first):
                act.wait_ge(sem("pT_ps"), g + 1)
                if not (first and m < 2):
                    act.wait_ge(sem("pp_ps"), g - 1)
                A.activation(flat(ohTp[:, m % 2, :, :]), PSB[m % 2][:, 0:PR * P], ACT.Copy).then_inc(sem("pT_ready"), 1)

            def relu(g, m, first):
                act.wait_ge(sem("hp_ready"), g + 1)
                if not (first and m < 2):
                    act.wait_ge(sem("seg_ps"), g - 1)
                A.activation(hid[:, m % 2, :, 0:HID], hp[:, m % 2, :, :], ACT.Relu).then_inc(sem("hid_ready"), 1)

            def sources(i, first=False):
                for m in range(SB):
                    turn_outp(SB * i + m, m, first)
                    if not (first and m < 2):
                        relu(SB * i + m - 2, (m - 2) % SB, first)
            sources(0, True)
            with act.Fori(1, NTURN) as i:
                sources(i)
            relu(NPAIR - 2, SB - 2, False)
            relu(NPAIR - 1, SB - 1, False)
            for c in range(NCH):
                if c:
                    act.wait_ge(sem("sT_ps"), c)
                else:
                    act.wait_ge(sem("accB_done"), NPAIR + 1)
                A.activation(stg, accB[:, c * NC:(c + 1) * NC, 0:HID], ACT.Copy).then_inc(sem("stg_ready"), 1)
                act.wait_ge(sem("sT_ps"), c + 1)
                if c:
                    act.wait_ge(sem("fo_ps"), c)
                for m in range(4):
                    n = min(2, NC - 2 * m)
                    last = A.activation(flat(sT[:, 2 * m:2 * m + n, :]), PSB[m][:, 0:n * HID], ACT.Copy)
                last.then_inc(sem("sT_ready"), 1)

        @block.vector
        def _(dve):
            V = nc.vector
            k = [0]

            def link(ins):
                k[0] += 1
                ins.then_inc(sem("dve_prep"), 1)
                dve.wait_ge(sem("dve_prep"), k[0])

            link(V.memset(hm, 0.0))
            for h in range(H):
                V.memset(hm[h * DH:(h + 1) * DH, h:h + 1], 1.0)
            V.memset(srcE[:, T:], -1.0)
            V.memset(dE[:, T:], -1.0)
            V.memset(nE[:, T:], -1.0)
            dve.wait_ge(sem("e_in"), 16 * 9)
            V.tensor_copy(rF, rI).then_inc(sem("rF_ready"), 1)
            dve.wait_ge(sem("x_in"), 32)
            link(V.tensor_reduce(mean, xs, AX.X, ALU.add))
            link(V.tensor_scalar(rstd, mean, 1.0 / D, None, ALU.mult))
            dve.wait_ge(sem("x_out"), 16)
            V.tensor_tensor(xs, xs, rstd.unsqueeze(2).to_broadcast([P, NT, D]), ALU.subtract).then_inc(sem("xc_ready"), 1)
            for g in range(NG):
                dve.wait_ge(sem("eT_ps"), g + 1)
                v = PSB[2 + g % 2][:, 0:3 * TG].rearrange("p (a t) -> p a t", a=3)
                V.tensor_copy(srcE[:, g * TG:(g + 1) * TG], v[:, 0, :])
                V.tensor_copy(dE[:, g * TG:(g + 1) * TG], v[:, 1, :])
                V.tensor_copy(nE[:, g * TG:(g + 1) * TG], v[:, 2, :]).then_inc(sem("eT_used"), 1)
            dve.wait_ge(sem("sq_ready"), 1)
            V.tensor_reduce(mean, sq, AX.X, ALU.add).then_inc(sem("var_ready"), 1)
            dve.wait_ge(sem("w_in"), 48)
            dve.wait_ge(sem("c0"), 9)
            V.tensor_scalar(attb[:, 0:H], hm, att[:, 0:1], None, ALU.mult)
            V.tensor_scalar(attb[:, H:], hm, att[:, 1:2], None, ALU.mult).then_inc(sem("attb_ready"), 1)
            dve.wait_ge(sem("wx_ps"), 1)
            V.tensor_copy(wx, PSB[4][:, 0:XC]).then_inc(sem("wx_ready"), 1)
            dve.wait_ge(sem("std_ready"), 1)
            link(V.reciprocal(mean, rstd))

            def chunk(c, first=False):
                if not first:
                    dve.wait_ge(sem("hT_ps"), c)
                V.scalar_tensor_tensor(hc, xs[:, bass.ds(c * NC, NC), :], 0.0,
                                       mean[:, bass.ds(c * NC, NC)].unsqueeze(2).to_broadcast([P, NC, D]),
                                       ALU.max, ALU.mult).then_inc(sem("hc_ready"), 1)
                dve.wait_ge(sem("hx_ps"), c + 1)
                if not first:
                    dve.wait_ge(sem("hx_used"), c)
                    dve.wait_ge(sem("h_out"), 16 * c)
                V.tensor_copy(hx[:, 0:3, :], PSB[5][:, 0:3 * XC].rearrange("p (j f) -> p j f", j=3))
                V.tensor_copy(hx[:, 3:6, :], PSB[6][:, 0:3 * XC].rearrange("p (j f) -> p j f", j=3))
                V.tensor_copy(hx[:, 6, :], PSB[7][:, 0:XC]).then_inc(sem("hx_ready"), 1)
            chunk(0, True)
            with dve.Fori(1, NCH) as c:
                chunk(c)

            link(V.tensor_tensor(tmpr, nE, dE, ALU.not_equal))
            V.tensor_copy(lastE, tmpr).then_inc(sem("last_ready"), 1)
            link(V.tensor_copy(isrc, srcE))
            link(V.tensor_scalar(isrc, isrc, 7, None, ALU.arith_shift_right))
            link(V.tensor_copy(hiE, isrc))
            for j, (lo, hi) in enumerate(chunks):
                dve.wait_ge(sem("rows_ps"), 2 * j + 2)
                V.tensor_copy(lastr[:, lo:hi], PSB[2][0:1, 0:hi - lo])
                V.tensor_copy(lflag[:, lo:hi], PSB[3][0:1, 0:hi - lo]).then_inc(sem("rows_used"), 1)
            dve.wait_ge(sem("rows_used"), len(chunks))
            V.memset(contN[:, 0:1], -BIG)
            V.tensor_scalar(contN[:, 1:], lflag[:, 0:TP - 1], -BIG, None, ALU.mult).then_inc(sem("cont_ready"), 1)
            dve.wait_ge(sem("cont_ready"), 1)
            link(V.tensor_tensor(lflag, dE[0:1, :], lastr, ALU.not_equal))
            link(V.tensor_scalar(lflag, lflag, -BIG, None, ALU.mult))
            V.tensor_tensor(thruF, contN, lflag, ALU.min)
            V.tensor_tensor(thruB[:, 0:TP - 1], contN[:, 1:], lflag[:, 0:TP - 1], ALU.min)
            ir = irow[0:1, :]
            link(V.tensor_copy(ir, dE[0:1, :]))
            link(V.tensor_scalar(ir, ir, 7, None, ALU.arith_shift_right))
            link(V.tensor_scalar(ir, ir, 0, None, ALU.max))
            V.tensor_copy(bin_row.rearrange("p (b t) -> p b t", t=RB)[:, :, 0:BT],
                          ir.rearrange("p (b t) -> p b t", t=BT)).then_inc(sem("bins_ready"), 1)
            V.tensor_scalar(tmpr[0:1, :], ir, float(P), None, ALU.mult).then_inc(sem("binf_ready"), 1)
            for j, (lo, hi) in enumerate(chunks):
                dve.wait_ge(sem("cols_ps"), j + 1)
                V.tensor_tensor(dBE[:, lo:hi], dE[:, lo:hi], PSB[4][:, 0:hi - lo], ALU.subtract)
                V.tensor_tensor(s1E[:, lo:hi], dE[:, lo:hi], PSB[5][:, 0:hi - lo], ALU.not_equal)
                V.tensor_tensor(s2E[:, lo:hi], dE[:, lo:hi], PSB[6][:, 0:hi - lo], ALU.not_equal).then_inc(sem("cols_used"), 1)
            dve.wait_ge(sem("cols_used"), len(chunks))
            V.tensor_scalar(s1E, s1E, -BIG, None, ALU.mult)
            link(V.tensor_scalar(s2E, s2E, -BIG, None, ALU.mult))

            def hot49(b, s, first=False):
                if not first:
                    dve.wait_ge(sem("counted"), b - 1)
                V.tensor_tensor(oh49p[:, s, :, :], hiE[:, bass.ds(b * BT, BT)].unsqueeze(2).to_broadcast([P, BT, NT]),
                                iota49.unsqueeze(1).to_broadcast([P, BT, NT]), ALU.is_equal).then_inc(sem("oh49_ready"), 1)
            hot49(0, 0, True)
            hot49(1, 1, True)
            with dve.Fori(1, NB // 2) as i:
                for q in range(2):
                    hot49(2 * i + q, q)
            dve.wait_ge(sem("counted"), NB)
            for m, tiles in enumerate((RK, RK, BT - 2 * RK)):
                last = V.tensor_reduce(c3[:, m, :], PSB[5 + m][:, 0:tiles * NT].rearrange("p (t b) -> p b t", b=NT), AX.X, ALU.add)
            link(last)
            link(V.tensor_tensor(cnt[:, 0, :], c3[:, 0, :], c3[:, 1, :], ALU.add))
            link(V.tensor_tensor(cnt[:, 1, :], cnt[:, 0, :], c3[:, 2, :], ALU.add))
            link(V.tensor_scalar(cnt[:, 2, :], cnt[:, 1, :], float(GR - 1), None, ALU.add))
            link(V.tensor_copy(cnti[:, 0, :], cnt[:, 2, :]))
            link(V.tensor_scalar(cnti[:, 1, :], cnti[:, 0, :], 8, None, ALU.arith_shift_right))
            link(V.tensor_copy(cnt[:, 3, :], cnti[:, 1, :]))
            link(V.tensor_scalar(cnt[:, 4, :], cnt[:, 3, :], float(GR), None, ALU.mult))
            link(V.memset(cnt[:, 5, :], 1.0))
            link(V.tensor_tensor_scan(cnt[:, 6, :], cnt[:, 5, :], cnt[:, 4, :], 0.0, ALU.mult, ALU.add))
            link(V.tensor_tensor(run0, cnt[:, 6, :], cnt[:, 4, :], ALU.subtract))
            link(V.tensor_tensor(cnt[:, 7, :], run0, cnt[:, 1, :], ALU.add))
            V.tensor_copy(rend, cnt[0:1, 7, :]).then_inc(sem("rend_ready"), 1)
            dve.wait_ge(sem("k256_ready"), 1)
            link(V.tensor_tensor(pbc, cnt[:, 6, :].unsqueeze(1).to_broadcast([P, PBJ, NT]),
                                 k256.unsqueeze(2).to_broadcast([P, PBJ, NT]), ALU.is_le))
            link(V.tensor_reduce(pbf, pbc, AX.X, ALU.add))
            link(V.tensor_scalar(pbf, pbf, float(NT - 1), None, ALU.min))
            V.tensor_copy(pbi, pbf).then_inc(sem("pbi_ready"), 1)

            dve.wait_ge(sem("pb_out"), 16)
            V.memset(rb, -BIG).then_inc(sem("rb_init"), 1)
            V.memset(resF, -BIG)
            V.memset(resB, -BIG)
            V.memset(CF, -BIG)
            link(V.memset(cin, -BIG))
            dve.wait_ge(sem("hx_used"), NCH)
            dve.wait_ge(sem("aT0"), 1)
            link(V.tensor_copy(aT3[:, :, 0, :], aT))
            link(V.tensor_tensor(aRes, aT, aT3[:, :, 0, :], ALU.subtract))
            link(V.tensor_copy(aT3[:, :, 1, :], aRes))
            V.tensor_tensor(aT3[:, :, 2, :], aRes, aT3[:, :, 1, :], ALU.subtract).then_inc(sem("aT3_ready"), 1)

            def indices(b, s):
                V.tensor_scalar(idx[:, s, :], srcE[:, bass.ds(b * BT, BT)], 0.0, None, ALU.max).then_inc(sem("idx_ready"), 1)

            def hot(b, s, t, first=False):
                if not first:
                    dve.wait_ge(sem("wide_ready"), (b - 2) * BT + t + 1)
                V.tensor_scalar(OHb[:, s, t, :], iotab, dBE[:, bass.ds(b * BT + t, 1)], None, ALU.is_equal).then_inc(sem("oh_ready"), 1)

            def logits(b, q, half):
                dve.wait_ge(sem("expanded"), b * BT + (half + 1) * (BT // 2))
                V.tensor_reduce(abS[:, q, half * (BT // 2):(half + 1) * (BT // 2), :], ab_ps[half].rearrange("p t s c -> p t c s"),
                                AX.X, ALU.add).then_inc(sem("ab_out"), 1)

            def chain(b, q, step, i):
                n, B = b + 1, b * BT
                row = lambda v: v[:, bass.ds(B, BT)].unsqueeze(1).to_broadcast([1, H, BT])
                col = lambda v: v[:, bass.ds(B, BT)].unsqueeze(1).to_broadcast([P, H, BT])
                as4 = abS[:, q, :, 0:H].rearrange("p t h -> p h t")
                ad4 = abS[:, q, :, H:].rearrange("p t h -> p h t")
                if step == "resets":
                    V.tensor_copy(resF[:, :, 1:], row(thruF))
                    V.tensor_copy(resB[:, :, 0:BT - 1], thruB[:, bass.ds(B, BT - 1)].unsqueeze(1).to_broadcast([1, H, BT - 1]))
                    V.tensor_copy(rowF[:, :, 0:1], CF[:, :, BT:]).then_inc(sem("rres_ready"), 1)
                elif step == "logits":
                    g4 = G[:, q, :, D:GW].rearrange("p t h -> p h t")
                    dve.wait_ge(sem(f"gath{q}"), 16 * BT * (i + 1))
                    dve.wait_ge(sem("ab_out"), 2 * n)
                    V.tensor_tensor(vE, g4, as4, ALU.max).then_inc(sem("v_ready"), 1)
                    V.tensor_tensor(ZZ[:, 0, :, :], g4, ad4, ALU.add)
                    V.tensor_tensor(ZZ[:, 1, :, :], as4, ad4, ALU.add)
                elif step == "forward":
                    dve.wait_ge(sem("vT_ready"), n)
                    dve.wait_ge(sem("rb_ready"), n)
                    V.tensor_tensor_scan(FT, rb[:, 0:P], vT_ps, -BIG, ALU.add, ALU.max).then_inc(sem("ft_ready"), 1)
                elif step == "backward":
                    dve.wait_ge(sem("ft_ready"), n)
                    V.tensor_tensor_scan(BK[:, ::-1], rb[:, 1:P + 1][:, ::-1], FT[:, ::-1], -BIG, ALU.add, ALU.max).then_inc(sem("bk_ready"), 1)
                elif step == "ends":
                    dve.wait_ge(sem("rows_ready"), n)
                    dve.wait_ge(sem("rres_ready"), n)
                    V.tensor_copy(rowF[:, :, 1:], rows_ps[:, 0:H * BT].rearrange("p (h t) -> p h t", h=H))
                    V.tensor_copy(rowB, rows_ps[:, H * BT:].rearrange("p (h t) -> p h t", h=H)).then_inc(sem("row_ready"), 1)
                elif step == "carries":
                    dve.wait_ge(sem("row_ready"), n)
                    V.tensor_tensor_scan(flat(CF), flat(resF), flat(rowF), -BIG, ALU.add, ALU.max)
                    V.tensor_tensor_scan(flat(CB)[:, ::-1], flat(resB)[:, ::-1], flat(rowB)[:, ::-1], -BIG, ALU.add, ALU.max).then_inc(sem("carry_ready"), 1)
                elif step == "come in":
                    dve.wait_ge(sem("carry_ready"), n)
                    V.tensor_tensor(cin[:, 0, :, :], CF[:, :, 0:BT], row(contN), ALU.add)
                    V.tensor_tensor(cin[:, 1, :, 0:BT - 1], CB[:, :, 1:],
                                    contN[:, bass.ds(B + 1, BT - 1)].unsqueeze(1).to_broadcast([1, H, BT - 1]), ALU.add).then_inc(sem("cin_ready"), 1)
                elif step == "masked":
                    dve.wait_ge(sem("bc_ready"), n)
                    V.tensor_tensor(y12[:, 0, :, :], bc_ps[:, 0, :, :], col(s1E), ALU.add)
                    V.tensor_tensor(y12[:, 1, :, :], bc_ps[:, 1, :, :], col(s2E), ALU.add).then_inc(sem("y_ready"), 1)
                elif step == "carried":
                    dve.wait_ge(sem("y_ready"), n)
                    V.tensor_tensor(ym, y12[:, 0, :, :], y12[:, 1, :, :], ALU.max).then_inc(sem("ym_ready"), 1)
                elif step == "maximum":
                    dve.wait_ge(sem("ym_ready"), n)
                    V.tensor_tensor(R, ym, BE_ps, ALU.max).then_inc(sem("R_ready"), 1)
                elif step == "sums":
                    dve.wait_ge(sem("R_ready"), n)
                    V.tensor_tensor(ZZ[:, 2, :, :], R, ad4, ALU.add).then_inc(sem("Z_ready"), 1)
                    V.tensor_tensor(ru[:, 0, :], cin[:, 0, :, 0], abS[0:1, q, 0, H:], ALU.add).then_inc(sem("r_step"), 1)
                elif step == "leaky":
                    dve.wait_ge(sem("Z_ready"), n)
                    V.scalar_tensor_tensor(flat(LL), flat(ZZ), SLOPE, flat(ZZ), ALU.mult, ALU.max).then_inc(sem("L_ready"), 1)
                    dve.wait_ge(sem("r_step"), 4 * b + 1)
                    V.scalar_tensor_tensor(ru[:, 1, :], ru[:, 0, :], SLOPE, ru[:, 0, :], ALU.mult, ALU.max).then_inc(sem("r_step"), 1)
                elif step == "differences":
                    dve.wait_ge(sem("L_ready"), n)
                    V.tensor_tensor(DF, LL[:, 0:2, :, :], LL[:, 2, :, :].unsqueeze(1).to_broadcast([P, 2, H, BT]), ALU.subtract).then_inc(sem("df_ready"), 1)
                    dve.wait_ge(sem("r_step"), 4 * b + 2)
                    V.tensor_tensor(ru[:, 2, :], ru[:, 1, :], LL[0:1, 2, :, 0], ALU.subtract).then_inc(sem("r_step"), 1)
                elif step == "floor":
                    dve.wait_ge(sem("r_step"), 4 * b + 3)
                    V.tensor_scalar(ru[:, 3, :], ru[:, 2, :], -1e4, None, ALU.max).then_inc(sem("ru_ready"), 1)

            STEPS = {2: "resets", 7: "logits", 9: "forward", 10: "backward", 12: "ends", 13: "carries", 14: "come in", 16: "masked",
                     17: "carried", 18: "maximum", 19: "sums", 20: "leaky", 21: "differences", 22: "floor"}
            wt = WT.rearrange("p s h t -> p s t h")

            def messages(q, lo, hi):
                last = V.tensor_tensor(msg[:, lo:hi, :, 0:DH], G[:, q, lo:hi, 0:D].rearrange("p t (h o) -> p t h o", h=H),
                                       wt[:, 0, lo:hi, :].unsqueeze(3).to_broadcast([P, hi - lo, H, DH]), ALU.mult)
                last.then_inc(sem("msg_ready"), 1)

            def add_up(b, t, regs):
                dve.wait_ge(sem("agg_ready"), b * BT + t + 1)
                dve.wait_ge(sem("acc_done"), b * (BT + 1) + 2 + t)
                a = flat(acc[:, bass.ds(regs[t], 2), :])
                V.tensor_tensor(a, a, PSB[3 + t % 2][:, 0:2 * H * MW], ALU.add).then_inc(sem("acc_done"), 1)

            def batch(i, q, ahead2=True, ahead1=True):
                b, n = 2 * i + q, 2 * i + q + 1
                dve.wait_ge(sem("wt_ready"), n)
                V.tensor_copy(msg[:, :, :, DH], wt[:, 0, :, :])
                V.tensor_tensor(msg[:, :, :, DH + 1], wt[:, 1, :, :],
                                lastE[:, bass.ds(b * BT, BT)].unsqueeze(2).to_broadcast([P, BT, H]), ALU.mult)
                messages(q, 0, BT // 2)
                dve.wait_ge(sem("f_ready"), n)
                V.tensor_scalar(ru[:, 2, :], ru[:, 4, :], -1.0, None, ALU.add).then_inc(sem("g_ready"), 1)
                regs = bins(ENG.DVE, b, BT)
                if ahead1:
                    logits(b + 1, 1 - q, 1)
                dve.wait_ge(sem("fac_ps"), n)
                V.tensor_scalar(fac, fac_ps, 1.0, None, ALU.add).then_inc(sem("r_step"), 1)
                for t in range(BT):
                    if ahead2:
                        hot(b + 2, q, t)
                    if t == 0:
                        dve.wait_ge(sem("r_step"), 4 * b + 4)
                        dve.wait_ge(sem("acc_done"), b * (BT + 1) + 1)
                        a = acc[:, bass.ds(regs[0], 1), :].rearrange("p a (h m) -> p (a h) m", h=H)
                        V.tensor_tensor(a, a, fac.unsqueeze(2).to_broadcast([P, H, MW]), ALU.mult).then_inc(sem("acc_done"), 1)
                    if t >= 2:
                        add_up(b, t - 2, regs)
                    if t == 5:
                        messages(q, BT // 2, BT)
                        if ahead2:
                            dve.wait_ge(sem(f"gath{q}"), 16 * BT * (i + 1))
                            indices(b + 2, q)
                    if ahead1 and t in STEPS:
                        chain(b + 1, 1 - q, STEPS[t], i + q)
                    if ahead2 and t == 15:
                        logits(b + 2, q, 0)
                add_up(b, BT - 2, regs)
                add_up(b, BT - 1, regs)

            indices(0, 0)
            indices(1, 1)
            for t in range(BT):
                hot(0, 0, t, True)
            logits(0, 0, 0)
            logits(0, 0, 1)
            for t in range(BT):
                hot(1, 1, t, True)
            logits(1, 1, 0)
            for t in sorted(STEPS):
                chain(0, 0, STEPS[t], 0)
            batch(0, 0)
            batch(0, 1)
            with dve.Fori(1, NB // 2 - 1) as i:
                for q in range(2):
                    batch(i, q)
            batch(NB // 2 - 1, 0, ahead2=False)
            batch(NB // 2 - 1, 1, ahead2=False, ahead1=False)

            V.memset(Qt[:, NT, :, :], 0.0)
            dve.wait_ge(sem("w1_in"), 16 * 8)
            dve.wait_ge(sem("filled"), 16 * (NFILL + NT))
            for c in range(NCH):
                a = acc[:, c * NC:(c + 1) * NC, :].rearrange("p n (h m) -> p n h m", h=H)
                hv = lambda v: v.rearrange("p n (h o) -> p n h o", h=H)
                wide = lambda v: v.unsqueeze(3).to_broadcast([P, NC, H, DH])
                link(V.tensor_tensor(den, a[:, :, :, DH], a[:, :, :, DH + 1], ALU.add))
                link(V.tensor_scalar(den, den, 1e-30, None, ALU.max))
                V.reciprocal(rec, den)
                dve.wait_ge(sem("hs_in"), 32 * (c + 1))
                link(V.tensor_tensor(hv(t1), hv(hs), wide(a[:, :, :, DH + 1]), ALU.mult))
                link(V.tensor_tensor(hv(t1), hv(t1), a[:, :, :, 0:DH], ALU.add))
                link(V.tensor_tensor(hv(t1), hv(t1), wide(rec), ALU.mult))
                link(V.tensor_tensor(t1, t1, biasB.unsqueeze(1).to_broadcast([P, NC, D]), ALU.add))
                if c:
                    dve.wait_ge(sem("x1_out"), 16 * c)
                V.tensor_tensor(x1c, t1, xi, ALU.add).then_inc(sem("x1_ready"), 1)
                dve.wait_ge(sem("x1_ready"), c + 1)
                link(V.tensor_reduce(v7, x1c, AX.X, ALU.add))
                link(V.tensor_scalar(v7, v7, 1.0 / D, None, ALU.mult))
                V.tensor_tensor(t1, x1c, v7.unsqueeze(2).to_broadcast([P, NC, D]), ALU.subtract).then_inc(sem("t_cent"), 1)
                dve.wait_ge(sem("sqm_ready"), c + 1)
                V.tensor_reduce(v7, sqm, AX.X, ALU.add).then_inc(sem("v_sum"), 1)
                dve.wait_ge(sem("s_ready"), c + 1)
                link(V.reciprocal(v7, m7))
                V.scalar_tensor_tensor(h2, t1, 0.0, v7.unsqueeze(2).to_broadcast([P, NC, D]), ALU.max, ALU.mult).then_inc(sem("h2_ready"), 1)
                for j in range(NC):
                    n, pq = c * NC + j, PSB[2 + (c * NC + j) % 6]
                    dve.wait_ge(sem("hi_ready"), n + 1)
                    V.tensor_tensor(res[:, n % 2, 0, :], pq[:, 0:HID], Pst[:, j, 0, :], ALU.subtract)
                    V.tensor_tensor(res[:, n % 2, 1, :], pq[:, HID:], Qt[:, n, 0, :], ALU.subtract).then_inc(sem("res_ready"), 1)
                    dve.wait_ge(sem("mid_ready"), n + 1)
                    V.tensor_tensor(Pst[:, j, 2, :], res[:, n % 2, 0, :], Pst[:, j, 1, :], ALU.subtract)
                    last = V.tensor_tensor(Qt[:, n, 2, :], res[:, n % 2, 1, :], Qt[:, n, 1, :], ALU.subtract)
                    if j < NC - 1:
                        last.then_inc(sem("lo_ready"), 1)
                last.then_inc(sem("split_done"), 1)

            V.tensor_scalar(cnt27[:, 0, :], run0[0:BT + 1, :], row26, None, ALU.mult).then_inc(sem("c27_init"), 1)

            def targets(i, q, first=False):
                b, n = 2 * i + q, 2 * i + q + 1
                B = b * BT
                hi = hiE[:, bass.ds(B, BT)]
                V.tensor_tensor(oh49[:, q, :, :], hi.unsqueeze(2).to_broadcast([P, BT, NT]),
                                iota49.unsqueeze(1).to_broadcast([P, BT, NT]), ALU.is_equal).then_inc(sem("b49_ready"), 1)
                if not (first and q == 0):
                    dve.wait_ge(sem("pos_ready"), b)
                V.tensor_scalar(padf, hi, 0.0, dump, ALU.is_lt, ALU.mult)
                if not first:
                    dve.wait_ge(sem(f"scat{q}"), 16 * BT * i)
                V.scalar_tensor_tensor(Rb[:, q, :, HID], hi, -float(P), srcE[:, bass.ds(B, BT)], ALU.mult, ALU.add)

                def hotb(t):
                    g = B + t
                    if not (first and q == 0 and t < 4):
                        dve.wait_ge(sem("bT_ps"), g - 3)
                    V.tensor_scalar(OHr[:, (t + 2 * q) % 4, :], iotab, dBE[:, bass.ds(g, 1)], None, ALU.is_equal).then_inc(sem("ohb_ready"), 1)

                def ea_out(j):
                    Gp = b * (BT // 2) + j
                    dve.wait_ge(sem("eaT_ps"), Gp + 1)
                    if not (first and q == 0 and j < 2):
                        dve.wait_ge(sem("main_done"), 2 * Gp - 2)
                    V.tensor_copy(EAT[:, (j + q) % 2, :], PSB[4][:, 0:P]).then_inc(sem("ea_out"), 1)

                def rank(m):
                    lo, hi_ = m * RK, min((m + 1) * RK, BT)
                    dve.wait_ge(sem("rk_ps"), 3 * b + m + 1)
                    V.tensor_tensor(t49[:, lo:hi_, :], PSB[5 + m % 2][:, 0:(hi_ - lo) * NT].rearrange("p (t b) -> p t b", b=NT),
                                    oh49[:, q, lo:hi_, :], ALU.mult).then_inc(sem("rk_used"), 1)
                hotb(0)
                hotb(1)
                for t in range(BT):
                    if t % 2 == 0:
                        ea_out(t // 2)
                    if t < BT - 2:
                        hotb(t + 2)
                    if t in (4, 8, 18):
                        rank({4: 0, 8: 1, 18: 2}[t])
                    if t == 20:
                        dve.wait_ge(sem("rk_used"), 3 * n)
                        V.tensor_reduce(posf, t49, AX.X, ALU.add).then_inc(sem("posf_ready"), 1)
                    if t == 22:
                        dve.wait_ge(sem("posf_ready"), n)
                        V.tensor_tensor(pos[:, q, :], posf, padf, ALU.add).then_inc(sem("pos_ready"), 1)
            targets(0, 0, True)
            targets(0, 1, True)
            with dve.Fori(1, NB // 2) as i:
                for q in range(2):
                    targets(i, q)

            for q in range(2):
                dve.wait_ge(sem(f"scat{q}"), 16 * BT * (NB // 2))
            V.memset(pbrow, 0).then_inc(sem("pbz"), 1)
            V.memset(hid[:, :, :, HID:], 1.0)
            V.memset(accB, 0.0).then_inc(sem("accB_done"), 1)
            dve.wait_ge(sem("accB_done"), 1)
            dve.wait_ge(sem("pb_in"), 16)

            def hotp(i, m, first):
                s, k, g = m // CP, m % CP, SB * i + m
                if k == 0:
                    dve.wait_ge(sem(f"xr_in{s}"), 16 * (i + 1))
                if not first:
                    dve.wait_ge(sem("seg_ps"), g - SB + 1)
                for j in range(PR):
                    c = j * XW + HID
                    last = V.tensor_scalar(OHp[:, m, j, :], iota[:, 0:P], XR[:, s, k, c:c + 1], None, ALU.is_equal)
                last.then_inc(sem("ohp_ready"), 1)

            def add_r(g, m, first):
                s, k = m // CP, m % CP
                dve.wait_ge(sem("pp_ps"), g + 1)
                if not (first and m < 2):
                    dve.wait_ge(sem("hid_ready"), g - 1)
                V.tensor_tensor(hp[:, m % 2, :, :], PSB[2 + m % 2][:].rearrange("p (j h) -> p j h", j=PR),
                                XR[:, s, k, :].rearrange("p (j w) -> p j w", j=PR)[:, :, 0:HID], ALU.add).then_inc(sem("hp_ready"), 1)

            def add_up(g, m, reg):
                dve.wait_ge(sem("seg_ps"), g + 1)
                dve.wait_ge(sem("accB_done"), g + 1)
                a = flat(accB[:, bass.ds(reg, 1), :])
                V.tensor_tensor(a, a, PSB[4 + m % 2][:, 0:XW], ALU.add).then_inc(sem("accB_done"), 1)

            def sources(i, first=False):
                regs = pair_bins(ENG.DVE, i)
                for m in range(SB):
                    hotp(i, m, first)
                    if not (first and m < 2):
                        add_r(SB * i + m - 2, (m - 2) % SB, first)
                    if not (first and m < 4):
                        add_up(SB * i + m - 4, (m - 4) % SB, regs[m])
            sources(0, True)
            with dve.Fori(1, NTURN) as i:
                sources(i)
            regs = pair_bins(ENG.DVE, NTURN)
            for m in range(SB - 4, SB):
                if m < SB - 2:
                    add_r(NPAIR - SB + m + 2, m + 2, False)
                add_up(NPAIR - SB + m, m, regs[m - SB + 4])
            dve.wait_ge(sem("accB_done"), NPAIR + 1)
            for c in range(NCH):
                if c:
                    dve.wait_ge(sem("fo_ready"), c)
                link(V.tensor_tensor(fo, b2B.unsqueeze(1).to_broadcast([P, NC, D]),
                                     accB[:, c * NC:(c + 1) * NC, HID:].to_broadcast([P, NC, D]), ALU.mult))
                dve.wait_ge(sem("x1_in"), 16 * (c + 1))
                link(V.tensor_tensor(fo, fo, x1b, ALU.add))
                dve.wait_ge(sem("fo_ps"), c + 1)
                if c:
                    dve.wait_ge(sem("stored"), 16 * c)
                V.tensor_tensor(flat(fo2[:, 0:4, :]), flat(fo[:, 0:4, :]), PSB[4][:], ALU.add)
                V.tensor_tensor(flat(fo2[:, 4:NC, :]), flat(fo[:, 4:NC, :]), PSB[5][:, 0:(NC - 4) * D], ALU.add).then_inc(sem("fo_ready"), 1)

        @block.tensor
        def _(pe):
            pe.wait_ge(sem("c0"), 9)
            pe.wait_ge(sem("rF_ready"), 1)
            for g in range(NG):
                if g >= 2:
                    pe.wait_ge(sem("eT_used"), g - 1)
                for a in range(3):
                    last = pe.transpose(PSB[2 + g % 2][:, a * TG:(a + 1) * TG], rF[:, a, g * P:(g + 1) * P], ident[0:TG, 0:TG])
                last.then_inc(sem("eT_ps"), 1)
            pe.wait_ge(sem("w_in"), 48)
            pe.transpose(PSB[4][:, 0:D], w_sb, ident)
            pe.wait_ge(sem("attb_ready"), 1)
            pe.matmul(PSB[4][:, D:XC], w_sb, attb, start=True, stop=True).then_inc(sem("wx_ps"), 1)
            pe.wait_ge(sem("wx_ready"), 1)

            def chunk(c, first=False):
                pe.wait_ge(sem("hc_ready"), c + 1)
                for j in range(NC):
                    last = pe.transpose(PSB[j // 4][:, (j % 4) * P:(j % 4 + 1) * P], hc[:, j, :], ident)
                last.then_inc(sem("hT_ps"), 1)
                pe.wait_ge(sem("hcT_ready"), c + 1)
                if not first:
                    pe.wait_ge(sem("hx_ready"), c)
                for j in range(NC):
                    last = pe.matmul(PSB[5 + j // 3][:, (j % 3) * XC:(j % 3 + 1) * XC], hcT[:, j, :], wx, start=True, stop=True)
                last.then_inc(sem("hx_ps"), 1)
            chunk(0, True)
            with pe.Fori(1, NCH) as c:
                chunk(c)

            last127 = ident[:, P - 1:P]
            pe.wait_ge(sem("last_ready"), 1)
            for j, (lo, hi) in enumerate(chunks):
                if j:
                    pe.wait_ge(sem("rows_used"), j)
                pe.matmul(PSB[2][0:1, 0:hi - lo], last127, dE[:, lo:hi], start=True, stop=True).then_inc(sem("rows_ps"), 1)
                pe.matmul(PSB[3][0:1, 0:hi - lo], last127, tmpr[:, lo:hi], start=True, stop=True).then_inc(sem("rows_ps"), 1)
            pe.wait_ge(sem("binf_ready"), 1)
            for j, (lo, hi) in enumerate(chunks):
                if j:
                    pe.wait_ge(sem("cols_used"), j)
                pe.matmul(PSB[4][:, 0:hi - lo], ones[0:1, :], tmpr[0:1, lo:hi], start=True, stop=True)
                pe.matmul(PSB[5][:, 0:hi - lo], ones[0:1, :], dE[0:1, lo:hi], start=True, stop=True)
                pe.matmul(PSB[6][:, 0:hi - lo], ones[0:1, :], lastr[0:1, lo:hi], start=True, stop=True).then_inc(sem("cols_ps"), 1)
            pe.wait_ge(sem("cols_used"), len(chunks))

            def count(b, s, start=False, stop=False):
                pe.wait_ge(sem("oh49_ready"), b + 1)
                for m in range(3):
                    lo, hi = m * RK, min((m + 1) * RK, BT)
                    last = pe.matmul(PSB[5 + m][:, 0:(hi - lo) * NT], onesb, flat(oh49p[:, s, lo:hi, :]), start=start, stop=stop)
                last.then_inc(sem("counted"), 1)
            count(0, 0, start=True)
            count(1, 1)
            with pe.Fori(1, NB // 2 - 1) as i:
                for q in range(2):
                    count(2 * i + q, q)
            count(NB - 2, 0)
            count(NB - 1, 1, stop=True)

            def turn(b, s, t, first=False):
                pe.wait_ge(sem("oh_ready"), b * BT + t + 1)
                if not (first and t < 2):
                    pe.wait_ge(sem("ohT_ready"), b * BT + t - 1)
                for k in range(2):
                    last = pe.transpose(PSB[t % 2][:].bitcast(BF16)[:, k * P:(k + 1) * P], OHb[:, s, t, k * P:(k + 1) * P], identb)
                last.then_inc(sem("ohT_ps"), 1)

            def expand(b, t, regs, first=False):
                pe.wait_ge(sem("ohT_ready"), b * BT + t + 1)
                half, j = divmod(t, BT // 2)
                if j == 0 and not first:
                    pe.wait_ge(sem("ab_out"), 2 * b - 1 + half)
                for k in range(2):
                    last = pe.matmul(ab_ps[half][:, j, :, :].rearrange("p s c -> p (s c)"), ohT[:, t % 2, k * P:(k + 1) * P],
                                     flat(aT3[:, bass.ds(regs[t] + k, 1), :, :]), start=(k == 0), stop=(k == 1))
                last.then_inc(sem("expanded"), 1)

            HB = H * BT

            def chain_resets(b):
                pe.wait_ge(sem("isl_ready"), b + 1)
                pe.transpose(rT_ps, flat(isl4), ident).then_inc(sem("rT_ready"), 1)

            def chain_v(b):
                pe.wait_ge(sem("rb_ready"), b + 1)
                pe.wait_ge(sem("v_ready"), b + 1)
                pe.transpose(vT_ps, flat(vE), ident).then_inc(sem("vT_ready"), 1)

            def chain_ends(b):
                pe.wait_ge(sem("bk_ready"), b + 1)
                pe.matmul(rows_ps[:, 0:HB], FT[:, P - 1:P], ident[0:HB, 0:HB], start=True, stop=True)
                pe.matmul(rows_ps[:, HB:], BK[:, 0:1], ident[0:HB, 0:HB], start=True, stop=True).then_inc(sem("rows_ready"), 1)
                pe.transpose(flat(BE_ps), BK, ident[0:HB, 0:HB])

            def chain_carry(b):
                pe.wait_ge(sem("cin_ready"), b + 1)
                pe.matmul(flat(bc_ps), ones[0:1, :], flat(cin), start=True, stop=True).then_inc(sem("bc_ready"), 1)

            pe.wait_ge(sem("bins_ready"), 1)
            pe.wait_ge(sem("aT3_ready"), 1)
            pe.wait_ge(sem("hx_used"), NCH)
            regs = bins(ENG.PE, 0, BT)
            for t in range(BT):
                turn(0, 0, t, True)
                expand(0, t, regs, True)
            chain_resets(0)
            regs = bins(ENG.PE, 1, BT)
            for t in range(BT):
                turn(1, 1, t)
                expand(1, t, regs)
            chain_v(0)
            chain_ends(0)
            chain_carry(0)

            def batch(b, q, ahead2=True, ahead1=True):
                if ahead2:
                    regs = bins(ENG.PE, b + 2, BT)
                pe.wait_ge(sem("g_ready"), b + 1)
                pe.wait_ge(sem("wide_ready"), b * BT + 1)
                pe.matmul(fac_ps, OH[0:1, 2 * q, 0:P], ru[:, 2, :], start=True, stop=True).then_inc(sem("fac_ps"), 1)
                for t in range(BT):
                    if ahead2:
                        turn(b + 2, q, t)
                        if t:
                            expand(b + 2, t - 1, regs)
                    pe.wait_ge(sem("wide_ready"), b * BT + t + 1)
                    pe.wait_ge(sem("msg_ready"), 2 * b + (1 if t < BT // 2 else 2))
                    if t >= 2:
                        pe.wait_ge(sem("acc_done"), b * (BT + 1) + t + 1)
                    for k in range(2):
                        last = pe.matmul(PSB[3 + t % 2][:, k * H * MW:(k + 1) * H * MW], OH[:, (t + 2 * q) % 4, k * P:(k + 1) * P],
                                         flat(msg[:, t, :, :]), start=True, stop=True)
                    last.then_inc(sem("agg_ready"), 1)
                    if ahead1:
                        for at, step in ((2, chain_resets), (7, chain_v), (10, chain_ends), (14, chain_carry)):
                            if t == at:
                                step(b + 1)
                if ahead2:
                    expand(b + 2, BT - 1, regs)
            batch(0, 0)
            batch(1, 1)
            with pe.Fori(1, NB // 2 - 1) as i:
                for q in range(2):
                    batch(2 * i + q, q)
            batch(NB - 2, 0, ahead2=False)
            batch(NB - 1, 1, ahead2=False, ahead1=False)

            for c in range(NCH):
                pe.wait_ge(sem("h2_ready"), c + 1)
                for j in range(NC):
                    last = pe.transpose(PSB[j // 4][:, (j % 4) * P:(j % 4 + 1) * P], h2[:, j, :], ident)
                last.then_inc(sem("h2T_ps"), 1)
                pe.wait_ge(sem("h2T_ready"), c + 1)
                for j in range(NC):
                    n = c * NC + j
                    if n >= 6:
                        pe.wait_ge(sem("res_ready"), n - 5)
                    pe.matmul(PSB[2 + n % 6][:], h2T[:, j, :], flat(w1n), start=True, stop=False)
                    pe.matmul(PSB[2 + n % 6][:, 0:HID], ones[0:1, :], b1r, start=False, stop=True).then_inc(sem("pq_ps"), 1)

            def targets(i, q, first=False, final=False):
                b, n = 2 * i + q, 2 * i + q + 1
                B = b * BT
                regs = bins(ENG.PE, b, BT)

                def turn(t):
                    pe.wait_ge(sem("ohb_ready"), B + t + 1)
                    for k in range(2):
                        last = pe.transpose(PSB[t % 2][:].bitcast(BF16)[:, k * P:(k + 1) * P],
                                            OHr[:, (t + 2 * q) % 4, k * P:(k + 1) * P], identb)
                    last.then_inc(sem("bT_ps"), 1)

                def turn_ea(j):
                    if not (first and q == 0 and j == 0):
                        pe.wait_ge(sem("ea_out"), b * (BT // 2) + j)
                    pe.transpose(PSB[4][:, 0:P], flat(EAb[:, q, 2 * j:2 * j + 2, :]), ident).then_inc(sem("eaT_ps"), 1)

                def main(t):
                    g = B + t
                    pe.wait_ge(sem("bT_ready"), g + 1)
                    if not (first and q == 0 and t < 2):
                        pe.wait_ge(sem("r_out"), g - 1)
                    o = PSB[2 + t % 2][:, 0:HID]
                    for k in range(2):
                        for part in range(3):
                            pe.matmul(o, ohTb[:, t % 2, k * P:(k + 1) * P],
                                      flat(Qt[:, bass.ds(regs[t] + k, 1), part, :]), start=(k == 0 and part == 0), stop=False)
                    pe.wait_ge(sem("ea_out"), b * (BT // 2) + t // 2 + 1)
                    h = (t % 2) * DE
                    pe.matmul(o, EAT[h:h + DE, (t // 2 + q) % 2, :], w1e[h:h + DE, :], start=False, stop=True).then_inc(sem("main_done"), 1)

                def rank(m):
                    lo, hi = m * RK, min((m + 1) * RK, BT)
                    if m == 2:
                        pe.wait_ge(sem("rk_used"), 3 * b + 1)
                    elif m == 0 and not (first and q == 0):
                        pe.wait_ge(sem("rk_used"), 3 * b)
                    o = PSB[5 + m % 2]
                    pe.matmul(o[:, 0:(hi - lo) * NT], tri, flat(oh49[:, q, lo:hi, :]), start=True, stop=False)
                    for t in range(lo, hi):
                        last = pe.matmul(o[:, (t - lo) * NT:(t - lo + 1) * NT], tri27[:, t:t + 1].to_broadcast([BT + 1, P]),
                                         cnt27[:, 1 - q, :], start=False, stop=(t == hi - 1))
                    last.then_inc(sem("rk_ps"), 1)

                pe.wait_ge(sem("b49_ready"), n)
                c27 = PSB[7][0:BT + 1, 0:NT]
                for t in range(BT):
                    pe.matmul(c27, band[:, BT - t:2 * BT + 1 - t], oh49[:, q, t, :], start=(t == 0), stop=False)
                pe.matmul(c27, col27, cnt27[:, q, :], start=False, stop=True).then_inc(sem("c27_ps"), 1)
                if q == 0:
                    pe.wait_ge(sem("ea_in0"), 16 * (i + 1))
                elif final:
                    pe.wait_ge(sem("ea_last"), 32)
                else:
                    pe.wait_ge(sem("ea_in1"), 16 * (i + 1))
                turn(0)
                turn_ea(0)
                for t in range(BT):
                    if t < BT - 1:
                        turn(t + 1)
                    if t % 2 == 1 and t < BT - 1:
                        turn_ea((t + 1) // 2)
                    main(t)
                    if t == 1:
                        pe.wait_ge(sem("c27_ready"), n)
                    if t in (1, 4, 14):
                        rank({1: 0, 4: 1, 14: 2}[t])
            pe.wait_ge(sem("split_done"), NCH)
            pe.wait_ge(sem("c27_init"), 1)
            targets(0, 0, True)
            targets(0, 1, True)
            with pe.Fori(1, NB // 2 - 1) as i:
                for q in range(2):
                    targets(i, q)
            for q in range(2):
                targets(NB // 2 - 1, q, final=True)

            def turnp(g, m):
                pe.wait_ge(sem("ohp_ready"), g + 1)
                for j in range(PR):
                    last = pe.transpose(PSB[m % 2][:, j * P:(j + 1) * P], OHp[:, m, j, :], ident)
                last.then_inc(sem("pT_ps"), 1)

            def source_rows(g, m, reg, first):
                pe.wait_ge(sem("pT_ready"), g + 1)
                if not (first and m < 2):
                    pe.wait_ge(sem("hp_ready"), g - 1)
                for j in range(PR):
                    for part in range(3):
                        last = pe.matmul(PSB[2 + m % 2][:, j * HID:(j + 1) * HID], ohTp[:, m % 2, j, :],
                                         flat(Pt[:, bass.ds(reg, 1), part, :]), start=(part == 0), stop=(part == 2))
                last.then_inc(sem("pp_ps"), 1)

            def segment(g, m, first):
                pe.wait_ge(sem("hid_ready"), g + 1)
                if not (first and m < 2):
                    pe.wait_ge(sem("accB_done"), g)
                for j in range(PR):
                    last = pe.matmul(PSB[4 + m % 2][:, 0:XW], OHp[:, m, j, :], hid[:, m % 2, j, :], start=(j == 0), stop=(j == PR - 1))
                last.then_inc(sem("seg_ps"), 1)

            def sources(i, first=False):
                regs = pair_bins(ENG.PE, i)
                for m in range(SB):
                    turnp(SB * i + m, m)
                    if not (first and m < 1):
                        source_rows(SB * i + m - 1, (m - 1) % SB, regs[m + 3], first)
                    if not (first and m < 3):
                        segment(SB * i + m - 3, (m - 3) % SB, first)
            pe.wait_ge(sem("pt_in"), 16)
            pe.wait_ge(sem("pb_in"), 16)
            sources(0, True)
            with pe.Fori(1, NTURN) as i:
                sources(i)
            regs = pair_bins(ENG.PE, NTURN)
            source_rows(NPAIR - 1, SB - 1, regs[3], False)
            for m in range(SB - 3, SB):
                segment(NPAIR - SB + m, m, False)
            for c in range(NCH):
                pe.wait_ge(sem("stg_ready"), c + 1)
                if c:
                    pe.wait_ge(sem("sT_ready"), c)
                for j in range(NC):
                    for k in range(2):
                        last = pe.transpose(PSB[j // 2][:, (j % 2) * HID + k * P:(j % 2) * HID + (k + 1) * P], stg[:, j, k * P:(k + 1) * P], ident)
                last.then_inc(sem("sT_ps"), 1)
                pe.wait_ge(sem("sT_ready"), c + 1)
                if c:
                    pe.wait_ge(sem("fo_ready"), c)
                for j in range(NC):
                    for k in range(2):
                        last = pe.matmul(PSB[4 + j // 4][:, (j % 4) * D:(j % 4 + 1) * D], sT[:, j, k * P:(k + 1) * P], w2_sb[:, k, :],
                                         start=(k == 0), stop=(k == 1))
                last.then_inc(sem("fo_ps"), 1)


_INS = ['x', 'src', 'dst', 'edge_attr_64', 'L0_gnn_W', 'L0_gnn_att_src', 'L0_gnn_att_dst', 'L0_gnn_bias',
        'L1_gnn_W1', 'L1_gnn_b1', 'L1_gnn_W2', 'L1_gnn_b2']


def kernel(**inputs):
    import numpy as _np
    import concourse.bacc as _bacc
    from concourse.bass_utils import run_bass_kernel_spmd as _run

    nc = _bacc.Bacc("TRN2", target_bir_lowering=False, num_devices=1)
    arrays, args = {}, []
    for name in _INS:
        a = _np.ascontiguousarray(inputs[name])
        arrays[f"in_{name}"] = a
        args.append(nc.dram_tensor(f"in_{name}", a.shape, mybir.dt.from_np(a.dtype), kind="ExternalInput").ap())
    args.append(nc.dram_tensor("out_0", (N, D), F32, kind="ExternalOutput").ap())
    gnn(nc, *args)
    r = _run(nc, [arrays], core_ids=[0])
    return r.results[0]["out_0"]
```

```python
import concourse.bass as bass
from concourse import mybir
from contextlib import ExitStack

F32 = mybir.dt.float32
BF16 = mybir.dt.bfloat16
I32 = mybir.dt.int32
ALU = mybir.AluOpType
ACT = mybir.ActivationFunctionType
AX = mybir.AxisListType
ENG = mybir.EngineType

P = 128
N = 6250
D = 128
E = 206250
DE = 64
HID = 256
H = 4
DH = D // H
NT = -(-N // P)
NLAST = N - (NT - 1) * P
NPAD = NT * P
T = -(-E // P)
ELAST = E - (T - 1) * P
BT = 26
NB = T // BT
TG = 124
NG = T // TG
TP = T + BT
TR = -(-TP // P)
RB = 28
GW = D + H
XC = D + 2 * H
MW = DH + 2
BIG = 1e30
EPS = 1e-5
SLOPE = 0.2
NC = 7
NCH = NT // NC
PR = 2
GR = PR * P
CP = 2
NS = 4
SB = CP * NS
NPAIR = -(-((E + NT * (GR - 1)) // GR) // SB) * SB
NTURN = NPAIR // SB
XROWS = NPAIR * GR
FILLR = 4 * P
NFILL = -(-(XROWS - E) // FILLR)
XW = HID + 1
PBJ = -(-NPAIR // P)
CK = 512
RK = CK // NT
assert NB * BT == T and NG * TG == T and NCH * NC == NT and NB % 2 == 0


def dims(n):
    return " ".join("abcd"[:n])


def gnn(nc, x, src, dst, ea, W, asrc, adst, bias, W1, b1, W2, b2, out):
    h_tab = nc.dram_tensor("h_tab", (NPAD, GW), F32).ap()
    x_tab = nc.dram_tensor("x_tab", (NPAD, D), F32).ap()
    x1_tab = nc.dram_tensor("x1_tab", (NPAD, D), F32).ap()
    p_tab = nc.dram_tensor("p_tab", (P, NT * 3 * HID), BF16).ap()
    xr = nc.dram_tensor("xr", (XROWS + GR, XW), F32).ap()
    pb_tab = nc.dram_tensor("pb_tab", (P * PBJ,), I32).ap()

    ctx = ExitStack()
    sems = {}
    with ctx:
        WORDS = 53120
        arena = ctx.enter_context(nc.sbuf_tensor("arena", [P, WORDS], F32))
        PSB = [ctx.enter_context(nc.psum_tensor(f"bank{i}", [P, CK], F32)) for i in range(8)]

        def sem(name):
            if name not in sems:
                sems[name] = ctx.enter_context(nc.semaphore(name))
            return sems[name]

        class Region:
            def __init__(self, start, end=WORDS):
                self.at, self.end = start, end

            def __call__(self, shape, dt=F32, parts=P):
                n = 1
                for s in shape:
                    n *= s
                words = -(-n // 2) if dt == BF16 else n
                words = -(-words // 8) * 8
                v = arena[0:parts, self.at:self.at + words]
                if dt != F32:
                    v = v.bitcast(dt)
                v = v[:, 0:n]
                if len(shape) > 1:
                    d = dims(len(shape))
                    v = v.rearrange(f"p ({d}) -> p {d}", **dict(zip(d.split(), shape)))
                self.at += words
                assert self.at <= self.end, (self.at, self.end)
                return v

        K = Region(0)
        ident, ones, iota = K([P]), K([P]), K([2 * P])
        identb, onesb, iota49, iotab = K([P], BF16), K([P], BF16), K([NT], BF16), K([2 * P], BF16)
        srcE, dBE = K([TP]), K([TP])
        hiE, lastE = K([TP], BF16), K([TP], BF16)
        bin_row = K([(NB + 1) * RB], I32, 1)
        run0, rend, eps = K([NT]), K([NT], I32, 1), K([1])
        mean, rstd = K([NT]), K([NT])
        w1n, w1e, w2_sb = K([2, HID]), K([HID]), K([2, D])
        biasB, b2B, b1r = K([D]), K([D]), K([HID], F32, 1)
        tri, band = K([P], BF16), K([2 * BT - 1], BF16)
        tri26 = K([BT], BF16, BT)
        dump = K([1])
        X0 = K.at
        X = Region(X0)
        G, OHb = X([2, BT, GW]), X([2, BT, 2 * P], BF16)
        X([6500])
        Y0 = X.at
        Y = Region(Y0)
        acc = Y([NT + 1, H * MW])
        Y1 = Y.at
        aT, aT3 = Y([NT + 1, 2 * H]), Y([NT + 1, 3, 2 * H], BF16)
        s1E, s2E = Y([TP], BF16), Y([TP], BF16)
        thruF, thruB, contN = Y([TP], BF16, 1), Y([TP], BF16, 1), Y([TP], F32, 1)
        zfill = Y([FILLR // P, XW])
        Z0 = Y.at

        S = Region(X0, Y0)
        rI, rF = S([3, NG * P], I32, TG), S([3, NG * P], F32, TG)
        sq = Region(X0, Y0)([NT, D])
        xs = S([NT, D])
        hc, hcT, hx = S([NC, D]), S([NC, P]), S([NC, XC])
        w_sb, wx, att, attb, hm = S([P]), S([XC]), S([2]), S([2 * H]), S([H])
        S = Region(X0 + 3 * NG * P * 2)
        inbin = S([NC, TR * P], BF16)
        cntT, cnt, cnti = S([NT]), S([8, NT]), S([2, NT], I32)
        k256, pbc, pbf, pbi = S([PBJ]), S([PBJ, NT]), S([PBJ]), S([PBJ], I32)
        S = Region(Z0)
        isrc, dE, nE = S([TP], I32), S([TP]), S([TP])
        lastr, lflag, tmpr = S([TP], F32, 1), S([TP], F32, 1), S([TP])
        irow = isrc

        S = Region(Z0)
        aRes, ohT, OH, msg, idx = S([NT + 1, 2 * H]), S([2, 2 * P], BF16), S([4, 2 * P]), S([BT, H, MW]), S([2, BT], I32)
        abS, vE, isl4 = S([2, BT, 2 * H]), S([H, BT]), S([H, BT])
        rb, FT, BK = S([P + 1], F32, H * BT), S([P], F32, H * BT), S([P], F32, H * BT)
        resF, resB = S([H, BT + 1], F32, 1), S([H, BT], F32, 1)
        rowF, rowB = S([H, BT + 1], F32, 1), S([H, BT], F32, 1)
        CF, CB, cin = S([H, BT + 1], F32, 1), S([H, BT], F32, 1), S([2, H, BT], F32, 1)
        y12, ym, R = S([2, H, BT]), S([H, BT]), S([H, BT])
        ZZ, LL, DF, WT = S([3, H, BT]), S([3, H, BT]), S([2, H, BT]), S([2, H, BT])
        ru, fac = S([5, H], F32, 1), S([H])

        Qt = Region(X0, Y0)([NT + 1, 3, HID], BF16)
        S = Region(Y1)
        hs, xi = S([2, NC, D]), S([2, NC, D])
        t1, x1c, sqm, h2, h2T = (S([NC, D]) for _ in range(5))
        den, rec, m7, v7 = S([NC, H]), S([NC, H]), S([NC]), S([NC])
        Pst, res = S([2, NC, 3, HID], BF16), S([2, 2, HID])

        S = Region(Y0)
        Rb, EAb, EAT = S([2, BT, XW]), S([2, BT, DE]), S([2, P])
        OHr, ohTb, oh49 = S([4, 2 * P], BF16), S([2, 2 * P], BF16), S([2, BT, NT], BF16)
        cnt26, t49, posf, padf, pos = S([NT], BF16, BT), S([BT, NT]), S([BT]), S([BT]), S([2, BT], I32)

        Pt = Region(X0, Y0)([NT, 3, HID], BF16)
        S = Region(Y0)
        accB, XR, OHp = S([NT, XW]), S([NS, CP, PR * XW]), S([SB, PR, P])
        OHq = S([4, PR, P], BF16)
        ohTp, hp, hid = S([2, PR, P], BF16), S([2, PR, HID]), S([2, PR, XW])
        pbrow = S([NPAIR + 16], I32, 1)
        S = Region(X0, Y0)
        stg, sT, x1b, fo, fo2 = S([NC, HID]), S([NC, HID]), S([NC, D]), S([NC, D]), S([NC, D])

        ab_ps = [PSB[j][:, 0:BT // 2 * 3 * 2 * H].rearrange("p (t s c) -> p t s c", s=3, c=2 * H) for j in (2, 7)]
        vT_ps = PSB[5][0:H * BT, 0:P]
        rT_ps = PSB[5][0:H * BT, P:2 * P]
        BE_ps = PSB[6][:, 0:H * BT].rearrange("p (h t) -> p h t", h=H)
        fac_ps = PSB[6][:, 128:128 + H]
        rows_ps = PSB[5][0:1, 256:256 + 2 * H * BT]
        bc_ps = PSB[6][:, 256:256 + 2 * H * BT].rearrange("p (c h t) -> p c h t", c=2, h=H)

        def flat(v):
            d = dims(len(v.shape) - 1)
            return v.rearrange(f"p {d} -> p ({d})") if len(v.shape) > 2 else v

        PIECES = [(m * BT // 4, (m + 1) * BT // 4) for m in range(4)]
        piece = lambda t: [lo <= t < hi for lo, hi in PIECES].index(True)
        chunks = [(c, min(c + CK, TP)) for c in range(0, TP, CK)]
        e0 = (NG - 1) * TG * P
        block = ctx.enter_context(nc.Block())

        def bins(engine, b, count):
            return nc.values_load_multi_w_load_instructions(
                bin_row[0:1, bass.ds(b * RB, count)], engines=[engine], min_val=0, max_val=NT - 1,
                skip_runtime_bounds_check_because="a node's tile, clamped at 0")[1]

        def pair_bins(engine, i):
            return nc.values_load_multi_w_load_instructions(
                pbrow[0:1, bass.ds(i * SB, SB + 4)], engines=[engine], min_val=0, max_val=NT - 1,
                skip_runtime_bounds_check_because="counted over the bins, held under their number")[1]

        @block.sync
        def _(sp):
            sp.dma_start(xs[:, 0:NT - 1, :], x[0:(NT - 1) * P, :].rearrange("(n p) f -> p n f", p=P)).then_inc(sem("x_in"), 16)
            sp.wait_ge(sem("xpad"), 1)
            sp.dma_start(xs[0:NLAST, NT - 1, :], x[(NT - 1) * P:N, :]).then_inc(sem("x_in"), 16)
            sp.wait_ge(sem("x_in"), 32)
            sp.dma_start(x_tab.rearrange("(n p) f -> p n f", p=P), xs).then_inc(sem("x_out"), 16)
            sp.wait_ge(sem("zf_ready"), 2)
            for f in range(NFILL):
                r0 = XROWS - (NFILL - f) * FILLR
                sp.dma_start(xr[r0:r0 + FILLR, :].rearrange("(p j) w -> p j w", p=P), zfill).then_inc(sem("filled"), 16)
            sp.wait_ge(sem("pbi_ready"), 1)
            sp.dma_start(pb_tab.rearrange("(p j) -> p j", p=P), pbi).then_inc(sem("pb_out"), 16)
            sp.wait_ge(sem("rend_ready"), 1)
            with sp.Fori(0, NT) as b:
                r = nc.values_load_multi_w_load_instructions(
                    rend[0:1, bass.ds(b, 1)], engines=[ENG.SP], min_val=0, max_val=XROWS,
                    skip_runtime_bounds_check_because="a sum of counts of edges, rounded up")[1][0]
                sp.wait_ge(sem("filled"), 16 * NFILL + 16 * b)
                sp.dma_start(xr[bass.ds(r, GR), :].rearrange("(p j) w -> p j w", p=P), zfill[:, 0:2, :]).then_inc(sem("filled"), 16)
            sp.wait_ge(sem("pb_out"), 16)
            sp.wait_ge(sem("x_out"), 16)
            sp.wait_ge(sem("filled"), 16 * (NFILL + NT))
            sp.wait_ge(sem("acc_done"), 1 + NB * (BT + 1))
            sp.wait_ge(sem("expanded"), NB * BT)
            rows = lambda v, c: v[c * NC * P:(c + 1) * NC * P, :].rearrange("(n p) f -> p n f", p=P)

            def load_nodes(c):
                sp.dma_start(hs[:, c % 2, :, :], rows(h_tab, c)[:, :, 0:D]).then_inc(sem(f"hs_in{c % 2}"), 16)
                sp.dma_start(xi[:, c % 2, :, :], rows(x_tab, c)).then_inc(sem(f"hs_in{c % 2}"), 16)
            load_nodes(0)
            load_nodes(1)
            for c in range(NCH):
                sp.wait_ge(sem("x1_ready"), c + 1)
                sp.dma_start(rows(x1_tab, c), x1c).then_inc(sem("x1_out"), 16)
                if c + 2 < NCH:
                    load_nodes(c + 2)
                sp.wait_ge(sem("split_done"), c + 1)
                sp.dma_start(p_tab[:, c * NC * 3 * HID:(c + 1) * NC * 3 * HID], flat(Pst[:, c % 2, :, :, :])).then_inc(sem(f"p_out{c % 2}"), 16)

            def load_ea(b, q, first=False):
                if not first:
                    sp.wait_ge(sem("eaT_ps"), (b - 1) * (BT // 2))
                sp.dma_start(EAb[:, q, :, :], ea[bass.ds(b * (BT * P), BT * P), :].rearrange("(t e) f -> e t f", e=P)).then_inc(sem(f"ea_in{q}"), 16)
            load_ea(0, 0, True)
            load_ea(1, 1, True)
            with sp.Fori(1, NB // 2 - 1) as i:
                for q in range(2):
                    load_ea(2 * i + q, q)
            load_ea(NB - 2, 0)
            sp.wait_ge(sem("eaT_ps"), (NB - 2) * (BT // 2))
            r0 = (NB - 1) * BT * P
            sp.dma_start(EAb[:, 1, 0:BT - 1, :], ea[r0:r0 + (BT - 1) * P, :].rearrange("(t e) f -> e t f", e=P)).then_inc(sem("ea_last"), 16)
            sp.dma_start(EAb[0:ELAST, 1, BT - 1, :], ea[r0 + (BT - 1) * P:E, :]).then_inc(sem("ea_last"), 16)

            sp.wait_ge(sem("main_done"), T)
            sp.wait_ge(sem("p_out0"), 16 * ((NCH + 1) // 2))
            sp.wait_ge(sem("p_out1"), 16 * (NCH // 2))
            sp.dma_start(Pt.rearrange("p a b c -> p (a b c)"), p_tab, max_dma_last_dim=32768).then_inc(sem("pt_in"), 16)
            for q in range(2):
                sp.wait_ge(sem(f"scat{q}"), 16 * BT * (NB // 2))
            def load_xr(c, s, first=False):
                if not first:
                    sp.wait_ge(sem("hp_ready"), c * CP - (NS - 1) * CP)
                sp.dma_start(XR[:, s, :, :], xr[bass.ds(c * (CP * GR), CP * GR), :].rearrange("(k p j) w -> p k (j w)", p=P, j=PR)).then_inc(sem(f"xr_in{s}"), 16)
            for s in range(NS):
                load_xr(s, s, True)
            sp.wait_ge(sem("pbz"), 1)
            sp.dma_start(pbrow[:, 4:4 + NPAIR], pb_tab[0:NPAIR].rearrange("(a n) -> a n", a=1)).then_inc(sem("pb_in"), 16)
            with sp.Fori(1, NTURN) as i:
                for s in range(NS):
                    load_xr(NS * i + s, s)
            sp.wait_ge(sem("accB_done"), NPAIR + 1)
            for c in range(NCH):
                if c:
                    sp.wait_ge(sem("fo_ready"), c)
                sp.dma_start(x1b, x1_tab[c * NC * P:(c + 1) * NC * P, :].rearrange("(n p) f -> p n f", p=P)).then_inc(sem("x1_in"), 16)
                sp.wait_ge(sem("fo_ready"), c + 1)
                full = NC if c < NCH - 1 else NC - 1
                o0 = c * NC * P
                sp.dma_start(out[o0:o0 + full * P, :].rearrange("(n p) f -> p n f", p=P), fo2[:, 0:full, :]).then_inc(sem("stored"), 16)
                if full < NC:
                    sp.dma_start(out[o0 + full * P:N, :], fo2[0:NLAST, full, :]).then_inc(sem("stored"), 16)
            sp.wait_ge(sem("stored"), 16 * (NCH + 1))

        @block.gpsimd
        def _(pool):
            M = nc.gpsimd
            M.memset(rI[:, :, (NG - 1) * P:], -1).then_inc(sem("ipad"), 1)
            M.memset(xs[:, NT - 1, :], 0.0).then_inc(sem("xpad"), 1)
            M.memset(ident, 0.0).then_inc(sem("c0"), 1)
            pool.wait_ge(sem("c0"), 1)
            M.affine_select(out=ident, in_=ident, compare_op=ALU.not_equal, fill=1.0, base=0,
                            pattern=[[-1, P]], channel_multiplier=1).then_inc(sem("c0"), 1)
            M.iota(iota, pattern=[[1, 2 * P]], base=0, channel_multiplier=0,
                   allow_small_or_imprecise_dtypes=True).then_inc(sem("c0"), 1)
            M.iota(iotab, pattern=[[1, 2 * P]], base=0, channel_multiplier=0,
                   allow_small_or_imprecise_dtypes=True).then_inc(sem("c0"), 1)
            M.iota(iota49, pattern=[[1, NT]], base=0, channel_multiplier=0,
                   allow_small_or_imprecise_dtypes=True).then_inc(sem("c0"), 1)
            M.memset(ones, 1.0).then_inc(sem("c0"), 1)
            M.memset(onesb, 1.0).then_inc(sem("c0"), 1)
            M.memset(eps, EPS).then_inc(sem("c0"), 1)
            pool.wait_ge(sem("c0"), 8)
            M.tensor_copy(identb, ident).then_inc(sem("c0"), 1)
            M.memset(zfill, 0.0).then_inc(sem("zf_ready"), 1)
            pool.wait_ge(sem("zf_ready"), 1)
            M.memset(zfill[:, :, HID:XW], -1.0).then_inc(sem("zf_ready"), 1)
            M.memset(aT[:, NT, :], 0.0).then_inc(sem("aT0"), 1)
            M.memset(acc, 0.0).then_inc(sem("acc_done"), 1)
            for m in (tri, tri26):
                M.memset(m, 1.0).then_inc(sem("c1"), 1)
            M.memset(band, 0.0).then_inc(sem("c1"), 1)
            pool.wait_ge(sem("c1"), 3)
            M.affine_select(out=tri, in_=tri, compare_op=ALU.is_gt, fill=0.0, base=0, pattern=[[1, P]], channel_multiplier=-1).then_inc(sem("c1"), 1)
            M.affine_select(out=tri26, in_=tri26, compare_op=ALU.is_gt, fill=0.0, base=0, pattern=[[1, BT]], channel_multiplier=-1).then_inc(sem("c1"), 1)
            M.memset(band[:, BT - 1:BT], 1.0).then_inc(sem("c1"), 1)
            M.iota(dump, pattern=[[0, 1]], base=XROWS, channel_multiplier=1, allow_small_or_imprecise_dtypes=True).then_inc(sem("c1"), 1)
            pool.wait_ge(sem("hx_used"), NCH)
            M.iota(k256, pattern=[[GR, PBJ]], base=0, channel_multiplier=GR * PBJ,
                   allow_small_or_imprecise_dtypes=True).then_inc(sem("k256_ready"), 1)
            pool.wait_ge(sem("h_out"), 16 * NCH)

            def gather(i, q, first=False):
                pool.wait_ge(sem("idx_ready"), 2 * i + q + 1)
                for h in range(2):
                    if not first:
                        pool.wait_ge(sem("msg_ready"), 4 * (2 * i + q - 2) + 2 * h + 2)
                    pool.nop(nofuse=True)
                    for t in range(h * (BT // 2), (h + 1) * (BT // 2)):
                        pool.indirect_dma_start(G[:, q, t, :], None, h_tab,
                                                bass.IndirectOffsetOnAxis(ap=idx[:, q, t:t + 1], axis=0)
                                                ).then_inc(sem(f"gath{q}"), 16)
            gather(0, 0, True)
            gather(0, 1, True)
            with pool.Fori(1, NB // 2) as i:
                for q in range(2):
                    gather(i, q)

            pool.wait_ge(sem("filled"), 16 * (NFILL + NT))
            with pool.Fori(0, NB // 2) as i:
                for q in range(2):
                    n = 2 * i + q + 1
                    pool.wait_ge(sem("pos_ready"), n)
                    for t in range(BT):
                        if t % (BT // 2) == 0:
                            pool.wait_ge(sem("r_out"), (n - 1) * BT + t + BT // 2)
                            pool.nop(nofuse=True)
                        pool.indirect_dma_start(xr, bass.IndirectOffsetOnAxis(ap=pos[:, q, t:t + 1], axis=0),
                                                Rb[:, q, t, :], None).then_inc(sem(f"scat{q}"), 16)

            for q in range(2):
                pool.wait_ge(sem(f"scat{q}"), 16 * BT * (NB // 2))
            M.memset(accB[:, NT // 2:, :], 0.0).then_inc(sem("accB_low"), 1)

            def hotq(i, m, first=False):
                g = SB * i + m
                pool.wait_ge(sem("ohp_ready"), g + 1)
                if not (first and m < 4):
                    pool.wait_ge(sem("pT_ps"), g - 3)
                pool.nop(nofuse=True)
                M.tensor_copy(OHq[:, m % 4, :, :], OHp[:, m, :, :]).then_inc(sem("ohq_ready"), 1)
            for m in range(SB):
                hotq(0, m, True)
            with pool.Fori(1, NTURN) as i:
                for m in range(SB):
                    hotq(i, m)

        @block.scalar
        def _(act):
            A = nc.scalar
            act.wait_ge(sem("ipad"), 1)
            for a, (v, off) in enumerate(((src, 0), (dst, 0), (dst, 1))):
                act.dma_start(rI[:, a, 0:(NG - 1) * P].rearrange("p (g e) -> p g e", e=P),
                              v[off:off + e0].rearrange("(g p e) -> p g e", p=TG, e=P)).then_inc(sem("e_in"), 16)
                act.dma_start(rI[0:TG - 1, a, (NG - 1) * P:],
                              v[off + e0:off + e0 + (TG - 1) * P].rearrange("(p e) -> p e", e=P)).then_inc(sem("e_in"), 16)
                act.dma_start(rI[TG - 1:TG, a, (NG - 1) * P:(NG - 1) * P + ELAST - off],
                              v[off + e0 + (TG - 1) * P:E].rearrange("(p e) -> p e", p=1)).then_inc(sem("e_in"), 16)
            act.dma_start(w_sb, W).then_inc(sem("w_in"), 16)
            act.dma_start(att[:, 0:1], asrc.rearrange("a h o -> (h o) a")).then_inc(sem("w_in"), 16)
            act.dma_start(att[:, 1:2], adst.rearrange("a h o -> (h o) a")).then_inc(sem("w_in"), 16)
            act.dma_start(w1n[:, 0, :], W1[0:D, :]).then_inc(sem("w1_in"), 16)
            act.dma_start(w1n[:, 1, :], W1[D:2 * D, :]).then_inc(sem("w1_in"), 16)
            act.dma_start(w1e[0:DE, :], W1[2 * D:, :]).then_inc(sem("w1_in"), 16)
            act.dma_start(w1e[DE:P, :], W1[2 * D:, :]).then_inc(sem("w1_in"), 16)
            act.dma_start(w2_sb, W2.rearrange("(k p) f -> p k f", p=P)).then_inc(sem("w1_in"), 16)
            act.dma_start(biasB, bias.partition_broadcast(P)).then_inc(sem("w1_in"), 16)
            act.dma_start(b2B, b2.partition_broadcast(P)).then_inc(sem("w1_in"), 16)
            act.dma_start(b1r, b1.rearrange("(a n) -> a n", a=1)).then_inc(sem("w1_in"), 16)
            act.wait_ge(sem("xc_ready"), 1)
            act.wait_ge(sem("eT_used"), NG)
            A.activation(sq, xs, ACT.Square).then_inc(sem("sq_ready"), 1)
            act.wait_ge(sem("var_ready"), 1)
            act.wait_ge(sem("c0"), 9)
            A.activation(rstd, mean, ACT.Sqrt, bias=eps, scale=1.0 / D).then_inc(sem("std_ready"), 1)

            def chunk(c, first=False):
                act.wait_ge(sem("hT_ps"), c + 1)
                A.activation(flat(hcT[:, 0:4, :]), PSB[0][:], ACT.Copy)
                A.activation(flat(hcT[:, 4:NC, :]), PSB[1][:, 0:(NC - 4) * P], ACT.Copy).then_inc(sem("hcT_ready"), 1)
                act.wait_ge(sem("hx_ready"), c + 1)
                A.activation(aT[:, bass.ds(c * NC, NC), :], hx[:, :, D:], ACT.Copy).then_inc(sem("hx_used"), 1)
                act.dma_start(h_tab[bass.ds(c * (NC * P), NC * P), :].rearrange("(n p) f -> p n f", p=P),
                              hx[:, :, 0:GW]).then_inc(sem("h_out"), 16)
            with act.Fori(0, NCH) as c:
                chunk(c)

            def turn_out(b, t, first=False):
                act.wait_ge(sem("ohT_ps"), b * BT + t + 1)
                if not (first and t < 2):
                    act.wait_ge(sem("expanded"), b * BT + t - 1)
                A.activation(ohT[:, t % 2, :], PSB[t % 2][:].bitcast(BF16)[:, 0:2 * P], ACT.Copy).then_inc(sem("ohT_ready"), 1)

            def widen(b, q, t, first=False):
                if not (first and t < 4):
                    act.wait_ge(sem("agg_ready"), b * BT + t - 3)
                act.wait_ge(sem("oh_ready"), b * BT + t + 1)
                A.activation(OH[:, (t + 2 * q) % 4, :], OHb[:, q, t, :], ACT.Copy).then_inc(sem("wide_ready"), 1)

            def chain_isl(b):
                A.activation(isl4, lastE[:, bass.ds(b * BT, BT)].unsqueeze(1).to_broadcast([P, H, BT]),
                             ACT.Copy, scale=-BIG).then_inc(sem("isl_ready"), 1)

            def chain_resets(b):
                A.activation(resF[:, :, 1:], thruF[:, bass.ds(b * BT, BT)].unsqueeze(1).to_broadcast([1, H, BT]), ACT.Copy)
                A.activation(resB[:, :, 0:BT - 1], thruB[:, bass.ds(b * BT, BT - 1)].unsqueeze(1).to_broadcast([1, H, BT - 1]), ACT.Copy)
                A.activation(rowF[:, :, 0:1], CF[:, :, BT:], ACT.Copy).then_inc(sem("rres_ready"), 1)

            def chain_rb(b):
                act.wait_ge(sem("rT_ready"), b + 1)
                A.activation(rb[:, 1:P + 1], rT_ps, ACT.Copy).then_inc(sem("rb_ready"), 1)

            def chain_exp(b, first=False):
                act.wait_ge(sem("df_ready"), b + 1)
                if not first:
                    act.wait_ge(sem("msg_ready"), 4 * b)
                A.activation(WT, DF, ACT.Exp).then_inc(sem("wt_ready"), 1)
                act.wait_ge(sem("ru_ready"), b + 1)
                A.activation(ru[:, 4, :], ru[:, 3, :], ACT.Exp).then_inc(sem("f_ready"), 1)

            act.wait_ge(sem("rb_init"), 2)
            for t in range(BT):
                turn_out(0, t, True)
            chain_isl(0)
            chain_resets(0)
            chain_rb(0)
            for t in range(BT):
                turn_out(1, t)
            chain_exp(0, True)

            def batch(b, q, ahead2=True, ahead1=True, first=False):
                widen(b, q, 0, first)
                widen(b, q, 1, first)
                for t in range(BT):
                    if t < BT - 2:
                        widen(b, q, t + 2, first)
                    if ahead2:
                        turn_out(b + 2, t)
                    if ahead1 and t == 1:
                        act.wait_ge(sem("vT_ready"), b + 1)
                        chain_isl(b + 1)
                    if ahead1 and t == 2:
                        act.wait_ge(sem("cin_ready"), b + 1)
                        chain_resets(b + 1)
                    if ahead1 and t == 3:
                        chain_rb(b + 1)
                    if ahead1 and t == 19:
                        chain_exp(b + 1)
            batch(0, 0, first=True)
            batch(1, 1)
            with act.Fori(1, NB // 2 - 1) as i:
                for q in range(2):
                    batch(2 * i + q, q)
            batch(NB - 2, 0, ahead2=False)
            batch(NB - 1, 1, ahead2=False, ahead1=False)

            def split(c, j):
                n, pq = c * NC + j, PSB[2 + (c * NC + j) % 6]
                if j == 0 and c >= 2:
                    act.wait_ge(sem(f"p_out{c % 2}"), 16 * (c // 2))
                act.wait_ge(sem("pq_ps"), n + 1)
                A.activation(Pst[:, c % 2, j, 0, :], pq[:, 0:HID], ACT.Copy)
                A.activation(Qt[:, n, 0, :], pq[:, HID:], ACT.Copy).then_inc(sem("hi_ready"), 1)
                act.wait_ge(sem("res_ready"), n + 1)
                A.activation(Pst[:, c % 2, j, 1, :], res[:, n % 2, 0, :], ACT.Copy)
                A.activation(Qt[:, n, 1, :], res[:, n % 2, 1, :], ACT.Copy).then_inc(sem("mid_ready"), 1)

            for c in range(NCH + 1):
                for j in range(NC):
                    if c:
                        split(c - 1, j)
                    if c < NCH and j == NC - 2:
                        act.wait_ge(sem("t_cent"), c + 1)
                        A.activation(sqm, t1, ACT.Square).then_inc(sem("sqm_ready"), 1)
                        act.wait_ge(sem("v_sum"), c + 1)
                        A.activation(m7, v7, ACT.Sqrt, bias=eps, scale=1.0 / D).then_inc(sem("s_ready"), 1)
                if c < NCH:
                    act.wait_ge(sem("h2T_ps"), c + 1)
                    if c:
                        act.wait_ge(sem("pq_ps"), c * NC)
                    A.activation(flat(h2T[:, 0:4, :]), PSB[0][:], ACT.Copy)
                    A.activation(flat(h2T[:, 4:NC, :]), PSB[1][:, 0:(NC - 4) * P], ACT.Copy).then_inc(sem("h2T_ready"), 1)

            def turn_outb(b, t, first):
                g = b * BT + t
                act.wait_ge(sem("bT_ps"), g + 1)
                if not (first and t < 2):
                    act.wait_ge(sem("main_done"), g - 1)
                A.activation(ohTb[:, t % 2, :], PSB[t % 2][:].bitcast(BF16)[:, 0:2 * P], ACT.Copy).then_inc(sem("bT_ready"), 1)

            def rows_out(b, q, t):
                act.wait_ge(sem("main_done"), b * BT + t + 1)
                A.activation(Rb[:, q, t, 0:HID], PSB[2 + t % 2][:, 0:HID], ACT.Copy).then_inc(sem("r_out"), 1)

            def targets(i, q, first=False):
                b = 2 * i + q
                turn_outb(b, 0, first and q == 0)
                if not first:
                    act.wait_ge(sem(f"scat{q}"), 16 * BT * i)
                if not (first and q == 0):
                    act.wait_ge(sem("total_ps"), b)
                act.wait_ge(sem("c26_ps"), b + 1)
                A.activation(cnt26, PSB[7][0:BT, 0:NT], ACT.Copy).then_inc(sem("c26_ready"), 1)
                for t in range(BT):
                    if t < BT - 1:
                        turn_outb(b, t + 1, first and q == 0)
                    rows_out(b, q, t)
            targets(0, 0, True)
            targets(0, 1, True)
            with act.Fori(1, NB // 2) as i:
                for q in range(2):
                    targets(i, q)

            def turn_outp(g, m, first):
                act.wait_ge(sem("pT_ps"), g + 1)
                if not (first and m < 2):
                    act.wait_ge(sem("pp_ps"), g - 1)
                A.activation(flat(ohTp[:, m % 2, :, :]), PSB[m % 2][:].bitcast(BF16)[:, 0:PR * P], ACT.Copy).then_inc(sem("pT_ready"), 1)

            def relu(g, m, first):
                act.wait_ge(sem("hp_ready"), g + 1)
                if not (first and m < 2):
                    act.wait_ge(sem("seg_ps"), g - 1)
                A.activation(hid[:, m % 2, :, 0:HID], hp[:, m % 2, :, :], ACT.Relu).then_inc(sem("hid_ready"), 1)

            def sources(i, first=False):
                for m in range(SB):
                    turn_outp(SB * i + m, m, first)
                    if not (first and m < 2):
                        relu(SB * i + m - 2, (m - 2) % SB, first)
            sources(0, True)
            with act.Fori(1, NTURN) as i:
                sources(i)
            relu(NPAIR - 2, SB - 2, False)
            relu(NPAIR - 1, SB - 1, False)
            for c in range(NCH):
                if c:
                    act.wait_ge(sem("sT_ps"), c)
                else:
                    act.wait_ge(sem("accB_done"), NPAIR + 1)
                A.activation(stg, accB[:, c * NC:(c + 1) * NC, 0:HID], ACT.Copy).then_inc(sem("stg_ready"), 1)
                act.wait_ge(sem("sT_ps"), c + 1)
                if c:
                    act.wait_ge(sem("fo_ps"), c)
                for m in range(4):
                    n = min(2, NC - 2 * m)
                    last = A.activation(flat(sT[:, 2 * m:2 * m + n, :]), PSB[m][:, 0:n * HID], ACT.Copy)
                last.then_inc(sem("sT_ready"), 1)

        @block.vector
        def _(dve):
            V = nc.vector
            k = [0]

            def link(ins):
                k[0] += 1
                ins.then_inc(sem("dve_prep"), 1)
                dve.wait_ge(sem("dve_prep"), k[0])

            link(V.memset(hm, 0.0))
            for h in range(H):
                V.memset(hm[h * DH:(h + 1) * DH, h:h + 1], 1.0)
            V.memset(srcE[:, T:], -1.0)
            V.memset(dE[:, T:], -1.0)
            V.memset(nE[:, T:], -1.0)
            dve.wait_ge(sem("e_in"), 16 * 9)
            V.tensor_copy(rF, rI).then_inc(sem("rF_ready"), 1)
            dve.wait_ge(sem("x_in"), 32)
            link(V.tensor_reduce(mean, xs, AX.X, ALU.add))
            link(V.tensor_scalar(rstd, mean, 1.0 / D, None, ALU.mult))
            dve.wait_ge(sem("x_out"), 16)
            V.tensor_tensor(xs, xs, rstd.unsqueeze(2).to_broadcast([P, NT, D]), ALU.subtract).then_inc(sem("xc_ready"), 1)
            for g in range(NG):
                dve.wait_ge(sem("eT_ps"), g + 1)
                v = PSB[2 + g % 2][:, 0:3 * TG].rearrange("p (a t) -> p a t", a=3)
                V.tensor_copy(srcE[:, g * TG:(g + 1) * TG], v[:, 0, :])
                V.tensor_copy(dE[:, g * TG:(g + 1) * TG], v[:, 1, :])
                V.tensor_copy(nE[:, g * TG:(g + 1) * TG], v[:, 2, :]).then_inc(sem("eT_used"), 1)
            dve.wait_ge(sem("sq_ready"), 1)
            V.tensor_reduce(mean, sq, AX.X, ALU.add).then_inc(sem("var_ready"), 1)
            dve.wait_ge(sem("w_in"), 48)
            dve.wait_ge(sem("c0"), 9)
            V.tensor_scalar(attb[:, 0:H], hm, att[:, 0:1], None, ALU.mult)
            V.tensor_scalar(attb[:, H:], hm, att[:, 1:2], None, ALU.mult).then_inc(sem("attb_ready"), 1)
            dve.wait_ge(sem("wx_ps"), 1)
            V.tensor_copy(wx, PSB[4][:, 0:XC]).then_inc(sem("wx_ready"), 1)
            dve.wait_ge(sem("std_ready"), 1)
            link(V.reciprocal(mean, rstd))

            def chunk(c, first=False):
                if not first:
                    dve.wait_ge(sem("hT_ps"), c)
                V.scalar_tensor_tensor(hc, xs[:, bass.ds(c * NC, NC), :], 0.0,
                                       mean[:, bass.ds(c * NC, NC)].unsqueeze(2).to_broadcast([P, NC, D]),
                                       ALU.max, ALU.mult).then_inc(sem("hc_ready"), 1)
                dve.wait_ge(sem("hx_ps"), c + 1)
                if not first:
                    dve.wait_ge(sem("hx_used"), c)
                    dve.wait_ge(sem("h_out"), 16 * c)
                V.tensor_copy(hx[:, 0:3, :], PSB[5][:, 0:3 * XC].rearrange("p (j f) -> p j f", j=3))
                V.tensor_copy(hx[:, 3:6, :], PSB[6][:, 0:3 * XC].rearrange("p (j f) -> p j f", j=3))
                V.tensor_copy(hx[:, 6, :], PSB[7][:, 0:XC]).then_inc(sem("hx_ready"), 1)
            chunk(0, True)
            with dve.Fori(1, NCH) as c:
                chunk(c)

            link(V.tensor_tensor(tmpr, nE, dE, ALU.not_equal))
            V.tensor_copy(lastE, tmpr).then_inc(sem("last_ready"), 1)
            link(V.tensor_copy(isrc, srcE))
            link(V.tensor_scalar(isrc, isrc, 7, None, ALU.arith_shift_right))
            link(V.tensor_copy(hiE, isrc))
            for j, (lo, hi) in enumerate(chunks):
                dve.wait_ge(sem("rows_ps"), 2 * j + 2)
                V.tensor_copy(lastr[:, lo:hi], PSB[2][0:1, 0:hi - lo])
                V.tensor_copy(lflag[:, lo:hi], PSB[3][0:1, 0:hi - lo]).then_inc(sem("rows_used"), 1)
            dve.wait_ge(sem("rows_used"), len(chunks))
            V.memset(contN[:, 0:1], -BIG)
            V.tensor_scalar(contN[:, 1:], lflag[:, 0:TP - 1], -BIG, None, ALU.mult).then_inc(sem("cont_ready"), 1)
            dve.wait_ge(sem("cont_ready"), 1)
            link(V.tensor_tensor(lflag, dE[0:1, :], lastr, ALU.not_equal))
            link(V.tensor_scalar(lflag, lflag, -BIG, None, ALU.mult))
            V.tensor_tensor(thruF, contN, lflag, ALU.min)
            V.tensor_tensor(thruB[:, 0:TP - 1], contN[:, 1:], lflag[:, 0:TP - 1], ALU.min)
            ir = irow[0:1, :]
            link(V.tensor_copy(ir, dE[0:1, :]))
            link(V.tensor_scalar(ir, ir, 7, None, ALU.arith_shift_right))
            link(V.tensor_scalar(ir, ir, 0, None, ALU.max))
            V.tensor_copy(bin_row.rearrange("p (b t) -> p b t", t=RB)[:, :, 0:BT],
                          ir.rearrange("p (b t) -> p b t", t=BT)).then_inc(sem("bins_ready"), 1)
            V.tensor_scalar(tmpr[0:1, :], ir, float(P), None, ALU.mult).then_inc(sem("binf_ready"), 1)
            for j, (lo, hi) in enumerate(chunks):
                dve.wait_ge(sem("cols_ps"), j + 1)
                V.tensor_tensor(dBE[:, lo:hi], dE[:, lo:hi], PSB[4][:, 0:hi - lo], ALU.subtract)
                V.tensor_tensor(s1E[:, lo:hi], dE[:, lo:hi], PSB[5][:, 0:hi - lo], ALU.not_equal)
                V.tensor_tensor(s2E[:, lo:hi], dE[:, lo:hi], PSB[6][:, 0:hi - lo], ALU.not_equal).then_inc(sem("cols_used"), 1)
            dve.wait_ge(sem("cols_used"), len(chunks))
            V.tensor_scalar(s1E, s1E, -BIG, None, ALU.mult)
            link(V.tensor_scalar(s2E, s2E, -BIG, None, ALU.mult))

            def in_bin(c, first=False):
                for j in range(NC):
                    if not first:
                        dve.wait_ge(sem("counted"), (c - 1) * NC + j + 1)
                    V.tensor_scalar(inbin[:, j, 0:TP], hiE, iota[:, bass.ds(c * NC + j, 1)], None, ALU.is_equal).then_inc(sem("in_bin"), 1)
            V.memset(inbin[:, :, TP:], 0.0)
            in_bin(0, True)
            with dve.Fori(1, NCH) as c:
                in_bin(c)
            dve.wait_ge(sem("counted"), NT)
            V.tensor_copy(cntT, PSB[5][:, 0:NT]).then_inc(sem("cntT_ready"), 1)
            dve.wait_ge(sem("cnt_ps"), 1)
            link(V.tensor_copy(cnt[:, 1, :], PSB[6][:, 0:NT]))
            link(V.tensor_scalar(cnt[:, 2, :], cnt[:, 1, :], float(GR - 1), None, ALU.add))
            link(V.tensor_copy(cnti[:, 0, :], cnt[:, 2, :]))
            link(V.tensor_scalar(cnti[:, 1, :], cnti[:, 0, :], 8, None, ALU.arith_shift_right))
            link(V.tensor_copy(cnt[:, 3, :], cnti[:, 1, :]))
            link(V.tensor_scalar(cnt[:, 4, :], cnt[:, 3, :], float(GR), None, ALU.mult))
            link(V.memset(cnt[:, 5, :], 1.0))
            link(V.tensor_tensor_scan(cnt[:, 6, :], cnt[:, 5, :], cnt[:, 4, :], 0.0, ALU.mult, ALU.add))
            link(V.tensor_tensor(run0, cnt[:, 6, :], cnt[:, 4, :], ALU.subtract))
            link(V.tensor_tensor(cnt[:, 7, :], run0, cnt[:, 1, :], ALU.add))
            V.tensor_copy(rend, cnt[0:1, 7, :]).then_inc(sem("rend_ready"), 1)
            dve.wait_ge(sem("k256_ready"), 1)
            link(V.tensor_tensor(pbc, cnt[:, 6, :].unsqueeze(1).to_broadcast([P, PBJ, NT]),
                                 k256.unsqueeze(2).to_broadcast([P, PBJ, NT]), ALU.is_le))
            link(V.tensor_reduce(pbf, pbc, AX.X, ALU.add))
            link(V.tensor_scalar(pbf, pbf, float(NT - 1), None, ALU.min))
            V.tensor_copy(pbi, pbf).then_inc(sem("pbi_ready"), 1)

            dve.wait_ge(sem("pb_out"), 16)
            V.memset(rb, -BIG).then_inc(sem("rb_init"), 1)
            V.memset(resF, -BIG)
            V.memset(resB, -BIG)
            V.memset(CF, -BIG)
            V.memset(cin, -BIG).then_inc(sem("rb_init"), 1)
            dve.wait_ge(sem("rb_init"), 2)
            dve.wait_ge(sem("hx_used"), NCH)
            dve.wait_ge(sem("aT0"), 1)
            link(V.tensor_copy(aT3[:, :, 0, :], aT))
            link(V.tensor_tensor(aRes, aT, aT3[:, :, 0, :], ALU.subtract))
            link(V.tensor_copy(aT3[:, :, 1, :], aRes))
            V.tensor_tensor(aT3[:, :, 2, :], aRes, aT3[:, :, 1, :], ALU.subtract).then_inc(sem("aT3_ready"), 1)

            def indices(b, s):
                V.tensor_scalar(idx[:, s, :], srcE[:, bass.ds(b * BT, BT)], 0.0, None, ALU.max).then_inc(sem("idx_ready"), 1)

            def hot(b, s, t, first=False):
                if not first:
                    dve.wait_ge(sem("wide_ready"), (b - 2) * BT + t + 1)
                V.tensor_scalar(OHb[:, s, t, :], iotab, dBE[:, bass.ds(b * BT + t, 1)], None, ALU.is_equal).then_inc(sem("oh_ready"), 1)

            def logits(b, q, half):
                dve.wait_ge(sem("expanded"), b * BT + (half + 1) * (BT // 2))
                V.tensor_reduce(abS[:, q, half * (BT // 2):(half + 1) * (BT // 2), :], ab_ps[half].rearrange("p t s c -> p t c s"),
                                AX.X, ALU.add).then_inc(sem("ab_out"), 1)

            def chain(b, q, step, i):
                n, B = b + 1, b * BT
                row = lambda v: v[:, bass.ds(B, BT)].unsqueeze(1).to_broadcast([1, H, BT])
                col = lambda v: v[:, bass.ds(B, BT)].unsqueeze(1).to_broadcast([P, H, BT])
                as4 = abS[:, q, :, 0:H].rearrange("p t h -> p h t")
                ad4 = abS[:, q, :, H:].rearrange("p t h -> p h t")
                if step == "logits":
                    g4 = G[:, q, :, D:GW].rearrange("p t h -> p h t")
                    dve.wait_ge(sem(f"gath{q}"), 16 * BT * (i + 1))
                    dve.wait_ge(sem("ab_out"), 2 * n)
                    V.tensor_tensor(vE, g4, as4, ALU.max).then_inc(sem("v_ready"), 1)
                    V.tensor_tensor(ZZ[:, 0, :, :], g4, ad4, ALU.add)
                    V.tensor_tensor(ZZ[:, 1, :, :], as4, ad4, ALU.add)
                elif step == "forward":
                    dve.wait_ge(sem("vT_ready"), n)
                    dve.wait_ge(sem("rb_ready"), n)
                    V.tensor_tensor_scan(FT, rb[:, 0:P], vT_ps, -BIG, ALU.add, ALU.max).then_inc(sem("ft_ready"), 1)
                elif step == "backward":
                    dve.wait_ge(sem("ft_ready"), n)
                    V.tensor_tensor_scan(BK[:, ::-1], rb[:, 1:P + 1][:, ::-1], FT[:, ::-1], -BIG, ALU.add, ALU.max).then_inc(sem("bk_ready"), 1)
                elif step == "ends":
                    dve.wait_ge(sem("rows_ready"), n)
                    dve.wait_ge(sem("rres_ready"), n)
                    V.tensor_copy(rowF[:, :, 1:], rows_ps[:, 0:H * BT].rearrange("p (h t) -> p h t", h=H))
                    V.tensor_copy(rowB, rows_ps[:, H * BT:].rearrange("p (h t) -> p h t", h=H)).then_inc(sem("row_ready"), 1)
                elif step == "carries":
                    dve.wait_ge(sem("row_ready"), n)
                    V.tensor_tensor_scan(flat(CF), flat(resF), flat(rowF), -BIG, ALU.add, ALU.max)
                    V.tensor_tensor_scan(flat(CB)[:, ::-1], flat(resB)[:, ::-1], flat(rowB)[:, ::-1], -BIG, ALU.add, ALU.max).then_inc(sem("carry_ready"), 1)
                elif step == "come in":
                    dve.wait_ge(sem("carry_ready"), n)
                    V.tensor_tensor(cin[:, 0, :, :], CF[:, :, 0:BT], row(contN), ALU.add)
                    V.tensor_tensor(cin[:, 1, :, 0:BT - 1], CB[:, :, 1:],
                                    contN[:, bass.ds(B + 1, BT - 1)].unsqueeze(1).to_broadcast([1, H, BT - 1]), ALU.add).then_inc(sem("cin_ready"), 1)
                elif step == "masked":
                    dve.wait_ge(sem("bc_ready"), n)
                    V.tensor_tensor(y12[:, 0, :, :], bc_ps[:, 0, :, :], col(s1E), ALU.add)
                    V.tensor_tensor(y12[:, 1, :, :], bc_ps[:, 1, :, :], col(s2E), ALU.add).then_inc(sem("y_ready"), 1)
                elif step == "carried":
                    dve.wait_ge(sem("y_ready"), n)
                    V.tensor_tensor(ym, y12[:, 0, :, :], y12[:, 1, :, :], ALU.max).then_inc(sem("ym_ready"), 1)
                elif step == "maximum":
                    dve.wait_ge(sem("ym_ready"), n)
                    V.tensor_tensor(R, ym, BE_ps, ALU.max).then_inc(sem("R_ready"), 1)
                elif step == "sums":
                    dve.wait_ge(sem("R_ready"), n)
                    V.tensor_tensor(ZZ[:, 2, :, :], R, ad4, ALU.add).then_inc(sem("Z_ready"), 1)
                    V.tensor_tensor(ru[:, 0, :], cin[:, 0, :, 0], abS[0:1, q, 0, H:], ALU.add).then_inc(sem("r_step"), 1)
                elif step == "leaky":
                    dve.wait_ge(sem("Z_ready"), n)
                    V.scalar_tensor_tensor(flat(LL), flat(ZZ), SLOPE, flat(ZZ), ALU.mult, ALU.max).then_inc(sem("L_ready"), 1)
                    dve.wait_ge(sem("r_step"), 4 * b + 1)
                    V.scalar_tensor_tensor(ru[:, 1, :], ru[:, 0, :], SLOPE, ru[:, 0, :], ALU.mult, ALU.max).then_inc(sem("r_step"), 1)
                elif step == "differences":
                    dve.wait_ge(sem("L_ready"), n)
                    V.tensor_tensor(DF, LL[:, 0:2, :, :], LL[:, 2, :, :].unsqueeze(1).to_broadcast([P, 2, H, BT]), ALU.subtract).then_inc(sem("df_ready"), 1)
                    dve.wait_ge(sem("r_step"), 4 * b + 2)
                    V.tensor_tensor(ru[:, 2, :], ru[:, 1, :], LL[0:1, 2, :, 0], ALU.subtract).then_inc(sem("r_step"), 1)
                elif step == "floor":
                    dve.wait_ge(sem("r_step"), 4 * b + 3)
                    V.tensor_scalar(ru[:, 3, :], ru[:, 2, :], -1e4, None, ALU.max).then_inc(sem("ru_ready"), 1)

            STEPS = {4: "logits", 6: "forward", 7: "backward", 9: "ends", 10: "carries", 11: "come in", 13: "masked",
                     14: "carried", 15: "maximum", 16: "sums", 17: "leaky", 18: "differences", 19: "floor"}
            wt = WT.rearrange("p s h t -> p s t h")

            def messages(b, q, m):
                lo, hi = PIECES[m]
                V.tensor_copy(msg[:, lo:hi, :, DH], wt[:, 0, lo:hi, :])
                V.tensor_tensor(msg[:, lo:hi, :, DH + 1], wt[:, 1, lo:hi, :],
                                lastE[:, bass.ds(b * BT + lo, hi - lo)].unsqueeze(2).to_broadcast([P, hi - lo, H]), ALU.mult)
                V.tensor_tensor(msg[:, lo:hi, :, 0:DH], G[:, q, lo:hi, 0:D].rearrange("p t (h o) -> p t h o", h=H),
                                wt[:, 0, lo:hi, :].unsqueeze(3).to_broadcast([P, hi - lo, H, DH]), ALU.mult).then_inc(sem("msg_ready"), 1)

            def factor(b):
                dve.wait_ge(sem("f_ready"), b + 1)
                V.tensor_scalar(ru[:, 2, :], ru[:, 4, :], -1.0, None, ALU.add).then_inc(sem("g_ready"), 1)

            def add_up(b, t, regs):
                dve.wait_ge(sem("agg_ready"), b * BT + t + 1)
                dve.wait_ge(sem("acc_done"), b * (BT + 1) + 2 + t)
                a = flat(acc[:, bass.ds(regs[t], 2), :])
                V.tensor_tensor(a, a, PSB[3 + t % 2][:, 0:2 * H * MW], ALU.add).then_inc(sem("acc_done"), 1)

            def batch(i, q, ahead3=True, ahead2=True, ahead1=True):
                b, n = 2 * i + q, 2 * i + q + 1
                regs = bins(ENG.DVE, b, BT)
                for t in range(BT):
                    if ahead2:
                        hot(b + 2, q, t)
                    if t == 0:
                        dve.wait_ge(sem("fac_ps"), n)
                        V.tensor_scalar(fac, fac_ps, 1.0, None, ALU.add).then_inc(sem("r_step"), 1)
                    if t == 1:
                        dve.wait_ge(sem("r_step"), 4 * b + 4)
                        dve.wait_ge(sem("acc_done"), b * (BT + 1) + 1)
                        a = acc[:, bass.ds(regs[0], 1), :].rearrange("p a (h m) -> p (a h) m", h=H)
                        V.tensor_tensor(a, a, fac.unsqueeze(2).to_broadcast([P, H, MW]), ALU.mult).then_inc(sem("acc_done"), 1)
                        if ahead1:
                            logits(b + 1, 1 - q, 1)
                    if t >= 2:
                        add_up(b, t - 2, regs)
                    if t in (3, 8):
                        messages(b, q, 2 if t == 3 else 3)
                    if ahead1 and t in STEPS:
                        chain(b + 1, 1 - q, STEPS[t], i + q)
                    if ahead2 and t == 15:
                        logits(b + 2, q, 0)
                    if ahead1 and t == 21:
                        if ahead3:
                            indices(b + 3, 1 - q)
                        dve.wait_ge(sem("wt_ready"), n + 1)
                        messages(b + 1, 1 - q, 0)
                    if ahead1 and t == 23:
                        factor(b + 1)
                        messages(b + 1, 1 - q, 1)
                add_up(b, BT - 2, regs)
                add_up(b, BT - 1, regs)

            indices(0, 0)
            indices(1, 1)
            for t in range(BT):
                hot(0, 0, t, True)
            logits(0, 0, 0)
            logits(0, 0, 1)
            for t in range(BT):
                hot(1, 1, t, True)
            logits(1, 1, 0)
            for t in sorted(STEPS):
                chain(0, 0, STEPS[t], 0)
            indices(2, 0)
            dve.wait_ge(sem("wt_ready"), 1)
            messages(0, 0, 0)
            factor(0)
            messages(0, 0, 1)
            batch(0, 0)
            batch(0, 1)
            with dve.Fori(1, NB // 2 - 2) as i:
                for q in range(2):
                    batch(i, q)
            batch(NB // 2 - 2, 0)
            batch(NB // 2 - 2, 1, ahead3=False)
            batch(NB // 2 - 1, 0, ahead3=False, ahead2=False)
            batch(NB // 2 - 1, 1, ahead3=False, ahead2=False, ahead1=False)

            V.memset(Qt[:, NT, :, :], 0.0)
            dve.wait_ge(sem("w1_in"), 16 * 8)
            dve.wait_ge(sem("filled"), 16 * (NFILL + NT))
            hv = lambda v: v.rearrange("p n (h o) -> p n h o", h=H)
            wide = lambda v: v.unsqueeze(3).to_broadcast([P, NC, H, DH])

            def node_step(c, step):
                a = acc[:, c * NC:(c + 1) * NC, :].rearrange("p n (h m) -> p n h m", h=H)
                if step == 0:
                    link(V.tensor_tensor(den, a[:, :, :, DH], a[:, :, :, DH + 1], ALU.add))
                    link(V.tensor_scalar(den, den, 1e-30, None, ALU.max))
                    V.reciprocal(rec, den)
                elif step == 1:
                    dve.wait_ge(sem(f"hs_in{c % 2}"), 32 * (c // 2 + 1))
                    link(V.tensor_tensor(hv(t1), hv(hs[:, c % 2, :, :]), wide(a[:, :, :, DH + 1]), ALU.mult))
                    link(V.tensor_tensor(hv(t1), hv(t1), a[:, :, :, 0:DH], ALU.add))
                elif step == 2:
                    link(V.tensor_tensor(hv(t1), hv(t1), wide(rec), ALU.mult))
                    link(V.tensor_tensor(t1, t1, biasB.unsqueeze(1).to_broadcast([P, NC, D]), ALU.add))
                elif step == 3:
                    if c:
                        dve.wait_ge(sem("x1_out"), 16 * c)
                    V.tensor_tensor(x1c, t1, xi[:, c % 2, :, :], ALU.add).then_inc(sem("x1_ready"), 1)
                    dve.wait_ge(sem("x1_ready"), c + 1)
                    link(V.tensor_reduce(v7, x1c, AX.X, ALU.add))
                elif step == 4:
                    link(V.tensor_scalar(v7, v7, 1.0 / D, None, ALU.mult))
                    V.tensor_tensor(t1, x1c, v7.unsqueeze(2).to_broadcast([P, NC, D]), ALU.subtract).then_inc(sem("t_cent"), 1)
                elif step == 5:
                    dve.wait_ge(sem("sqm_ready"), c + 1)
                    V.tensor_reduce(v7, sqm, AX.X, ALU.add).then_inc(sem("v_sum"), 1)
                else:
                    dve.wait_ge(sem("s_ready"), c + 1)
                    link(V.reciprocal(v7, m7))
                    if c:
                        dve.wait_ge(sem("h2T_ps"), c)
                    V.scalar_tensor_tensor(h2, t1, 0.0, v7.unsqueeze(2).to_broadcast([P, NC, D]), ALU.max, ALU.mult).then_inc(sem("h2_ready"), 1)

            for c in range(NCH + 1):
                for j in range(NC):
                    n, pq = (c - 1) * NC + j, PSB[2 + ((c - 1) * NC + j) % 6]
                    if c:
                        dve.wait_ge(sem("hi_ready"), n + 1)
                        V.tensor_tensor(res[:, n % 2, 0, :], pq[:, 0:HID], Pst[:, (c - 1) % 2, j, 0, :], ALU.subtract)
                        V.tensor_tensor(res[:, n % 2, 1, :], pq[:, HID:], Qt[:, n, 0, :], ALU.subtract).then_inc(sem("res_ready"), 1)
                    if c < NCH:
                        node_step(c, j)
                    if c:
                        dve.wait_ge(sem("mid_ready"), n + 1)
                        V.tensor_tensor(Pst[:, (c - 1) % 2, j, 2, :], res[:, n % 2, 0, :], Pst[:, (c - 1) % 2, j, 1, :], ALU.subtract)
                        V.tensor_tensor(Qt[:, n, 2, :], res[:, n % 2, 1, :], Qt[:, n, 1, :], ALU.subtract
                                        ).then_inc(sem("split_done" if j == NC - 1 else "lo_ready"), 1)

            dve.wait_ge(sem("p_out0"), 16 * ((NCH + 1) // 2))
            dve.wait_ge(sem("p_out1"), 16 * (NCH // 2))

            def targets(i, q, first=False):
                b, n = 2 * i + q, 2 * i + q + 1
                B = b * BT
                hi = hiE[:, bass.ds(B, BT)]
                V.tensor_tensor(oh49[:, q, :, :], hi.unsqueeze(2).to_broadcast([P, BT, NT]),
                                iota49.unsqueeze(1).to_broadcast([P, BT, NT]), ALU.is_equal).then_inc(sem("b49_ready"), 1)
                if not (first and q == 0):
                    dve.wait_ge(sem("pos_ready"), b)
                    dve.wait_ge(sem("run_ready"), b)
                V.tensor_scalar(padf, hi, 0.0, dump, ALU.is_lt, ALU.mult)
                if not first:
                    dve.wait_ge(sem(f"scat{q}"), 16 * BT * i)
                V.scalar_tensor_tensor(Rb[:, q, :, HID], hi, -float(P), srcE[:, bass.ds(B, BT)], ALU.mult, ALU.add)

                def hotb(t):
                    g = B + t
                    if not (first and q == 0 and t < 4):
                        dve.wait_ge(sem("bT_ps"), g - 3)
                    V.tensor_scalar(OHr[:, (t + 2 * q) % 4, :], iotab, dBE[:, bass.ds(g, 1)], None, ALU.is_equal).then_inc(sem("ohb_ready"), 1)

                def ea_out(j):
                    Gp = b * (BT // 2) + j
                    dve.wait_ge(sem("eaT_ps"), Gp + 1)
                    if not (first and q == 0 and j < 2):
                        dve.wait_ge(sem("main_done"), 2 * Gp - 2)
                    V.tensor_copy(EAT[:, (j + q) % 2, :], PSB[4][:, 0:P]).then_inc(sem("ea_out"), 1)

                def rank(m):
                    lo, hi_ = m * RK, min((m + 1) * RK, BT)
                    dve.wait_ge(sem("rk_ps"), 3 * b + m + 1)
                    V.tensor_tensor(t49[:, lo:hi_, :], PSB[5 + m % 2][:, 0:(hi_ - lo) * NT].rearrange("p (t b) -> p t b", b=NT),
                                    run0.unsqueeze(1).to_broadcast([P, hi_ - lo, NT]), ALU.add).then_inc(sem("rk_used"), 1)

                def own(m):
                    lo, hi_ = m * RK, min((m + 1) * RK, BT)
                    dve.wait_ge(sem("rk_used"), 3 * b + m + 1)
                    V.tensor_tensor(t49[:, lo:hi_, :], t49[:, lo:hi_, :], oh49[:, q, lo:hi_, :], ALU.mult).then_inc(sem("own_ready"), 1)
                hotb(0)
                hotb(1)
                for t in range(BT):
                    if t % 2 == 0:
                        ea_out(t // 2)
                    if t < BT - 2:
                        hotb(t + 2)
                    if t in (4, 7, 11):
                        rank({4: 0, 7: 1, 11: 2}[t])
                    if t in (5, 8, 12):
                        own({5: 0, 8: 1, 12: 2}[t])
                    if t == 13:
                        dve.wait_ge(sem("total_ps"), n)
                        V.tensor_tensor(run0, run0, PSB[7][:, 64:64 + NT], ALU.add).then_inc(sem("run_ready"), 1)
                    if t == 14:
                        dve.wait_ge(sem("own_ready"), 3 * n)
                        V.tensor_reduce(posf, t49, AX.X, ALU.add).then_inc(sem("posf_ready"), 1)
                    if t == 16:
                        dve.wait_ge(sem("posf_ready"), n)
                        V.tensor_tensor(pos[:, q, :], posf, padf, ALU.add).then_inc(sem("pos_ready"), 1)
            targets(0, 0, True)
            targets(0, 1, True)
            with dve.Fori(1, NB // 2) as i:
                for q in range(2):
                    targets(i, q)

            for q in range(2):
                dve.wait_ge(sem(f"scat{q}"), 16 * BT * (NB // 2))
            V.memset(pbrow, 0).then_inc(sem("pbz"), 1)
            V.memset(hid[:, :, :, HID:], 1.0)
            V.memset(accB[:, 0:NT // 2, :], 0.0).then_inc(sem("accB_done"), 1)
            dve.wait_ge(sem("accB_done"), 1)
            dve.wait_ge(sem("accB_low"), 1)
            dve.wait_ge(sem("pb_in"), 16)

            def hotp(i, m, first):
                s, k, g = m // CP, m % CP, SB * i + m
                if k == 0:
                    dve.wait_ge(sem(f"xr_in{s}"), 16 * (i + 1))
                if not first:
                    dve.wait_ge(sem("seg_ps"), g - SB + 1)
                for j in range(PR):
                    c = j * XW + HID
                    last = V.tensor_scalar(OHp[:, m, j, :], iota[:, 0:P], XR[:, s, k, c:c + 1], None, ALU.is_equal)
                last.then_inc(sem("ohp_ready"), 1)

            def add_r(g, m, first):
                s, k = m // CP, m % CP
                dve.wait_ge(sem("pp_ps"), g + 1)
                if not (first and m < 2):
                    dve.wait_ge(sem("hid_ready"), g - 1)
                V.tensor_tensor(hp[:, m % 2, :, :], PSB[2 + m % 2][:].rearrange("p (j h) -> p j h", j=PR),
                                XR[:, s, k, :].rearrange("p (j w) -> p j w", j=PR)[:, :, 0:HID], ALU.add).then_inc(sem("hp_ready"), 1)

            def add_up(g, m, reg):
                dve.wait_ge(sem("seg_ps"), g + 1)
                dve.wait_ge(sem("accB_done"), g + 1)
                a = flat(accB[:, bass.ds(reg, 1), :])
                V.tensor_tensor(a, a, PSB[4 + m % 2][:, 0:XW], ALU.add).then_inc(sem("accB_done"), 1)

            def sources(i, first=False, last=False):
                regs = pair_bins(ENG.DVE, i)
                for m in range(SB):
                    if m < SB - 1:
                        hotp(i, m + 1, first)
                    else:
                        if not last:
                            hotp(i + 1, 0, False)
                    if not (first and m < 2):
                        add_r(SB * i + m - 2, (m - 2) % SB, first)
                    if not (first and m < 4):
                        add_up(SB * i + m - 4, (m - 4) % SB, regs[m])
            hotp(0, 0, True)
            sources(0, True)
            with dve.Fori(1, NTURN - 1) as i:
                sources(i)
            sources(NTURN - 1, last=True)
            regs = pair_bins(ENG.DVE, NTURN)
            for m in range(SB - 4, SB):
                if m < SB - 2:
                    add_r(NPAIR - SB + m + 2, m + 2, False)
                add_up(NPAIR - SB + m, m, regs[m - SB + 4])
            dve.wait_ge(sem("accB_done"), NPAIR + 1)
            for c in range(NCH):
                if c:
                    dve.wait_ge(sem("fo_ready"), c)
                link(V.tensor_tensor(fo, b2B.unsqueeze(1).to_broadcast([P, NC, D]),
                                     accB[:, c * NC:(c + 1) * NC, HID:].to_broadcast([P, NC, D]), ALU.mult))
                dve.wait_ge(sem("x1_in"), 16 * (c + 1))
                link(V.tensor_tensor(fo, fo, x1b, ALU.add))
                dve.wait_ge(sem("fo_ps"), c + 1)
                if c:
                    dve.wait_ge(sem("stored"), 16 * c)
                V.tensor_tensor(flat(fo2[:, 0:4, :]), flat(fo[:, 0:4, :]), PSB[4][:], ALU.add)
                V.tensor_tensor(flat(fo2[:, 4:NC, :]), flat(fo[:, 4:NC, :]), PSB[5][:, 0:(NC - 4) * D], ALU.add).then_inc(sem("fo_ready"), 1)

        @block.tensor
        def _(pe):
            pe.wait_ge(sem("c0"), 9)
            pe.wait_ge(sem("rF_ready"), 1)
            for g in range(NG):
                if g >= 2:
                    pe.wait_ge(sem("eT_used"), g - 1)
                for a in range(3):
                    last = pe.transpose(PSB[2 + g % 2][:, a * TG:(a + 1) * TG], rF[:, a, g * P:(g + 1) * P], ident[0:TG, 0:TG])
                last.then_inc(sem("eT_ps"), 1)
            pe.wait_ge(sem("w_in"), 48)
            pe.transpose(PSB[4][:, 0:D], w_sb, ident)
            pe.wait_ge(sem("attb_ready"), 1)
            pe.matmul(PSB[4][:, D:XC], w_sb, attb, start=True, stop=True).then_inc(sem("wx_ps"), 1)
            pe.wait_ge(sem("wx_ready"), 1)

            def chunk(c, first=False):
                pe.wait_ge(sem("hc_ready"), c + 1)
                for j in range(NC):
                    last = pe.transpose(PSB[j // 4][:, (j % 4) * P:(j % 4 + 1) * P], hc[:, j, :], ident)
                last.then_inc(sem("hT_ps"), 1)
                pe.wait_ge(sem("hcT_ready"), c + 1)
                if not first:
                    pe.wait_ge(sem("hx_ready"), c)
                for j in range(NC):
                    last = pe.matmul(PSB[5 + j // 3][:, (j % 3) * XC:(j % 3 + 1) * XC], hcT[:, j, :], wx, start=True, stop=True)
                last.then_inc(sem("hx_ps"), 1)
            chunk(0, True)
            with pe.Fori(1, NCH) as c:
                chunk(c)

            last127 = ident[:, P - 1:P]
            pe.wait_ge(sem("last_ready"), 1)
            for j, (lo, hi) in enumerate(chunks):
                if j:
                    pe.wait_ge(sem("rows_used"), j)
                pe.matmul(PSB[2][0:1, 0:hi - lo], last127, dE[:, lo:hi], start=True, stop=True).then_inc(sem("rows_ps"), 1)
                pe.matmul(PSB[3][0:1, 0:hi - lo], last127, tmpr[:, lo:hi], start=True, stop=True).then_inc(sem("rows_ps"), 1)
            pe.wait_ge(sem("binf_ready"), 1)
            for j, (lo, hi) in enumerate(chunks):
                if j:
                    pe.wait_ge(sem("cols_used"), j)
                pe.matmul(PSB[4][:, 0:hi - lo], ones[0:1, :], tmpr[0:1, lo:hi], start=True, stop=True)
                pe.matmul(PSB[5][:, 0:hi - lo], ones[0:1, :], dE[0:1, lo:hi], start=True, stop=True)
                pe.matmul(PSB[6][:, 0:hi - lo], ones[0:1, :], lastr[0:1, lo:hi], start=True, stop=True).then_inc(sem("cols_ps"), 1)
            pe.wait_ge(sem("cols_used"), len(chunks))

            def count(c):
                for j in range(NC):
                    pe.wait_ge(sem("in_bin"), c * NC + j + 1)
                    for r in range(TR):
                        last = pe.matmul(PSB[5][:, bass.ds(c * NC + j, 1)], inbin[:, j, r * P:(r + 1) * P], onesb[:, 0:1],
                                         start=(r == 0), stop=(r == TR - 1))
                    last.then_inc(sem("counted"), 1)
            with pe.Fori(0, NCH) as c:
                count(c)
            pe.wait_ge(sem("cntT_ready"), 1)
            pe.matmul(PSB[6][:, 0:NT], ones, cntT, start=True, stop=True).then_inc(sem("cnt_ps"), 1)

            def turn(b, s, t, first=False):
                pe.wait_ge(sem("oh_ready"), b * BT + t + 1)
                if not (first and t < 2):
                    pe.wait_ge(sem("ohT_ready"), b * BT + t - 1)
                for k in range(2):
                    last = pe.transpose(PSB[t % 2][:].bitcast(BF16)[:, k * P:(k + 1) * P], OHb[:, s, t, k * P:(k + 1) * P], identb)
                last.then_inc(sem("ohT_ps"), 1)

            def expand(b, t, regs, first=False):
                pe.wait_ge(sem("ohT_ready"), b * BT + t + 1)
                half, j = divmod(t, BT // 2)
                if j == 0 and not first:
                    pe.wait_ge(sem("ab_out"), 2 * b - 1 + half)
                for k in range(2):
                    last = pe.matmul(ab_ps[half][:, j, :, :].rearrange("p s c -> p (s c)"), ohT[:, t % 2, k * P:(k + 1) * P],
                                     flat(aT3[:, bass.ds(regs[t] + k, 1), :, :]), start=(k == 0), stop=(k == 1))
                last.then_inc(sem("expanded"), 1)

            HB = H * BT

            def chain_resets(b):
                pe.wait_ge(sem("isl_ready"), b + 1)
                pe.transpose(rT_ps, flat(isl4), ident).then_inc(sem("rT_ready"), 1)

            def chain_v(b):
                pe.wait_ge(sem("rb_ready"), b + 1)
                pe.wait_ge(sem("v_ready"), b + 1)
                pe.transpose(vT_ps, flat(vE), ident).then_inc(sem("vT_ready"), 1)

            def chain_ends(b):
                pe.wait_ge(sem("bk_ready"), b + 1)
                pe.matmul(rows_ps[:, 0:HB], FT[:, P - 1:P], ident[0:HB, 0:HB], start=True, stop=True)
                pe.matmul(rows_ps[:, HB:], BK[:, 0:1], ident[0:HB, 0:HB], start=True, stop=True).then_inc(sem("rows_ready"), 1)
                pe.transpose(flat(BE_ps), BK, ident[0:HB, 0:HB])

            def chain_carry(b):
                pe.wait_ge(sem("cin_ready"), b + 1)
                pe.matmul(flat(bc_ps), ones[0:1, :], flat(cin), start=True, stop=True).then_inc(sem("bc_ready"), 1)

            pe.wait_ge(sem("bins_ready"), 1)
            pe.wait_ge(sem("aT3_ready"), 1)
            pe.wait_ge(sem("hx_used"), NCH)
            regs = bins(ENG.PE, 0, BT)
            for t in range(BT):
                turn(0, 0, t, True)
                expand(0, t, regs, True)
            chain_resets(0)
            regs = bins(ENG.PE, 1, BT)
            for t in range(BT):
                turn(1, 1, t)
                expand(1, t, regs)
            chain_v(0)
            chain_ends(0)
            chain_carry(0)

            def batch(b, q, ahead2=True, ahead1=True, first=False):
                if ahead2:
                    regs = bins(ENG.PE, b + 2, BT)
                pe.wait_ge(sem("g_ready"), b + 1)
                pe.wait_ge(sem("wide_ready"), b * BT + 1)
                pe.matmul(fac_ps, OH[0:1, 2 * q, 0:P], ru[:, 2, :], start=True, stop=True).then_inc(sem("fac_ps"), 1)
                for t in range(BT):
                    if ahead2:
                        turn(b + 2, q, t)
                        if t:
                            expand(b + 2, t - 1, regs)
                    pe.wait_ge(sem("wide_ready"), b * BT + t + 1)
                    pe.wait_ge(sem("msg_ready"), 4 * b + piece(t) + 1)
                    if t >= 2:
                        pe.wait_ge(sem("acc_done"), b * (BT + 1) + t + 1)
                    elif not first:
                        pe.wait_ge(sem("acc_done"), b * (BT + 1) + t)
                    for k in range(2):
                        last = pe.matmul(PSB[3 + t % 2][:, k * H * MW:(k + 1) * H * MW], OH[:, (t + 2 * q) % 4, k * P:(k + 1) * P],
                                         flat(msg[:, t, :, :]), start=True, stop=True)
                    last.then_inc(sem("agg_ready"), 1)
                    if ahead1:
                        for at, step in ((2, chain_resets), (4, chain_v), (7, chain_ends), (11, chain_carry)):
                            if t == at:
                                step(b + 1)
                if ahead2:
                    expand(b + 2, BT - 1, regs)
            batch(0, 0, first=True)
            batch(1, 1)
            with pe.Fori(1, NB // 2 - 1) as i:
                for q in range(2):
                    batch(2 * i + q, q)
            batch(NB - 2, 0, ahead2=False)
            batch(NB - 1, 1, ahead2=False, ahead1=False)

            for c in range(NCH):
                pe.wait_ge(sem("h2_ready"), c + 1)
                for j in range(NC):
                    last = pe.transpose(PSB[j // 4][:, (j % 4) * P:(j % 4 + 1) * P], h2[:, j, :], ident)
                last.then_inc(sem("h2T_ps"), 1)
                pe.wait_ge(sem("h2T_ready"), c + 1)
                for j in range(NC):
                    n = c * NC + j
                    if n >= 6:
                        pe.wait_ge(sem("res_ready"), n - 5)
                    pe.matmul(PSB[2 + n % 6][:], h2T[:, j, :], flat(w1n), start=True, stop=False)
                    pe.matmul(PSB[2 + n % 6][:, 0:HID], ones[0:1, :], b1r, start=False, stop=True).then_inc(sem("pq_ps"), 1)

            def targets(i, q, first=False, final=False):
                b, n = 2 * i + q, 2 * i + q + 1
                B = b * BT
                regs = bins(ENG.PE, b, BT)

                def turn(t):
                    pe.wait_ge(sem("ohb_ready"), B + t + 1)
                    for k in range(2):
                        last = pe.transpose(PSB[t % 2][:].bitcast(BF16)[:, k * P:(k + 1) * P],
                                            OHr[:, (t + 2 * q) % 4, k * P:(k + 1) * P], identb)
                    last.then_inc(sem("bT_ps"), 1)

                def turn_ea(j):
                    if not (first and q == 0 and j == 0):
                        pe.wait_ge(sem("ea_out"), b * (BT // 2) + j)
                    pe.transpose(PSB[4][:, 0:P], flat(EAb[:, q, 2 * j:2 * j + 2, :]), ident).then_inc(sem("eaT_ps"), 1)

                def main(t):
                    g = B + t
                    pe.wait_ge(sem("bT_ready"), g + 1)
                    if not (first and q == 0 and t < 2):
                        pe.wait_ge(sem("r_out"), g - 1)
                    o = PSB[2 + t % 2][:, 0:HID]
                    for k in range(2):
                        for part in range(3):
                            pe.matmul(o, ohTb[:, t % 2, k * P:(k + 1) * P],
                                      flat(Qt[:, bass.ds(regs[t] + k, 1), part, :]), start=(k == 0 and part == 0), stop=False)
                    pe.wait_ge(sem("ea_out"), b * (BT // 2) + t // 2 + 1)
                    h = (t % 2) * DE
                    pe.matmul(o, EAT[h:h + DE, (t // 2 + q) % 2, :], w1e[h:h + DE, :], start=False, stop=True).then_inc(sem("main_done"), 1)

                def rank(m):
                    lo, hi = m * RK, min((m + 1) * RK, BT)
                    if m == 2:
                        pe.wait_ge(sem("rk_used"), 3 * b + 1)
                    elif m == 0 and not (first and q == 0):
                        pe.wait_ge(sem("rk_used"), 3 * b)
                    o = PSB[5 + m % 2]
                    pe.matmul(o[:, 0:(hi - lo) * NT], tri, flat(oh49[:, q, lo:hi, :]), start=True, stop=False)
                    for t in range(lo, hi):
                        last = pe.matmul(o[:, (t - lo) * NT:(t - lo + 1) * NT], tri26[:, t:t + 1].to_broadcast([BT, P]), cnt26, start=False, stop=(t == hi - 1))
                    last.then_inc(sem("rk_ps"), 1)

                pe.wait_ge(sem("b49_ready"), n)
                if not (first and q == 0):
                    pe.wait_ge(sem("run_ready"), b)
                for t in range(BT):
                    last = pe.matmul(PSB[7][0:BT, 0:NT], band[:, BT - 1 - t:2 * BT - 1 - t], oh49[:, q, t, :],
                                     start=(t == 0), stop=(t == BT - 1))
                last.then_inc(sem("c26_ps"), 1)
                if q == 0:
                    pe.wait_ge(sem("ea_in0"), 16 * (i + 1))
                elif final:
                    pe.wait_ge(sem("ea_last"), 32)
                else:
                    pe.wait_ge(sem("ea_in1"), 16 * (i + 1))
                turn(0)
                turn_ea(0)
                for t in range(BT):
                    if t < BT - 1:
                        turn(t + 1)
                    if t % 2 == 1 and t < BT - 1:
                        turn_ea((t + 1) // 2)
                    main(t)
                    if t == 1:
                        pe.wait_ge(sem("c26_ready"), n)
                    if t in (1, 4, 8):
                        rank({1: 0, 4: 1, 8: 2}[t])
                    if t == 9:
                        pe.matmul(PSB[7][:, 64:64 + NT], onesb[0:BT, :], cnt26, start=True, stop=True).then_inc(sem("total_ps"), 1)
            pe.wait_ge(sem("split_done"), NCH)
            targets(0, 0, True)
            targets(0, 1, True)
            with pe.Fori(1, NB // 2 - 1) as i:
                for q in range(2):
                    targets(i, q)
            for q in range(2):
                targets(NB // 2 - 1, q, final=True)

            def turnp(g, m):
                pe.wait_ge(sem("ohq_ready"), g + 1)
                for j in range(PR):
                    last = pe.transpose(PSB[m % 2][:].bitcast(BF16)[:, j * P:(j + 1) * P], OHq[:, m % 4, j, :], identb)
                last.then_inc(sem("pT_ps"), 1)

            def source_rows(g, m, reg, first):
                pe.wait_ge(sem("pT_ready"), g + 1)
                if not (first and m < 2):
                    pe.wait_ge(sem("hp_ready"), g - 1)
                for j in range(PR):
                    for part in range(3):
                        last = pe.matmul(PSB[2 + m % 2][:, j * HID:(j + 1) * HID], ohTp[:, m % 2, j, :],
                                         flat(Pt[:, bass.ds(reg, 1), part, :]), start=(part == 0), stop=(part == 2))
                last.then_inc(sem("pp_ps"), 1)

            def segment(g, m, first):
                pe.wait_ge(sem("ohp_ready"), g + 1)
                pe.wait_ge(sem("hid_ready"), g + 1)
                if not (first and m < 2):
                    pe.wait_ge(sem("accB_done"), g)
                for j in range(PR):
                    last = pe.matmul(PSB[4 + m % 2][:, 0:XW], OHp[:, m, j, :], hid[:, m % 2, j, :], start=(j == 0), stop=(j == PR - 1))
                last.then_inc(sem("seg_ps"), 1)

            def sources(i, first=False):
                regs = pair_bins(ENG.PE, i)
                for m in range(SB):
                    turnp(SB * i + m, m)
                    if not (first and m < 1):
                        source_rows(SB * i + m - 1, (m - 1) % SB, regs[m + 3], first)
                    if not (first and m < 3):
                        segment(SB * i + m - 3, (m - 3) % SB, first)
            pe.wait_ge(sem("pt_in"), 16)
            pe.wait_ge(sem("pb_in"), 16)
            sources(0, True)
            with pe.Fori(1, NTURN) as i:
                sources(i)
            regs = pair_bins(ENG.PE, NTURN)
            source_rows(NPAIR - 1, SB - 1, regs[3], False)
            for m in range(SB - 3, SB):
                segment(NPAIR - SB + m, m, False)
            for c in range(NCH):
                pe.wait_ge(sem("stg_ready"), c + 1)
                if c:
                    pe.wait_ge(sem("sT_ready"), c)
                for j in range(NC):
                    for k in range(2):
                        last = pe.transpose(PSB[j // 2][:, (j % 2) * HID + k * P:(j % 2) * HID + (k + 1) * P], stg[:, j, k * P:(k + 1) * P], ident)
                last.then_inc(sem("sT_ps"), 1)
                pe.wait_ge(sem("sT_ready"), c + 1)
                if c:
                    pe.wait_ge(sem("fo_ready"), c)
                for j in range(NC):
                    for k in range(2):
                        last = pe.matmul(PSB[4 + j // 4][:, (j % 4) * D:(j % 4 + 1) * D], sT[:, j, k * P:(k + 1) * P], w2_sb[:, k, :],
                                         start=(k == 0), stop=(k == 1))
                last.then_inc(sem("fo_ps"), 1)


_INS = ['x', 'src', 'dst', 'edge_attr_64', 'L0_gnn_W', 'L0_gnn_att_src', 'L0_gnn_att_dst', 'L0_gnn_bias',
        'L1_gnn_W1', 'L1_gnn_b1', 'L1_gnn_W2', 'L1_gnn_b2']


def kernel(**inputs):
    import numpy as _np
    import concourse.bacc as _bacc
    from concourse.bass_utils import run_bass_kernel_spmd as _run

    nc = _bacc.Bacc("TRN2", target_bir_lowering=False, num_devices=1)
    arrays, args = {}, []
    for name in _INS:
        a = _np.ascontiguousarray(inputs[name])
        arrays[f"in_{name}"] = a
        args.append(nc.dram_tensor(f"in_{name}", a.shape, mybir.dt.from_np(a.dtype), kind="ExternalInput").ap())
    args.append(nc.dram_tensor("out_0", (N, D), F32, kind="ExternalOutput").ap())
    gnn(nc, *args)
    r = _run(nc, [arrays], core_ids=[0])
    return r.results[0]["out_0"]
```
